# Optimizing a Trainium2 kernel written in Bass

```python
import numpy as np
import jax
import jax.numpy as jnp

def _softmax(x, axis=-1):
    return jax.nn.softmax(x, axis=axis)

def _gelu(x):
    return jax.nn.gelu(x, approximate=True)

def _silu(x):
    return jax.nn.silu(x)

def _sigmoid(x):
    return jax.nn.sigmoid(x)

def _layernorm(x, axis=-1, eps=1e-05):
    m = jnp.mean(x, axis=axis, keepdims=True)
    v = jnp.var(x, axis=axis, keepdims=True)
    return (x - m) / jnp.sqrt(v + eps)

def _scatter_add(tgt, idx, src, axis=0):
    return tgt.at[idx].add(src)

def _segment_sum(src, seg, n):
    return jax.ops.segment_sum(src, seg, n)
kernel_name = 'mk_macaron_d1_jaxref_r4_de8296'

def setup_inputs(seed: int=0):
    np.random.seed(seed)
    _w = jnp.asarray

    def _L0_attn_setup():
        import jax, jax.numpy as jnp
        from jax import lax
        import numpy as np
        D_MODEL = 256
        K = 32
        K_Q = 4
        N_ANCHOR = 4
        N_DECAY = K - N_ANCHOR
        M = 8
        KS = 4
        H = D_MODEL // K
        N_REP = K // K_Q
        DIM_K = D_MODEL
        DIM_DECAY = K
        DIM_Q = K_Q * H * M * 2
        TOTAL = DIM_K + DIM_DECAY + DIM_Q
        B, L = (2, 512)
        key = jax.random.key(seed)
        ks = jax.random.split(key, 8)
        x = jax.random.normal(ks[0], (B, L, D_MODEL), jnp.float32)
        W_in = jax.random.normal(ks[1], (D_MODEL, TOTAL), jnp.float32) * D_MODEL ** (-0.5)
        conv_k = jax.random.normal(ks[2], (KS, 1, DIM_K + DIM_DECAY), jnp.float32) * 0.3
        grid = np.linspace(-np.pi / 3, np.pi / 3, M)
        theta = jnp.asarray(np.tile(grid.reshape(1, 1, 1, 1, M), (1, 1, K, H, 1)), jnp.float32)
        decay_slopes = jnp.log(jnp.exp(jnp.asarray(np.geomspace(0.001, 0.1, N_DECAY), jnp.float32)) - 1.0)
        anchor_slopes = jnp.log(jnp.exp(jnp.asarray(np.geomspace(0.01, 0.1, N_ANCHOR), jnp.float32)) - 1.0)
        score_scale = jnp.ones((K,), jnp.float32)
        lim = float(np.sqrt(6.0 / (H + H)))
        W_re = jax.random.uniform(ks[3], (H, H), jnp.float32, -lim, lim)
        W_im = jax.random.uniform(ks[4], (H, H), jnp.float32, -lim, lim)
        norm_scale = jnp.ones((2 * H,), jnp.float32)
        W_out = jax.random.normal(ks[5], (D_MODEL, D_MODEL), jnp.float32) * D_MODEL ** (-0.5)
        return dict(x=x, W_in=W_in, conv_k=conv_k, theta=theta, decay_slopes=decay_slopes, anchor_slopes=anchor_slopes, score_scale=score_scale, W_re=W_re, W_im=W_im, norm_scale=norm_scale, W_out=W_out)
    _L0_attn_in = _L0_attn_setup()

    def _L0_ffn_setup():
        import jax, jax.numpy as jnp
        import numpy as np
        B, T, C = (2, 512, 256)
        E, F = (8, 256)
        FS = 512
        TOP_K = 2
        key = jax.random.key(seed)
        ks = jax.random.split(key, 6)
        s = lambda *d: 1.0 / np.sqrt(d[-1])
        return {'hidden_tensor': jax.random.normal(ks[0], (B, T, C), jnp.float32), 'w_router': jax.random.normal(ks[1], (E, C), jnp.float32) * s(C), 'w1_stack': jax.random.normal(ks[2], (E, F, C), jnp.float32) * s(C), 'w2_stack': jax.random.normal(ks[3], (E, C, F), jnp.float32) * s(F), 'ws1': jax.random.normal(ks[4], (FS, C), jnp.float32) * s(C), 'ws2': jax.random.normal(ks[5], (C, FS), jnp.float32) * s(FS)}
    _L0_ffn_in = _L0_ffn_setup()
    _d = {'L0_attn_x': _L0_attn_in['x'], 'L0_attn_W_in': _L0_attn_in['W_in'], 'L0_attn_conv_k': _L0_attn_in['conv_k'], 'L0_attn_theta': _L0_attn_in['theta'], 'L0_attn_decay_slopes': _L0_attn_in['decay_slopes'], 'L0_attn_anchor_slopes': _L0_attn_in['anchor_slopes'], 'L0_attn_score_scale': _L0_attn_in['score_scale'], 'L0_attn_W_re': _L0_attn_in['W_re'], 'L0_attn_W_im': _L0_attn_in['W_im'], 'L0_attn_norm_scale': _L0_attn_in['norm_scale'], 'L0_attn_W_out': _L0_attn_in['W_out'], 'L0_ffn_w_router': _L0_ffn_in['w_router'], 'L0_ffn_w1_stack': _L0_ffn_in['w1_stack'], 'L0_ffn_w2_stack': _L0_ffn_in['w2_stack'], 'L0_ffn_ws1': _L0_ffn_in['ws1'], 'L0_ffn_ws2': _L0_ffn_in['ws2']}
    _x0 = _d['L0_attn_x']
    _d['L0_attn_x'] = jax.random.normal(jax.random.fold_in(jax.random.key(seed), 1), (1, 4096, 256), dtype=_x0.dtype)
    del _x0
    return _d

def reference(L0_attn_x, L0_attn_W_in, L0_attn_conv_k, L0_attn_theta, L0_attn_decay_slopes, L0_attn_anchor_slopes, L0_attn_score_scale, L0_attn_W_re, L0_attn_W_im, L0_attn_norm_scale, L0_attn_W_out, L0_ffn_w_router, L0_ffn_w1_stack, L0_ffn_w2_stack, L0_ffn_ws1, L0_ffn_ws2):

    def _L0_attn_ref(x, W_in, conv_k, theta, decay_slopes, anchor_slopes, score_scale, W_re, W_im, norm_scale, W_out):
        import jax, jax.numpy as jnp
        from jax import lax
        import numpy as np
        D_MODEL = 256
        K = 32
        K_Q = 4
        N_ANCHOR = 4
        N_DECAY = K - N_ANCHOR
        M = 8
        KS = 4
        H = D_MODEL // K
        N_REP = K // K_Q
        DIM_K = D_MODEL
        DIM_DECAY = K
        DIM_Q = K_Q * H * M * 2
        TOTAL = DIM_K + DIM_DECAY + DIM_Q
        B, L = (2, 512)
        b, l, _ = x.shape
        z = x @ W_in
        z_mem = z[..., :DIM_K + DIM_DECAY]
        q_raw = z[..., DIM_K + DIM_DECAY:]
        zp = jnp.pad(z_mem, ((0, 0), (KS - 1, 0), (0, 0)))
        z_mem = lax.conv_general_dilated(zp, conv_k, window_strides=(1,), padding='VALID', dimension_numbers=('NWC', 'WIO', 'NWC'), feature_group_count=DIM_K + DIM_DECAY)
        k_val = z_mem[..., :DIM_K].reshape(b, l, K, H)
        s_raw = z_mem[..., -K:].reshape(b, l, K, 1)
        q = q_raw.reshape(b, l, K_Q, H, M, 2)
        q_re, q_im = (q[..., 0], q[..., 1])
        pos = jnp.arange(l, dtype=jnp.float32)
        slopes_d = jax.nn.softplus(decay_slopes).reshape(1, 1, N_DECAY, 1)
        dist = jnp.maximum(jnp.float32(l - 1) - pos, 0.0)
        lw_d = -slopes_d * dist[None, :, None, None]
        slopes_a = jax.nn.softplus(anchor_slopes).reshape(1, 1, N_ANCHOR, 1)
        lw_a = -slopes_a * pos[None, :, None, None]
        log_tw = jnp.concatenate([lw_d, lw_a], axis=2)
        log_p = jnp.clip(score_scale[None, None, :, None] * s_raw, -20.0, 20.0)
        p_w = jnp.exp(log_p + log_tw)
        phi = k_val[..., None] * theta
        re_k = jnp.cos(phi)
        im_k = jnp.sin(phi)
        den = jnp.cumsum(p_w[..., 0], axis=1)
        pwb = p_w[..., None]
        num_re = jnp.cumsum(pwb * re_k, axis=1)
        num_im = jnp.cumsum(pwb * im_k, axis=1)
        inv = lax.rsqrt(jnp.maximum(den, 0.0001))
        inv = (inv * inv)[..., None, None]
        s_re = (num_re * inv).reshape(b, l, K_Q, N_REP, H, M)
        s_im = (num_im * inv).reshape(b, l, K_Q, N_REP, H, M)
        qr = q_re.reshape(b, l, K_Q, 1, H, M)
        qi = q_im.reshape(b, l, K_Q, 1, H, M)
        out_re = jnp.sum(s_re * qr + s_im * qi, axis=-1).reshape(b, l, K, H)
        out_im = jnp.sum(s_im * qr - s_re * qi, axis=-1).reshape(b, l, K, H)
        y_re = out_re * norm_scale[:H] * jnp.diagonal(W_re)
        y_im = out_im * norm_scale[H:] * jnp.diagonal(W_im)
        y = jax.nn.silu((y_re + y_im).reshape(b, l, DIM_K))
        return y @ W_out

    def _L0_ffn_ref(hidden_tensor, w_router, w1_stack, w2_stack, ws1, ws2):
        import jax, jax.numpy as jnp
        import numpy as np
        B, T, C = (2, 512, 256)
        E, F = (8, 256)
        FS = 512
        TOP_K = 2
        Bb, Tt, Cc = hidden_tensor.shape
        x = hidden_tensor.reshape(-1, Cc)
        t = x.shape[0]
        logits = x @ w_router.T
        probs = jax.nn.softmax(logits, axis=-1)
        expert_weight, expert_idx = jax.lax.top_k(probs, TOP_K)
        expert_weight = expert_weight / jnp.sum(expert_weight, axis=-1, keepdims=True)
        flat_e = expert_idx.reshape(-1)
        order = jnp.argsort(flat_e, stable=True)
        sorted_e = flat_e[order]
        flat_tok = jnp.repeat(jnp.arange(t), TOP_K)
        sorted_tok = flat_tok[order]
        sorted_w = expert_weight.reshape(-1)[order]
        counts = jnp.bincount(sorted_e, length=E)
        offsets = jnp.concatenate([jnp.zeros((1,), counts.dtype), jnp.cumsum(counts)])
        local_pos = jnp.arange(t * TOP_K) - offsets[sorted_e]
        cap = t * TOP_K
        binned = jnp.zeros((E, cap, Cc), x.dtype).at[sorted_e, local_pos].set(x[sorted_tok])
        inter = jnp.einsum('ecd,efd->ecf', binned, w1_stack)
        inter = jnp.square(jax.nn.relu(inter))
        outb = jnp.einsum('ecf,edf->ecd', inter, w2_stack)
        flat_out = outb[sorted_e, local_pos] * sorted_w[:, None]
        moe_out = jnp.zeros((t, Cc), x.dtype).at[sorted_tok].add(flat_out)
        moe_out = moe_out.reshape(Bb, Tt, Cc)
        sh = jnp.square(jax.nn.relu(jnp.einsum('btc,fc->btf', hidden_tensor, ws1)))
        shared_out = jnp.einsum('btf,cf->btc', sh, ws2)
        return shared_out + moe_out
    x = L0_attn_x
    x = x + 0.5 * _L0_ffn_ref(_layernorm(x, axis=-1), L0_ffn_w_router, L0_ffn_w1_stack, L0_ffn_w2_stack, L0_ffn_ws1, L0_ffn_ws2)
    x = x + _L0_attn_ref(_layernorm(x, axis=-1), L0_attn_W_in, L0_attn_conv_k, L0_attn_theta, L0_attn_decay_slopes, L0_attn_anchor_slopes, L0_attn_score_scale, L0_attn_W_re, L0_attn_W_im, L0_attn_norm_scale, L0_attn_W_out)
    x = x + 0.5 * _L0_ffn_ref(_layernorm(x, axis=-1), L0_ffn_w_router, L0_ffn_w1_stack, L0_ffn_w2_stack, L0_ffn_ws1, L0_ffn_ws2)
    return x

_drawn_inputs = setup_inputs


def setup_inputs(seed=0):
    import zlib

    import numpy as np

    out = dict(_drawn_inputs(seed))
    spreads = {'L0_attn_score_scale': (1.0, 0.6), 'L0_attn_norm_scale': (1.0, 0.2)}
    factors = {'L0_attn_anchor_slopes': 25.952}
    for name, (base, spread) in spreads.items():
        noise = np.random.default_rng([zlib.crc32(name.encode()), seed]).standard_normal(out[name].shape)
        drawn = base * np.exp(spread * noise) if base else spread * noise
        out[name] = jnp.asarray(drawn.astype(out[name].dtype))
    for name, factor in factors.items():
        out[name] = (out[name] * factor).astype(out[name].dtype)
    return out
```

```python
import math
from contextlib import ExitStack

import numpy as np
import concourse.bass as bass
from concourse import mybir

F32 = mybir.dt.float32
F32R = mybir.dt.float32r
I32 = mybir.dt.int32
U32 = mybir.dt.uint32
ALU = mybir.AluOpType
ACT = mybir.ActivationFunctionType
AX = mybir.AxisListType

P = 128
TOKENS, D = 4096, 256
TILES = TOKENS // P
CB = D // P
E, FE, FS = 8, 256, 512
FALL = E * FE + FS
FB = FALL // P
UNITS = FALL // FE
GT = 4
GROUPS = TILES // GT
GN = GT * P
K, H, M, KQ, TAPS = 32, 8, 8, 4, 4
NDECAY = 28
KH = K * H
CH = K * H * M
HM = H * M
REP = K // KQ
QW = KQ * HM
MEM = KH + K
CHUNK = REP * HM
CHUNKS = 2 * KQ
ROW = 2 * CH + K
RP = 96
RW = ROW // RP
EPS = 1e-5
MAGIC = 12582912.0
LOG2E = 1.0 / math.log(2.0)
LN2_HI = 0.693359375
LN2_LO = math.log(2.0) - LN2_HI


class Chain:

    def __init__(self, eng, sem):
        self.eng, self.sem, self.base, self.n = eng, sem, 0, 0

    def link(self, ins):
        ins.then_inc(self.sem, 1)
        self.n += 1
        self.eng.wait_ge(self.sem, self.base + self.n)

    def enter(self, it, per):
        self.start, self.per, self.before = self.n, per, self.base
        self.base = it * per

    def leave(self, passes):
        assert self.n - self.start == self.per, (self.n - self.start, self.per)
        self.base = 0
        self.n = self.start + self.per * passes


ACT_LINKS, DVE_LINKS = 2, 17


def chunk_cols(e):
    lo = (1 - e // KQ) * CH + (e % KQ) * CHUNK
    return lo, lo + CHUNK


def need(eng, sem, value):
    if not (isinstance(value, int) and value <= 0):
        eng.wait_ge(sem, value)


def build(nc, a):
    with ExitStack() as top:
        def sem(name):
            return top.enter_context(nc.semaphore(name))

        def sb(stack, name, shape, dt=F32):
            return stack.enter_context(nc.sbuf_tensor(name, shape, dt))

        k = {}
        k["x"] = sb(top, "x_all", [P, TILES * D])
        for part in ("hi", "lo"):
            k["w1" + part] = sb(top, "w1" + part, [P, CB * FALL], F32R)
            k["wr" + part] = sb(top, "wr" + part, [P, CB * E], F32R)
            k["wo" + part] = sb(top, "wo" + part, [P, CB * D], F32R)
            k["wc" + part] = sb(top, "wc" + part, [P, CB * TAPS * MEM], F32R)
            k["wq" + part] = sb(top, "wq" + part, [P, CB * 2 * QW], F32R)
        k["theta"] = sb(top, "theta_turns", [P, CH])
        k["ident"] = sb(top, "ident", [P, P])
        k["halfpi"] = sb(top, "half_pi", [P, 1])
        k["tri"] = sb(top, "tri", [P, P])
        k["ones2"] = sb(top, "ones2", [2, P], F32R)
        k["slope"] = sb(top, "neg_slope", [P, K])
        k["sscale"] = sb(top, "score_scale", [P, K])
        k["pos"] = sb(top, "pos_all", [P, TILES])
        k["dist"] = sb(top, "dist_all", [P, TILES])
        k["iota8"] = sb(top, "iota8", [P, E])
        k["st"] = sb(top, "bn_all", [P, TILES * 6])
        k["mean"] = sb(top, "mean_all", [P, TILES])
        k["rstd"] = sb(top, "rstd_all", [P, TILES])

        setup(nc, a, k, sem, sb)
        ffn(nc, a, k, sem, sb, "f1", store=False)
        attention(nc, a, k, sem, sb)
        ffn(nc, a, k, sem, sb, "f2", store=True)


def rsqrt_rows(ch, v, k, tmp):
    st = k["st"][:, :].rearrange("p (n s) -> p n s", s=6)
    var, t, y = tmp[:, 0:TILES], tmp[:, TILES:2 * TILES], k["rstd"][:, :]
    ch.link(v.tensor_tensor(t, st[:, :, 1], st[:, :, 4], ALU.subtract))
    ch.link(v.tensor_tensor(t, t, t, ALU.mult))
    ch.link(v.tensor_tensor(var, st[:, :, 2], st[:, :, 5], ALU.add))
    ch.link(v.tensor_scalar(var, var, 1.0 / D, EPS, ALU.mult, ALU.add))
    ch.link(v.scalar_tensor_tensor(var, t, 0.25, var, ALU.mult, ALU.add))
    ch.link(v.tensor_tensor(t, st[:, :, 1], st[:, :, 4], ALU.add))
    ch.link(v.tensor_scalar(k["mean"][:, :], t, 0.5, None, ALU.mult))
    ch.link(v.tensor_copy(t, var.bitcast(I32)))
    ch.link(v.tensor_scalar(y.bitcast(I32), t, -0.5, 1597463007.0, ALU.mult, ALU.add))
    for _ in range(4):
        ch.link(v.tensor_tensor(t, y, y, ALU.mult))
        ch.link(v.tensor_tensor(t, t, var, ALU.mult))
        ch.link(v.tensor_scalar(t, t, -0.5, 1.5, ALU.mult, ALU.add))
        ch.link(v.tensor_tensor(y, y, t, ALU.mult))


def setup(nc, a, k, sem, sb):
    SW = 2560
    with ExitStack() as c:
        stage = [sb(c, f"stage{i}", [P, SW]) for i in range(3)]
        convb = sb(c, "conv_rows", [P, TAPS * MEM])
        qstage = sb(c, "q_stage", [P, CB * 2 * QW])
        qtmp = sb(c, "q_tmp", [P, CB * QW])
        small = sb(c, "small", [P, 4 * H + 8 * K])
        ipos = sb(c, "ipos", [P, TILES], I32)
        tmp = sb(c, "root_tmp", [P, 2 * TILES])
        weights_in = [sem(f"weights_in{i}") for i in range(3)]
        smalls_in, x_in = sem("smalls_in"), [sem(f"x_in{g}") for g in range(GROUPS)]
        hi_done, lo_done = sem("w_hi_done"), sem("w_lo_done")
        folded, sp_exp, consts, g_chain = sem("folded"), sem("sp_exp"), sem("consts"), sem("setup_pool_chain")
        v_chain, sp_in = sem("setup_dve_chain"), sem("softplus_in")

        w1v = a["w1t"].rearrange("(c p) f -> p c f", p=P)
        def pair(name, lo, n):
            return [k[name + part][:, lo:lo + n] for part in ("hi", "lo")]

        loads = [(SW, w1v[:, 0, :], pair("w1", 0, SW)), (SW, w1v[:, 1, :], pair("w1", SW, SW)),
                 (CB * E, a["wrt"].rearrange("(c p) f -> p c f", p=P), pair("wr", 0, CB * E)),
                 (CB * D, a["w_out"].rearrange("(c p) f -> p c f", p=P), pair("wo", 0, CB * D))]
        NL = len(loads)
        xv = a["x"].rearrange("(n p) d -> p n d", p=P)

        with nc.Block() as block:
            @block.sync
            def _(sp):
                for g in range(GROUPS):
                    sp.dma_start(k["x"][:, g * GT * D:(g + 1) * GT * D].rearrange("p (n d) -> p n d", d=D),
                                 xv[:, g * GT:(g + 1) * GT, :]).then_inc(x_in[g], 16)
                for i, (n, src, _) in enumerate(loads):
                    if i >= 3:
                        sp.wait_ge(lo_done, i - 2)
                    sp.dma_start(stage[i % 3][:, 0:n].rearrange("p (c f) -> p c f", c=src.shape[1]),
                                 src).then_inc(weights_in[i % 3], 16)
                sp.wait_ge(lo_done, NL)
                winv = a["w_mem"].rearrange("(c p) f -> p c f", p=P)
                sp.dma_start(stage[0][:, 0:CB * MEM].rearrange("p (c f) -> p c f", c=CB), winv).then_inc(smalls_in, 16)
                for i, nm in ((1, "w_qre"), (2, "w_qim")):
                    sp.dma_start(stage[i][:, 0:CB * QW].rearrange("p (c f) -> p c f", c=CB),
                                 a[nm].rearrange("(c p) f -> p c f", p=P)).then_inc(smalls_in, 16)

            @block.gpsimd
            def _(g):
                ch = Chain(g, g_chain)
                for nm in ("ident", "tri"):
                    ch.link(g.memset(k[nm][:, :], 0.0 if nm == "ident" else 1.0))
                ch.link(g.affine_select(out=k["ident"][:, :], in_=k["ident"][:, :], compare_op=ALU.not_equal,
                                        fill=1.0, base=0, pattern=[[-1, P]], channel_multiplier=1))
                ch.link(g.affine_select(out=k["tri"][:, :], in_=k["tri"][:, :], compare_op=ALU.is_ge,
                                        fill=0.0, base=0, pattern=[[1, P]], channel_multiplier=-1))
                g.memset(k["ones2"][:, :].bitcast(F32), 1.0).then_inc(consts, 1)
                g.iota(ipos[:, :], pattern=[[P, TILES]], base=0, channel_multiplier=1).then_inc(consts, 1)

            @block.scalar
            def _(act):
                bc = lambda ap: ap.partition_broadcast(P)
                act.dma_start(convb[:, :], bc(a["conv_k"])).then_inc(smalls_in, 16)
                act.dma_start(k["theta"][:, :], bc(a["theta"])).then_inc(smalls_in, 16)
                act.dma_start(small[:, 0:2 * H], bc(a["norm_scale"])).then_inc(smalls_in, 16)
                act.dma_start(small[:, 2 * H:3 * H], bc(a["re_diag"])).then_inc(smalls_in, 16)
                act.dma_start(small[:, 3 * H:4 * H], bc(a["im_diag"])).then_inc(smalls_in, 16)
                act.dma_start(small[:, 4 * H:4 * H + K], bc(a["slopes"])).then_inc(smalls_in, 16)
                act.dma_start(k["sscale"][:, :], bc(a["score_scale"])).then_inc(smalls_in, 16)
                for i, (n, _, (hi, lo)) in enumerate(loads):
                    act.wait_ge(weights_in[i % 3], 16 * (i // 3 + 1))
                    act.activation(hi, stage[i % 3][:, 0:n], ACT.Copy).then_inc(hi_done, 1)
                act.wait_ge(sp_in, 1)
                act.activation(small[:, 4 * H + K:4 * H + 2 * K], small[:, 4 * H + K:4 * H + 2 * K],
                               ACT.Exp).then_inc(sp_exp, 1)
                for j in range(TAPS):
                    act.wait_ge(folded, j + 1)
                    act.activation(k["wchi"][:, :].rearrange("p (c j f) -> p c j f", c=CB, j=TAPS)[:, :, j, :],
                                   qstage[:, 0:CB * MEM].rearrange("p (c f) -> p c f", c=CB),
                                   ACT.Copy).then_inc(hi_done, 1)
                act.wait_ge(folded, TAPS + 1)
                act.activation(k["wqhi"][:, :], qstage[:, :], ACT.Copy).then_inc(hi_done, 1)

            @block.vector
            def _(v):
                ch = Chain(v, v_chain)
                for g in range(GROUPS):
                    v.wait_ge(x_in[g], 16)
                    for i in range(g * GT, (g + 1) * GT):
                        ins = v.bn_stats(k["st"][:, 6 * i:6 * i + 6], k["x"][:, i * D:(i + 1) * D])
                ch.link(ins)
                rsqrt_rows(ch, v, k, tmp)
                ch.link(v.memset(k["halfpi"][:, :], math.pi / 2.0))
                for e in range(E):
                    ch.link(v.memset(k["iota8"][:, e:e + 1], float(e)))
                for i, (n, _, (hi, lo)) in enumerate(loads):
                    v.wait_ge(weights_in[i % 3], 16 * (i // 3 + 1))
                    v.wait_ge(hi_done, i + 1)
                    v.tensor_tensor(lo, stage[i % 3][:, 0:n], hi.bitcast(F32), ALU.subtract).then_inc(lo_done, 1)
                v.wait_ge(consts, 2)
                ch.link(v.tensor_copy(k["pos"][:, :], ipos[:, :]))
                ch.link(v.tensor_scalar(k["dist"][:, :], k["pos"][:, :], -1.0, float(TOKENS - 1), ALU.mult, ALU.add))
                v.wait_ge(smalls_in, 16 * 10)
                ch.link(v.tensor_scalar(k["theta"][:, :], k["theta"][:, :], 1.0 / (2.0 * math.pi), None, ALU.mult))
                o = 4 * H
                s, e_, z, z2, q, r = (small[:, o + i * K:o + (i + 1) * K] for i in range(6))
                ch.link(v.tensor_scalar(z, s, -1.0, None, ALU.mult))
                ch.link(v.tensor_tensor(e_, s, z, ALU.min))
                v.tensor_copy(q, e_).then_inc(sp_in, 1)
                v.wait_ge(sp_exp, 1)
                ch.link(v.tensor_scalar(z2, e_, 2.0, None, ALU.add))
                ch.link(v.reciprocal(r, z2))
                ch.link(v.tensor_tensor(z, e_, r, ALU.mult))
                ch.link(v.tensor_tensor(z2, z, z, ALU.mult))
                ch.link(v.memset(q, 1.0 / 19.0))
                for n in range(17, 0, -2):
                    ch.link(v.tensor_tensor(q, q, z2, ALU.mult))
                    ch.link(v.tensor_scalar(q, q, 1.0 / n, None, ALU.add))
                ch.link(v.tensor_tensor(q, q, z, ALU.mult))
                ch.link(v.tensor_scalar(s, s, 0.0, None, ALU.max))
                ch.link(v.scalar_tensor_tensor(q, q, 2.0, s, ALU.mult, ALU.add))
                ch.link(v.tensor_scalar(k["slope"][:, :], q, -1.0, None, ALU.mult))
                wm = stage[0][:, 0:CB * MEM].rearrange("p (c f) -> p c f", c=CB)
                for j in range(TAPS):
                    if j:
                        v.wait_ge(lo_done, NL + j)
                    tap = convb[:, j * MEM:(j + 1) * MEM].unsqueeze(1).to_broadcast([P, CB, MEM])
                    v.tensor_tensor(qstage[:, 0:CB * MEM].rearrange("p (c f) -> p c f", c=CB), wm, tap,
                                    ALU.mult).then_inc(folded, 1)
                    v.wait_ge(folded, j + 1)
                    v.wait_ge(hi_done, NL + j + 1)
                    v.tensor_tensor(k["wclo"][:, :].rearrange("p (c j f) -> p c j f", c=CB, j=TAPS)[:, :, j, :],
                                    qstage[:, 0:CB * MEM].rearrange("p (c f) -> p c f", c=CB),
                                    k["wchi"][:, :].bitcast(F32).rearrange("p (c j f) -> p c j f", c=CB, j=TAPS)[:, :, j, :],
                                    ALU.subtract).then_inc(lo_done, 1)
                v.wait_ge(lo_done, NL + TAPS)
                ch.link(v.tensor_tensor(small[:, 2 * H:3 * H], small[:, 0:H], small[:, 2 * H:3 * H], ALU.mult))
                ch.link(v.tensor_tensor(small[:, 3 * H:4 * H], small[:, H:2 * H], small[:, 3 * H:4 * H], ALU.mult))

                def hs(i):
                    return small[:, i * H:(i + 1) * H].unsqueeze(1).unsqueeze(3).to_broadcast([P, KQ, H, M])

                def v4(ap):
                    return ap.rearrange("p (q h m) -> p q h m", q=KQ, h=H)

                for cb in range(CB):
                    re = v4(stage[1][:, cb * QW:(cb + 1) * QW])
                    im = v4(stage[2][:, cb * QW:(cb + 1) * QW])
                    t = v4(qtmp[:, cb * QW:(cb + 1) * QW])
                    q1 = v4(qstage[:, cb * 2 * QW:cb * 2 * QW + QW])
                    q2 = v4(qstage[:, cb * 2 * QW + QW:(cb + 1) * 2 * QW])
                    ch.link(v.tensor_tensor(q1, re, hs(2), ALU.mult))
                    ch.link(v.tensor_tensor(t, im, hs(3), ALU.mult))
                    ch.link(v.tensor_tensor(q1, q1, t, ALU.subtract))
                    ch.link(v.tensor_tensor(q2, im, hs(2), ALU.mult))
                    ch.link(v.tensor_tensor(t, re, hs(3), ALU.mult))
                    last = v.tensor_tensor(q2, q2, t, ALU.add)
                    if cb < CB - 1:
                        ch.link(last)
                last.then_inc(folded, 1)
                v.wait_ge(folded, TAPS + 1)
                v.wait_ge(hi_done, NL + TAPS + 1)
                v.tensor_tensor(k["wqlo"][:, :], qstage[:, :], k["wqhi"][:, :].bitcast(F32),
                                ALU.subtract).then_inc(lo_done, 1)


def ffn(nc, a, k, sem, sb, ph, store):
    with ExitStack() as c:
        s = lambda n: c.enter_context(nc.semaphore(f"{ph}_{n}"))
        w2 = {part: sb(c, ph + "w2" + part, [P, FB * D], F32R) for part in ("hi", "lo")}
        w2raw = [sb(c, f"{ph}w2raw{i}", [P, FE // P * D]) for i in range(2)]
        w2_in, w2_ready = [s(f"w2_in{i}") for i in range(2)], s("w2_ready")
        xn = sb(c, ph + "xn", [P, GT * D])
        xh, xl = (sb(c, ph + n, [P, CB * GN], F32R) for n in ("xh", "xl"))
        r = [sb(c, f"{ph}relu{i}", [P, GN]) for i in range(2)]
        h = [sb(c, f"{ph}h{i}", [P, GN]) for i in range(2)]
        hh, hl = ([sb(c, f"{ph}{n}{i}", [P, GN], F32R) for i in range(4)] for n in ("hh", "hl"))
        lg, mx = (sb(c, ph + n, [P, GT * E]) for n in ("lg", "mx"))
        ix = sb(c, ph + "ix", [P, GT * E], U32)
        ixf, oh = (sb(c, ph + n, [P, GT * E]) for n in ("ixf", "oh"))
        gate = sb(c, ph + "gate", [P, GT * UNITS])
        idle = sb(c, ph + "idle", [P, 2])
        d12, ge = (sb(c, ph + n, [P, GT]) for n in ("d12", "ge"))
        g12 = sb(c, ph + "g12", [P, 3 * GT])
        tmp = sb(c, ph + "rt", [P, 2 * TILES])
        psT = [c.enter_context(nc.psum_tensor(f"{ph}psT{i}", [P, GN], F32)) for i in range(2)]
        psU = [c.enter_context(nc.psum_tensor(f"{ph}psU{i}", [P, GN], F32)) for i in range(2)]
        psO = [c.enter_context(nc.psum_tensor(f"{ph}psO{i}", [P, 2 * D], F32)) for i in range(4)]
        xn_ready, xT_ready, xh_ready, xl_ready = s("xn_ready"), s("xT_ready"), s("xh_ready"), s("xl_ready")
        logits_ready, logits_read, gap_ready, exp_ready = s("logits_ready"), s("logits_read"), s("gap_ready"), s("exp_ready")
        up_ready, relu_ready, h_ready = s("up_ready"), s("relu_ready"), s("h_ready")
        hh_ready, hl_ready, out_ready, out_added = s("hh_ready"), s("hl_ready"), s("out_ready"), s("out_added")
        x_done, chain, stored = s("x_done"), s("dve_chain"), s("stored")
        X = k["x"]
        FU = FE // P

        with nc.Block() as block:
            @block.tensor
            def _(pe):
                with pe.Fori(0, GROUPS) as it:
                    pe.wait_ge(xn_ready, it + 1)
                    for cb in range(CB):
                        for i in range(GT):
                            ins = pe.transpose(psT[cb][:, i * P:(i + 1) * P], xn[:, i * D + cb * P:i * D + (cb + 1) * P],
                                               k["ident"][:, :])
                        ins.then_inc(xT_ready, 1)
                    pe.wait_ge(xh_ready, CB * (it + 1))
                    pe.wait_ge(xl_ready, CB * (it + 1))
                    for i in range(GT):
                        n = 0
                        for cb in range(CB):
                            for xp in (xh, xl):
                                for wp in ("hi", "lo"):
                                    ins = pe.matmul(psT[0][:, i * E:(i + 1) * E], xp[:, cb * GN + i * P:cb * GN + (i + 1) * P],
                                                    k["wr" + wp][:, cb * E:(cb + 1) * E], start=(n == 0), stop=(n == 7))
                                    n += 1
                    ins.then_inc(logits_ready, 1)

                    def up(f):
                        if f >= 2:
                            pe.wait_ge(h_ready, it * FB + f - 1)
                        n = 0
                        for cb in range(CB):
                            w = slice(cb * FALL + f * P, cb * FALL + (f + 1) * P)
                            for xp, wp in ((xh, "hi"), (xl, "hi"), (xh, "lo")):
                                ins = pe.matmul(psU[f % 2][:, :], k["w1" + wp][:, w], xp[:, cb * GN:(cb + 1) * GN],
                                                start=(n == 0), stop=(n == 5))
                                n += 1
                        ins.then_inc(up_ready, 1)

                    def down(u):
                        pe.wait_ge(w2_ready, 2 * (u + 1))
                        pe.wait_ge(hh_ready, it * FB + FU * (u + 1))
                        pe.wait_ge(hl_ready, it * FB + FU * (u + 1))
                        if u >= 2:
                            pe.wait_ge(out_added, it * UNITS + u - 1)
                        for i in range(GT):
                            n = 0
                            o = psO[2 * (u % 2) + i // 2][:, (i % 2) * D:(i % 2 + 1) * D]
                            for j in range(FU):
                                f = FU * u + j
                                for hp, wp in ((hh, "hi"), (hl, "hi"), (hh, "lo")):
                                    ins = pe.matmul(o, hp[f % 4][:, i * P:(i + 1) * P], w2[wp][:, f * D:(f + 1) * D],
                                                    start=(n == 0), stop=(n == 5))
                                    n += 1
                        ins.then_inc(out_ready, 1)

                    for f in range(FU):
                        up(f)
                    for u in range(UNITS):
                        if u < UNITS - 1:
                            for j in range(FU):
                                up(FU * (u + 1) + j)
                        down(u)
                    pe.wait_ge(out_added, (it + 1) * UNITS)

            @block.scalar
            def _(act):
                with act.Fori(0, GROUPS) as it:
                    for cb in range(CB):
                        act.wait_ge(xT_ready, it * CB + cb + 1)
                        act.activation(xh[:, cb * GN:(cb + 1) * GN], psT[cb][:, :], ACT.Copy).then_inc(xh_ready, 1)

                    def relu(f):
                        act.wait_ge(up_ready, it * FB + f + 1)
                        if f >= 2:
                            act.wait_ge(h_ready, it * FB + f - 1)
                        act.activation(r[f % 2][:, :], psU[f % 2][:, :], ACT.Relu).then_inc(relu_ready, 1)

                    def high(f):
                        act.wait_ge(h_ready, it * FB + f + 1)
                        if f >= 4:
                            act.wait_ge(out_ready, it * UNITS + (f - 4) // FU + 1)
                        act.activation(hh[f % 4][:, :], h[f % 2][:, :], ACT.Copy).then_inc(hh_ready, 1)

                    relu(0)
                    for f in range(FB):
                        if f + 1 < FB:
                            relu(f + 1)
                        high(f)
                        if f == 2:
                            act.wait_ge(gap_ready, it + 1)
                            act.activation(ge[:, :], d12[:, :], ACT.Exp).then_inc(exp_ready, 1)

            @block.vector
            def _(v):
                ch = Chain(v, chain)

                def normalise(g):
                    for i in range(GT):
                        n = g * GT + i
                        ins = v.tensor_scalar(xn[:, i * D:(i + 1) * D], X[:, bass.ds(n * D, D)],
                                              k["mean"][:, bass.ds(n, 1)], k["rstd"][:, bass.ds(n, 1)],
                                              ALU.subtract, ALU.mult)
                    ins.then_inc(xn_ready, 1)

                for i in range(GT):
                    for u in range(E, UNITS):
                        v.memset(gate[:, i * UNITS + u:i * UNITS + u + 1], 0.5)
                normalise(0)
                lg3, mx3 = (t[:, :].rearrange("p (i e) -> p i e", e=E) for t in (lg, mx))
                ixf3, oh3 = (t[:, :].rearrange("p (i e) -> p i e", e=E) for t in (ixf, oh))
                gate3 = gate[:, :].rearrange("p (i u) -> p i u", u=UNITS)

                def group(it, last):
                    for cb in range(CB):
                        v.wait_ge(xh_ready, it * CB + cb + 1)
                        v.tensor_tensor(xl[:, cb * GN:(cb + 1) * GN], psT[cb][:, :],
                                        xh[:, cb * GN:(cb + 1) * GN].bitcast(F32), ALU.subtract).then_inc(xl_ready, 1)

                    def squares(f):
                        v.wait_ge(relu_ready, it * FB + f + 1)
                        if f >= 2:
                            v.wait_ge(hh_ready, it * FB + f - 1)
                            v.wait_ge(hl_ready, it * FB + f - 1)
                        v.scalar_tensor_tensor(h[f % 2][:, :], psU[f % 2][:, :], 0.0, r[f % 2][:, :],
                                               ALU.max, ALU.mult).then_inc(h_ready, 1)

                    def low(f):
                        v.wait_ge(h_ready, it * FB + f + 1)
                        v.wait_ge(hh_ready, it * FB + f + 1)
                        v.tensor_tensor(hl[f % 4][:, :], h[f % 2][:, :], hh[f % 4][:, :].bitcast(F32),
                                        ALU.subtract).then_inc(hl_ready, 1)

                    def add(u):
                        v.wait_ge(out_ready, it * UNITS + u + 1)
                        if u:
                            v.wait_ge(out_added, it * UNITS + u)
                        for i in range(GT):
                            xs = X[:, bass.ds((it * GT + i) * D, D)]
                            ins = v.scalar_tensor_tensor(xs, psO[2 * (u % 2) + i // 2][:, (i % 2) * D:(i % 2 + 1) * D],
                                                         gate[:, i * UNITS + u:i * UNITS + u + 1], xs, ALU.mult, ALU.add)
                        ins.then_inc(out_added, 1)

                    def route():
                        v.wait_ge(logits_ready, it + 1)
                        ch.link(v.tensor_copy(lg[:, :], psT[0][:, 0:GT * E]))
                        v.memset(idle[:, 0:1], 0.0)
                        for i in range(GT):
                            e = slice(i * E, (i + 1) * E)
                            ins = v.max(mx[:, e], lg[:, e])
                            if i == GT - 1:
                                ch.link(ins)
                        v.memset(idle[:, 1:2], 0.0)
                        for i in range(GT):
                            e = slice(i * E, (i + 1) * E)
                            ins = v.max_index(ix[:, e], mx[:, e], lg[:, e])
                            if i == GT - 1:
                                ch.link(ins)
                        ch.link(v.tensor_copy(ixf[:, :], ix[:, :]))
                        v.tensor_tensor(d12[:, :], mx3[:, :, 1], mx3[:, :, 0], ALU.subtract).then_inc(gap_ready, 1)

                    def gates():
                        v.wait_ge(exp_ready, it + 1)
                        ch.link(v.tensor_scalar(g12[:, 2 * GT:3 * GT], ge[:, :], 2.0, 2.0, ALU.mult, ALU.add))
                        ch.link(v.reciprocal(g12[:, 0:GT], g12[:, 2 * GT:3 * GT]))
                        ch.link(v.tensor_tensor(g12[:, GT:2 * GT], g12[:, 0:GT], ge[:, :], ALU.mult))
                        for j in range(2):
                            which = ixf3[:, :, j:j + 1].to_broadcast([P, GT, E])
                            amount = g12[:, j * GT:(j + 1) * GT].unsqueeze(2).to_broadcast([P, GT, E])
                            dst = gate3[:, :, 0:E] if j == 0 else oh3
                            index = k["iota8"][:, :].unsqueeze(1).to_broadcast([P, GT, E])
                            ch.link(v.tensor_tensor(dst, index, which, ALU.is_equal))
                            ch.link(v.tensor_tensor(dst, dst, amount, ALU.mult))
                        ch.link(v.tensor_tensor(gate3[:, :, 0:E], gate3[:, :, 0:E], oh3, ALU.add))

                    route()
                    squares(0)
                    for f in range(FB):
                        if f + 1 < FB:
                            squares(f + 1)
                        low(f)
                        if f == 2:
                            gates()
                        if f % FU == 1 and f // FU >= 2:
                            add(f // FU - 2)
                    add(UNITS - 2)
                    add(UNITS - 1)
                    v.wait_ge(out_added, (it + 1) * UNITS)
                    for i in range(GT):
                        n = it * GT + i
                        ins = v.bn_stats(k["st"][:, bass.ds(n * 6, 6)], X[:, bass.ds(n * D, D)])
                    ins.then_inc(x_done, 1)
                    if not last:
                        normalise(it + 1)

                with v.Fori(0, GROUPS - 1) as it:
                    ch.enter(it, 12)
                    group(it, False)
                    ch.leave(GROUPS - 1)
                group(GROUPS - 1, True)
                v.wait_ge(x_done, GROUPS)
                rsqrt_rows(ch, v, k, tmp)

            @block.gpsimd
            def _(g):
                for u in range(UNITS):
                    cols = slice(u * FU * D, (u + 1) * FU * D)
                    g.wait_ge(w2_in[u % 2], 16 * (u // 2 + 1))
                    g.tensor_copy(w2["hi"][:, cols], w2raw[u % 2][:, :]).then_inc(w2_ready, 1)
                    g.wait_ge(w2_ready, 2 * u + 1)
                    g.tensor_tensor(w2["lo"][:, cols], w2raw[u % 2][:, :], w2["hi"][:, cols].bitcast(F32),
                                    ALU.subtract).then_inc(w2_ready, 1)

            @block.sync
            def _(sp):
                w2v = a["w2t"].rearrange("(u b p) d -> u p b d", p=P, b=FU)
                for u in range(UNITS):
                    if u >= 2:
                        sp.wait_ge(w2_ready, 2 * (u - 1))
                    sp.dma_start(w2raw[u % 2][:, :].rearrange("p (b d) -> p b d", d=D),
                                 w2v[u]).then_inc(w2_in[u % 2], 16)
                if store:
                    ov = a["out"].rearrange("(n p) d -> p n d", p=P)
                    with sp.Fori(0, GROUPS) as it:
                        sp.wait_ge(x_done, it + 1)
                        sp.dma_start(ov[:, bass.ds(it * GT, GT), :],
                                     X[:, bass.ds(it * GT * D, GT * D)].rearrange("p (n d) -> p n d", d=D)).then_inc(stored, 16)
                    sp.wait_ge(stored, 16 * GROUPS)


def attention(nc, a, k, sem, sb):
    X = k["x"]
    TWO_PI = 2.0 * math.pi
    XC = P + TAPS
    with ExitStack() as c:
        s = lambda n: c.enter_context(nc.semaphore("at_" + n))
        xn = sb(c, "at_xn", [P, D])
        xh, xl = ([sb(c, f"at_{n}{i}", [P, CB * XC], F32R) for i in range(2)] for n in ("xh", "xl"))
        turns = sb(c, "at_turns", [P, CH])
        feat = [sb(c, f"at_feat{i}", [P, 2 * CH]) for i in range(2)]
        qs = [sb(c, f"at_qs{i}", [P, 2 * QW]) for i in range(2)]
        prod = sb(c, "at_prod", [P, 2 * CHUNK])
        srow = sb(c, "at_srow", [P, ROW])
        crow = sb(c, "at_crow", [RP, RW])
        split = sb(c, "at_split", [RP, 2 * RW], F32R)
        ones, ones_set = sb(c, "at_ones", [RP, RW]), s("ones_set")
        carry = sb(c, "at_carry", [2, ROW], F32R)
        pw = [sb(c, f"at_p{i}", [P, K]) for i in range(2)]
        ex = sb(c, "at_exp", [P, 8 * K])
        pow2 = sb(c, "at_pow2", [P, K], I32)
        y2 = sb(c, "at_y2", [P, 2 * KH])
        y = sb(c, "at_y", [P, KH])
        ys = y
        yh, yl = (sb(c, "at_" + n, [P, KH], F32R) for n in ("yh", "yl"))
        rden = sb(c, "at_rden", [P, 2 * K])
        tmp = sb(c, "at_rt", [P, 2 * TILES])
        ps = lambda n: c.enter_context(nc.psum_tensor("at_ps" + n, [P, 512], F32))
        psT, psK, psQ, psY = ps("T"), ps("K"), ps("Q"), ps("Y")
        psS = [ps(f"S{i}") for i in range(4)]
        den = psY[:, 0:K]

        xT_ready, mem_ready, q_ready, yT_ready = s("xT_ready"), s("mem_ready"), s("q_ready"), s("yT_ready")
        den_ready, sums_ready, out_ready = s("den_ready"), s("sums_ready"), s("out_ready")
        xh_ready, yh_ready, whole_ready, tanh_ready = s("xh_ready"), s("yh_ready"), s("whole_ready"), s("tanh_ready")
        feat_ready, row_ready, q_copied, silu_ready = s("feat_ready"), s("row_ready"), s("q_copied"), s("silu_ready")
        xn_ready, xl_ready, turns_ready, mem_read = s("xn_ready"), s("xl_ready"), s("turns_ready"), s("mem_read")
        rem_ready, p_ready, frac_ready, prod_done = s("rem_ready"), s("p_ready"), s("frac_ready"), s("prod_done")
        den_read, y_ready, yl_ready, x_added = s("den_read"), s("y_ready"), s("yl_ready"), s("x_added")
        v_ready, split_ready, row_moved, carry_in = s("v_ready"), s("split_ready"), s("row_moved"), s("carry_in")
        v_chain, a_chain = s("dve_chain"), s("act_chain")

        def steps(eng, step, chain=None, per=0):
            pairs = (TILES - 4) // 2
            for n in range(-2, 2):
                step(n, n % 2)
            with eng.Fori(0, pairs) as it:
                if chain:
                    chain.enter(it, per)
                for par in range(2):
                    step(it * 2 + (2 + par), par)
                if chain:
                    chain.leave(pairs)
            for n in range(TILES - 2, TILES + 1):
                step(n, n % 2)

        def has(n):
            return not isinstance(n, int) or 0 <= n < TILES

        def first(n):
            return isinstance(n, int) and n == 0

        def ahead(n, by):
            return not isinstance(n, int) or 0 <= n + by < TILES

        with nc.Block() as block:
            @block.tensor
            def _(pe):
                def step(n, par):
                    if ahead(n, 2):
                        pe.wait_ge(xn_ready, n + 3)
                        need(pe, xl_ready, n + 2)
                        for cb in range(CB):
                            ins = pe.transpose(psT[:, cb * P:(cb + 1) * P], xn[:, cb * P:(cb + 1) * P], k["ident"][:, :])
                        ins.then_inc(xT_ready, 1)
                    if ahead(n, -1):
                        pe.wait_ge(silu_ready, n)
                        need(pe, x_added, n - 1)
                        pe.wait_ge(den_read, n)
                        for cb in range(CB):
                            ins = pe.transpose(psY[:, cb * P:(cb + 1) * P], ys[:, cb * P:(cb + 1) * P], k["ident"][:, :])
                        ins.then_inc(yT_ready, 1)

                    def project_out():
                        pe.wait_ge(yh_ready, n)
                        pe.wait_ge(yl_ready, n)
                        i = 0
                        for cb in range(CB):
                            for yp, wp in ((yh, "hi"), (yl, "hi"), (yh, "lo")):
                                ins = pe.matmul(psY[:, D:2 * D], yp[:, cb * P:(cb + 1) * P],
                                                k["wo" + wp][:, cb * D:(cb + 1) * D], start=(i == 0), stop=(i == 5))
                                i += 1
                        ins.then_inc(out_ready, 1)

                    def project_in():
                        pe.wait_ge(xh_ready, n + 3)
                        pe.wait_ge(xl_ready, n + 3)
                        need(pe, mem_read, n + 2)
                        parts = ((xh[par], "hi"), (xl[par], "hi"), (xh[par], "lo"))
                        total, i = CB * TAPS * 3, 0
                        for cb in range(CB):
                            for j in range(TAPS):
                                for xp, wp in parts:
                                    ins = pe.matmul(psK[:, 0:MEM], xp[:, cb * XC + j:cb * XC + j + P],
                                                    k["wc" + wp][:, (cb * TAPS + j) * MEM:(cb * TAPS + j + 1) * MEM],
                                                    start=(i == 0), stop=(i == total - 1))
                                    i += 1
                        ins.then_inc(mem_ready, 1)
                        need(pe, q_copied, n + 2)
                        i = 0
                        for cb in range(CB):
                            for xp, wp in parts:
                                ins = pe.matmul(psQ[:, :], xp[:, cb * XC + TAPS - 1:cb * XC + TAPS - 1 + P],
                                                k["wq" + wp][:, cb * 2 * QW:(cb + 1) * 2 * QW],
                                                start=(i == 0), stop=(i == 5))
                                i += 1
                        ins.then_inc(q_ready, 1)

                    if has(n):
                        if not first(n):
                            pe.wait_ge(carry_in, 32 * n)
                        for e in range(CHUNKS):
                            if e % KQ == 0:
                                pe.wait_ge(v_ready, 2 * n + e // KQ + 1)
                            need(pe, prod_done, 8 * n + (e - 3))
                            if ahead(n, 1) or e < 4:
                                need(pe, row_ready, 8 * n + (e - 3))
                            cols = slice(*chunk_cols(e))
                            last = pe.matmul(psS[e % 4][:, :], k["tri"][:, :], feat[par][:, cols], start=True, stop=first(n))
                            if not first(n):
                                last = pe.matmul(psS[e % 4][:, :], k["ones2"][:, :], carry[:, cols], start=False, stop=True)
                            last.then_inc(sums_ready, 1)
                            if e == 2:
                                if ahead(n, -1):
                                    project_out()
                                pe.wait_ge(p_ready, n + 1)
                                last = pe.matmul(den, k["tri"][:, :], pw[par][:, :], start=True, stop=first(n))
                                if not first(n):
                                    last = pe.matmul(den, k["ones2"][:, :], carry[:, 2 * CH:ROW], start=False, stop=True)
                                last.then_inc(den_ready, 1)
                            if e == 5 and ahead(n, 2):
                                project_in()
                    else:
                        if ahead(n, -1):
                            project_out()
                        if ahead(n, 2):
                            project_in()

                steps(pe, step)

            @block.scalar
            def _(act):
                ch = Chain(act, a_chain)

                def step(n, par):
                    if ahead(n, 1):
                        act.wait_ge(turns_ready, n + 2)
                        need(act, sums_ready, 8 * n)
                        act.activation(feat[1 - par][:, 0:CH], turns[:, :], ACT.Copy, bias=MAGIC).then_inc(whole_ready, 1)
                        act.wait_ge(rem_ready, n + 2)
                        act.activation(ex[:, 4 * K:5 * K], ex[:, 3 * K:4 * K], ACT.Tanh, scale=0.5).then_inc(tanh_ready, 1)
                    if ahead(n, -1):
                        act.wait_ge(yT_ready, n)
                        need(act, out_ready, n - 1)
                        act.activation(yh[:, :], psY[:, 0:KH], ACT.Copy).then_inc(yh_ready, 1)
                    if ahead(n, 2):
                        act.wait_ge(xT_ready, n + 3)
                        need(act, mem_ready, n + 1)
                        need(act, q_ready, n + 1)
                        x3 = [t[:, :].rearrange("p (c t) -> p c t", c=CB) for t in xh]
                        if isinstance(n, int) and n == -2:
                            ch.link(act.activation(x3[par][:, :, 0:TAPS - 1], psT[:, 0:CB * (TAPS - 1)].rearrange(
                                "p (c t) -> p c t", c=CB), ACT.Copy, scale=0.0))
                        else:
                            act.wait_ge(xh_ready, n + 2)
                            ch.link(act.activation(x3[par][:, :, 0:TAPS - 1],
                                                   x3[1 - par][:, :, P:P + TAPS - 1].bitcast(F32), ACT.Copy))
                        act.activation(x3[par][:, :, TAPS - 1:TAPS - 1 + P],
                                       psT[:, 0:D].rearrange("p (c t) -> p c t", c=CB), ACT.Copy).then_inc(xh_ready, 1)

                    def rows(lo, hi):
                        if not (has(n) and ahead(n, 1)):
                            return
                        for e in range(lo, hi):
                            act.wait_ge(prod_done, 8 * n + (e + 1))
                            if e == 0:
                                need(act, row_moved, 16 * n)
                            act.activation(srow[96:P, slice(*chunk_cols(e))], psS[e % 4][96:P, :], ACT.Copy).then_inc(row_ready, 1)

                    if ahead(n, 1):
                        act.wait_ge(frac_ready, n + 2)
                        f = feat[1 - par]
                        ch.link(act.activation(f[:, 0:CH], f[:, CH:2 * CH], ACT.Abs))
                        act.activation(f[:, CH:2 * CH], f[:, CH:2 * CH], ACT.Sin, scale=-TWO_PI).then_inc(feat_ready, 1)
                    rows(0, 4)
                    if ahead(n, 1):
                        act.activation(f[:, 0:CH], f[:, 0:CH], ACT.Sin, scale=-TWO_PI,
                                       bias=k["halfpi"][:, 0:1]).then_inc(feat_ready, 1)
                    rows(4, 8)
                    if ahead(n, 2):
                        act.wait_ge(q_ready, n + 3)
                        need(act, prod_done, 8 * n + 8)
                        act.activation(qs[par][:, :], psQ[:, :], ACT.Copy).then_inc(q_copied, 1)
                    if has(n):
                        act.wait_ge(y_ready, n + 1)
                        act.activation(ys[:, :], y[:, :], ACT.Silu).then_inc(silu_ready, 1)

                steps(act, step, ch, 2 * ACT_LINKS)

            @block.vector
            def _(v):
                ch = Chain(v, v_chain)
                lp, t0, k2, rem, th, t1, t2, _ = (ex[:, i * K:(i + 1) * K] for i in range(8))

                def step(n, par):
                    if ahead(n, 1):
                        v.wait_ge(mem_ready, n + 2)
                        need(v, whole_ready, n + 1)
                        v.tensor_tensor(turns[:, :].rearrange("p (c m) -> p c m", m=M),
                                        psK[:, 0:KH].unsqueeze(2).to_broadcast([P, KH, M]),
                                        k["theta"][:, :].rearrange("p (c m) -> p c m", m=M), ALU.mult).then_inc(turns_ready, 1)
                        v.tensor_tensor(t0, psK[:, KH:MEM], k["sscale"][:, :], ALU.mult).then_inc(mem_read, 1)
                        v.wait_ge(mem_read, n + 2)
                        ch.link(v.tensor_scalar(t0, t0, 20.0, -20.0, ALU.min, ALU.max))
                        v.scalar_tensor_tensor(lp[:, 0:NDECAY], k["slope"][:, 0:NDECAY], k["dist"][:, bass.ds(n + 1, 1)],
                                               t0[:, 0:NDECAY], ALU.mult, ALU.add)
                        ch.link(v.scalar_tensor_tensor(lp[:, NDECAY:K], k["slope"][:, NDECAY:K],
                                                       k["pos"][:, bass.ds(n + 1, 1)], t0[:, NDECAY:K], ALU.mult, ALU.add))
                        ch.link(v.tensor_scalar(k2, lp, LOG2E, MAGIC, ALU.mult, ALU.add))
                        ch.link(v.tensor_scalar(k2, k2, -MAGIC, None, ALU.add))
                        ch.link(v.scalar_tensor_tensor(rem, k2, -LN2_HI, lp, ALU.mult, ALU.add))
                        v.scalar_tensor_tensor(rem, k2, -LN2_LO, rem, ALU.mult, ALU.add).then_inc(rem_ready, 1)
                        ch.link(v.tensor_scalar(k2, k2, -127.0, 127.0, ALU.max, ALU.add))
                        ch.link(v.tensor_scalar(pow2[:, :], k2, 8388608.0, None, ALU.mult))
                    if ahead(n, 2):
                        need(v, xT_ready, n + 2)
                        v.tensor_scalar(xn[:, :], X[:, bass.ds((n + 2) * D, D)], k["mean"][:, bass.ds(n + 2, 1)],
                                        k["rstd"][:, bass.ds(n + 2, 1)], ALU.subtract, ALU.mult).then_inc(xn_ready, 1)
                    if ahead(n, -1):
                        v.wait_ge(yh_ready, n)
                        v.tensor_tensor(yl[:, :], psY[:, 0:KH], yh[:, :].bitcast(F32), ALU.subtract).then_inc(yl_ready, 1)
                    if ahead(n, 1):
                        v.wait_ge(whole_ready, n + 2)
                        f = feat[1 - par]
                        v.scalar_tensor_tensor(f[:, CH:2 * CH], f[:, 0:CH], -MAGIC, turns[:, :],
                                               ALU.add, ALU.subtract).then_inc(frac_ready, 1)
                        v.wait_ge(tanh_ready, n + 2)
                        ch.link(v.tensor_scalar(t1, th, -1.0, 1.0, ALU.mult, ALU.add))
                        ch.link(v.reciprocal(t2, t1))
                        ch.link(v.scalar_tensor_tensor(t1, th, 1.0, t2, ALU.add, ALU.mult))
                        need(v, den_ready, n)
                        need(v, v_ready, 2 * n)
                        v.tensor_tensor(pw[1 - par][:, :], t1, pow2[:, :].bitcast(F32), ALU.mult).then_inc(p_ready, 1)

                    def between():
                        if ahead(n, 2):
                            v.wait_ge(xh_ready, n + 3)
                            need(v, mem_ready, n + 1)
                            need(v, q_ready, n + 1)
                            x3 = [t[:, :].rearrange("p (c t) -> p c t", c=CB) for t in xl]
                            h3 = xh[par][:, :].rearrange("p (c t) -> p c t", c=CB)
                            if isinstance(n, int) and n == -2:
                                ch.link(v.memset(x3[par][:, :, 0:TAPS - 1].bitcast(F32), 0.0))
                            else:
                                v.wait_ge(xl_ready, n + 2)
                                ch.link(v.tensor_copy(x3[par][:, :, 0:TAPS - 1],
                                                      x3[1 - par][:, :, P:P + TAPS - 1].bitcast(F32)))
                            v.tensor_tensor(x3[par][:, :, TAPS - 1:TAPS - 1 + P],
                                            psT[:, 0:D].rearrange("p (c t) -> p c t", c=CB),
                                            h3[:, :, TAPS - 1:TAPS - 1 + P].bitcast(F32), ALU.subtract).then_inc(xl_ready, 1)
                        if ahead(n, -1):
                            v.wait_ge(out_ready, n)
                            xs = X[:, bass.ds((n - 1) * D, D)]
                            v.tensor_tensor(xs, psY[:, D:2 * D], xs, ALU.add).then_inc(x_added, 1)
                            v.wait_ge(x_added, n)
                            v.bn_stats(k["st"][:, bass.ds((n - 1) * 6, 6)], xs)
                        if has(n):
                            v.wait_ge(den_ready, n + 1)
                            if ahead(n, 1):
                                need(v, row_moved, 16 * n)
                                v.tensor_copy(srow[96:P, 2 * CH:ROW], den[96:P, :])
                            v.tensor_scalar(rden[:, 0:K], den, 1e-4, None, ALU.max).then_inc(den_read, 1)

                    if has(n):
                        y2v = y2[:, :].rearrange("p (c f) -> p c f", c=2)
                        for e in range(CHUNKS):
                            part, q = 1 - e // KQ, e % KQ
                            v.wait_ge(sums_ready, 8 * n + (e + 1))
                            if e == 0:
                                v.wait_ge(q_copied, n + 1)
                            pr = prod
                            v.tensor_tensor(pr[:, (e % 2) * CHUNK:(e % 2 + 1) * CHUNK].rearrange("p (r f) -> p r f", r=REP),
                                            psS[e % 4][:, :].rearrange("p (r f) -> p r f", r=REP),
                                            qs[par][:, part * QW + q * HM:part * QW + (q + 1) * HM].unsqueeze(1).to_broadcast([P, REP, HM]),
                                            ALU.mult).then_inc(prod_done, 1)
                            if e % 2 == 1:
                                v.wait_ge(prod_done, 8 * n + (e + 1))
                                ch.link(v.tensor_reduce(y2v[:, part, (q - 1) * HM:(q + 1) * HM],
                                                        pr[:, :].rearrange("p (c m) -> p c m", m=M), AX.X, ALU.add))
                            if e == 3:
                                between()
                        v.wait_ge(den_read, n + 1)
                        ch.link(v.reciprocal(rden[:, K:2 * K], rden[:, 0:K]))
                        ch.link(v.tensor_tensor(y2[:, 0:KH], y2[:, 0:KH], y2[:, KH:2 * KH], ALU.add))
                        need(v, yT_ready, n)
                        v.tensor_tensor(y[:, :].rearrange("p (k h) -> p k h", h=H),
                                        y2[:, 0:KH].rearrange("p (k h) -> p k h", h=H),
                                        rden[:, K:2 * K].unsqueeze(2).to_broadcast([P, K, H]), ALU.mult).then_inc(y_ready, 1)
                    else:
                        between()

                steps(v, step, ch, 2 * DVE_LINKS)
                ch.link(v.memset(tmp[:, 0:1], 0.0))
                rsqrt_rows(ch, v, k, tmp)

            @block.gpsimd
            def _(g):
                g.memset(ones[:, :], 1.0).then_inc(ones_set, 1)
                g.wait_ge(ones_set, 1)

                def step(n, par):
                    if ahead(n, 1):
                        g.wait_ge(p_ready, n + 2)
                        for i, part in enumerate((1, 0)):
                            g.wait_ge(feat_ready, 2 * n + 3 + i)
                            f = feat[1 - par][:, part * CH:(part + 1) * CH].rearrange("p (k f) -> p k f", k=K)
                            g.tensor_tensor(f, f, pw[1 - par][:, :].unsqueeze(2).to_broadcast([P, K, HM]),
                                            ALU.mult).then_inc(v_ready, 1)
                    if has(n) and ahead(n, 1):
                        g.wait_ge(row_moved, 16 * n + 16)
                        need(g, carry_in, 32 * n)
                        g.tensor_tensor(split[:, 0:RW], crow[:, :], ones[:, :], ALU.mult).then_inc(split_ready, 1)
                        g.wait_ge(split_ready, 2 * n + 1)
                        g.tensor_tensor(split[:, RW:2 * RW], crow[:, :], split[:, 0:RW].bitcast(F32),
                                        ALU.subtract).then_inc(split_ready, 1)

                steps(g, step)

            @block.sync
            def _(sp):
                def step(n, par):
                    if has(n) and ahead(n, 1):
                        sp.wait_ge(row_ready, 8 * n + 8)
                        sp.dma_start(crow[:, :], srow[P - 1:P, :].rearrange("o (r w) -> o r w", r=RP)).then_inc(row_moved, 16)
                        sp.wait_ge(split_ready, 2 * n + 2)
                        sp.wait_ge(sums_ready, 8 * n + 8)
                        for i in range(2):
                            sp.dma_start(carry[i:i + 1, :].bitcast(F32).rearrange("o (r w) -> o r w", r=RP),
                                         split[:, i * RW:(i + 1) * RW].bitcast(F32)).then_inc(carry_in, 16)

                steps(sp, step)


def kernel(**inputs):
    import concourse.bacc as bacc
    from concourse.bass_utils import run_bass_kernel_spmd

    g = {n[3:]: np.asarray(v) for n, v in inputs.items()}
    nk = KH + K
    w_in = g["attn_W_in"]
    wq = w_in[:, nk:].reshape(D, KQ, H, M, 2)
    arrays = {
        "x": g["attn_x"].reshape(TOKENS, D),
        "w1t": np.concatenate([g["ffn_w1_stack"].reshape(E * FE, D), g["ffn_ws1"]]).T,
        "w2t": np.concatenate([g["ffn_w2_stack"].transpose(0, 2, 1).reshape(E * FE, D), g["ffn_ws2"].T]),
        "wrt": g["ffn_w_router"].T,
        "w_out": g["attn_W_out"],
        "w_mem": w_in[:, :nk],
        "w_qre": wq[..., 0].reshape(D, QW),
        "w_qim": wq[..., 1].reshape(D, QW),
        "conv_k": g["attn_conv_k"].reshape(TAPS * MEM),
        "theta": g["attn_theta"].reshape(CH),
        "norm_scale": g["attn_norm_scale"],
        "re_diag": np.diagonal(g["attn_W_re"]),
        "im_diag": np.diagonal(g["attn_W_im"]),
        "slopes": np.concatenate([g["attn_decay_slopes"], g["attn_anchor_slopes"]]),
        "score_scale": g["attn_score_scale"],
    }
    arrays = {n: np.ascontiguousarray(v) for n, v in arrays.items()}
    nc = bacc.Bacc("TRN2", target_bir_lowering=False, num_devices=1)
    aps = {n: nc.dram_tensor("in_" + n, v.shape, F32, kind="ExternalInput").ap() for n, v in arrays.items()}
    aps["out"] = nc.dram_tensor("out_x", (TOKENS, D), F32, kind="ExternalOutput").ap()
    build(nc, aps)
    r = run_bass_kernel_spmd(nc, [{"in_" + n: v for n, v in arrays.items()}], core_ids=[0])
    return r.results[0]["out_x"].reshape(1, TOKENS, D)
```

```python
import math
from contextlib import ExitStack

import numpy as np
import concourse.bass as bass
from concourse import mybir

F32 = mybir.dt.float32
F32R = mybir.dt.float32r
I32 = mybir.dt.int32
U32 = mybir.dt.uint32
ALU = mybir.AluOpType
ACT = mybir.ActivationFunctionType
AX = mybir.AxisListType

P = 128
TOKENS, D = 4096, 256
TILES = TOKENS // P
CB = D // P
E, FE, FS = 8, 256, 512
FALL = E * FE + FS
FB = FALL // P
UNITS = FALL // FE
GT = 4
GROUPS = TILES // GT
GN = GT * P
K, H, M, KQ, TAPS = 32, 8, 8, 4, 4
NDECAY = 28
KH = K * H
CH = K * H * M
HM = H * M
REP = K // KQ
QW = KQ * HM
MEM = KH + K
CHUNK = REP * HM
CHUNKS = 2 * KQ
ROW = 2 * CH + K
RW = 32
HALF = (CH // RW, (CH + K) // RW)
EPS = 1e-5
TOP = 2
PT = 2 * P
PAIRS = (TOP * TOKENS + E * (PT - 1)) // PT
MAGIC = 12582912.0
LOG2E = 1.0 / math.log(2.0)
LN2_HI = 0.693359375
LN2_LO = math.log(2.0) - LN2_HI


class Chain:

    def __init__(self, eng, sem):
        self.eng, self.sem, self.base, self.n = eng, sem, 0, 0

    def mark(self, ins):
        ins.then_inc(self.sem, 1)
        self.n += 1
        return self.base + self.n

    def wait(self, mark):
        self.eng.wait_ge(self.sem, mark)

    def link(self, ins):
        self.wait(self.mark(ins))

    def enter(self, it, per):
        self.start, self.per, self.before = self.n, per, self.base
        self.base = it * per

    def leave(self, passes):
        assert self.n - self.start == self.per, (self.n - self.start, self.per)
        self.base = 0
        self.n = self.start + self.per * passes


ACT_LINKS, DVE_LINKS = 2, 17
OUT_AFTER = 7


def chunk_cols(e):
    lo = (1 - e // KQ) * CH + (e % KQ) * CHUNK
    return lo, lo + CHUNK


def row_cols(e):
    return e * CHUNK, (e + 1) * CHUNK


def need(eng, sem, value):
    if not (isinstance(value, int) and value <= 0):
        eng.wait_ge(sem, value)


def build(nc, a):
    with ExitStack() as top:
        def sem(name):
            return top.enter_context(nc.semaphore(name))

        def sb(stack, name, shape, dt=F32):
            return stack.enter_context(nc.sbuf_tensor(name, shape, dt))

        k = {}
        k["x"] = sb(top, "x_all", [P, TILES * D])
        for part in ("hi", "lo"):
            k["w1" + part] = sb(top, "w1" + part, [P, CB * FALL], F32R)
            k["wo" + part] = sb(top, "wo" + part, [P, CB * D], F32R)
            k["wc" + part] = sb(top, "wc" + part, [P, CB * TAPS * MEM], F32R)
            k["wq" + part] = sb(top, "wq" + part, [P, CB * 2 * QW], F32R)
        k["wr"] = sb(top, "w_router", [P, CB * E])
        k["theta"] = sb(top, "theta_turns", [P, CH])
        k["ident"] = sb(top, "ident", [P, P])
        k["halfpi"] = sb(top, "half_pi", [P, 1])
        k["tri"] = sb(top, "tri", [P, P])
        k["ones"] = sb(top, "ones", [P, P])
        k["ones2"] = sb(top, "ones2", [2, P], F32R)
        k["slope"] = sb(top, "neg_slope", [P, K])
        k["sscale"] = sb(top, "score_scale", [P, K])
        k["pos"] = sb(top, "pos_all", [P, TILES])
        k["dist"] = sb(top, "dist_all", [P, TILES])
        k["iota8"] = sb(top, "iota8", [P, E])
        k["st"] = sb(top, "bn_all", [P, TILES * 6])
        k["mean"] = sb(top, "mean_all", [P, TILES])
        k["rstd"] = sb(top, "rstd_all", [P, TILES])

        setup(nc, a, k, sem, sb)
        k["moved"] = {ph: [sem(f"{ph}_moved{i}") for i in range(2 * TILES // GROUPS)] for ph in ("f1s", "f1c", "f2s", "f2c")}
        with_semaphores(nc, lambda sem: ffn(nc, a, k, sem, sb, "f1", store=False))
        with_semaphores(nc, lambda sem: attention(nc, a, k, sem, sb))
        with_semaphores(nc, lambda sem: ffn(nc, a, k, sem, sb, "f2", store=True))


def with_semaphores(nc, part):
    taken = []

    def sem(name):
        taken.append(nc.alloc_semaphore(name=name))
        return taken[-1]

    part(sem)
    nc.clear_and_free_semaphores(taken)
    nc.all_engine_barrier()


def rsqrt_rows(ch, v, k, tmp):
    st = k["st"][:, :].rearrange("p (n s) -> p n s", s=6)
    var, t, y = tmp[:, 0:TILES], tmp[:, TILES:2 * TILES], k["rstd"][:, :]
    ch.link(v.tensor_tensor(t, st[:, :, 1], st[:, :, 4], ALU.subtract))
    ch.link(v.tensor_tensor(t, t, t, ALU.mult))
    ch.link(v.tensor_tensor(var, st[:, :, 2], st[:, :, 5], ALU.add))
    ch.link(v.tensor_scalar(var, var, 1.0 / D, EPS, ALU.mult, ALU.add))
    ch.link(v.scalar_tensor_tensor(var, t, 0.25, var, ALU.mult, ALU.add))
    ch.link(v.tensor_tensor(t, st[:, :, 1], st[:, :, 4], ALU.add))
    ch.link(v.tensor_scalar(k["mean"][:, :], t, 0.5, None, ALU.mult))
    ch.link(v.tensor_copy(t, var.bitcast(I32)))
    ch.link(v.tensor_scalar(y.bitcast(I32), t, -0.5, 1597463007.0, ALU.mult, ALU.add))
    for _ in range(4):
        ch.link(v.tensor_tensor(t, y, y, ALU.mult))
        ch.link(v.tensor_tensor(t, t, var, ALU.mult))
        ch.link(v.tensor_scalar(t, t, -0.5, 1.5, ALU.mult, ALU.add))
        ch.link(v.tensor_tensor(y, y, t, ALU.mult))


def setup(nc, a, k, sem, sb):
    SW = FALL
    ZT = 6
    with ExitStack() as c:
        stage = [sb(c, f"stage{i}", [P, SW]) for i in range(3)]
        convb = sb(c, "conv_rows", [P, TAPS * MEM])
        qstage = sb(c, "q_stage", [P, CB * 2 * QW])
        qtmp = sb(c, "q_tmp", [P, CB * QW])
        small = sb(c, "small", [P, 4 * H + 8 * K])
        zeros, zeroed, slots_zeroed = sb(c, "zeros", [P, ZT * D]), sem("zeroed"), sem("slots_zeroed")
        ipos = sb(c, "ipos", [P, TILES], I32)
        tmp = sb(c, "root_tmp", [P, 2 * TILES])
        weights_in = [sem(f"weights_in{i}") for i in range(3)]
        smalls_in, x_in = sem("smalls_in"), [sem(f"x_in{g}") for g in range(GROUPS)]
        hi_done, lo_done = sem("w_hi_done"), sem("w_lo_done")
        folded, sp_exp, consts, g_chain = sem("folded"), sem("sp_exp"), sem("consts"), sem("setup_pool_chain")
        v_chain, sp_in = sem("setup_dve_chain"), sem("softplus_in")

        w1v = a["w1t"].rearrange("(c p) f -> p c f", p=P)
        def pair(name, lo, n):
            return [k[name + part][:, lo:lo + n] for part in ("hi", "lo")]

        loads = [(SW, w1v[:, 0, :], pair("w1", 0, SW)), (SW, w1v[:, 1, :], pair("w1", SW, SW)),
                 (CB * D, a["w_out"].rearrange("(c p) f -> p c f", p=P), pair("wo", 0, CB * D))]
        NL = len(loads)
        xv = a["x"].rearrange("(n p) d -> p n d", p=P)

        with nc.Block() as block:
            @block.sync
            def _(sp):
                for g in range(GROUPS):
                    sp.dma_start(k["x"][:, g * GT * D:(g + 1) * GT * D].rearrange("p (n d) -> p n d", d=D),
                                 xv[:, g * GT:(g + 1) * GT, :]).then_inc(x_in[g], 16)
                sp.wait_ge(zeroed, 1)
                zv = a["slots_x"].rearrange("(n p) d -> p n d", p=P)
                for i in range(2 * PAIRS // ZT):
                    sp.dma_start(zv[:, ZT * i:ZT * (i + 1), :], zeros[:, :].rearrange("p (n d) -> p n d", d=D)).then_inc(slots_zeroed, 16)
                for i, (n, src, _) in enumerate(loads):
                    if i >= 3:
                        sp.wait_ge(lo_done, i - 2)
                    sp.dma_start(stage[i % 3][:, 0:n].rearrange("p (c f) -> p c f", c=src.shape[1]),
                                 src).then_inc(weights_in[i % 3], 16)
                sp.wait_ge(lo_done, NL)
                winv = a["w_mem"].rearrange("(c p) f -> p c f", p=P)
                sp.dma_start(stage[0][:, 0:CB * MEM].rearrange("p (c f) -> p c f", c=CB), winv).then_inc(smalls_in, 16)
                for i, nm in ((1, "w_qre"), (2, "w_qim")):
                    sp.dma_start(stage[i][:, 0:CB * QW].rearrange("p (c f) -> p c f", c=CB),
                                 a[nm].rearrange("(c p) f -> p c f", p=P)).then_inc(smalls_in, 16)
                sp.wait_ge(slots_zeroed, 16 * (2 * PAIRS // ZT))

            @block.gpsimd
            def _(g):
                ch = Chain(g, g_chain)
                g.memset(zeros[:, :], 0.0).then_inc(zeroed, 1)
                for nm in ("ident", "tri"):
                    ch.link(g.memset(k[nm][:, :], 0.0 if nm == "ident" else 1.0))
                ch.link(g.affine_select(out=k["ident"][:, :], in_=k["ident"][:, :], compare_op=ALU.not_equal,
                                        fill=1.0, base=0, pattern=[[-1, P]], channel_multiplier=1))
                ch.link(g.affine_select(out=k["tri"][:, :], in_=k["tri"][:, :], compare_op=ALU.is_ge,
                                        fill=0.0, base=0, pattern=[[1, P]], channel_multiplier=-1))
                ch.link(g.memset(k["ones"][:, :], 1.0))
                g.memset(k["ones2"][:, :].bitcast(F32), 1.0).then_inc(consts, 1)
                g.iota(ipos[:, :], pattern=[[P, TILES]], base=0, channel_multiplier=1).then_inc(consts, 1)

            @block.scalar
            def _(act):
                bc = lambda ap: ap.partition_broadcast(P)
                act.dma_start(convb[:, :], bc(a["conv_k"])).then_inc(smalls_in, 16)
                act.dma_start(k["theta"][:, :], bc(a["theta"])).then_inc(smalls_in, 16)
                act.dma_start(small[:, 0:2 * H], bc(a["norm_scale"])).then_inc(smalls_in, 16)
                act.dma_start(small[:, 2 * H:3 * H], bc(a["re_diag"])).then_inc(smalls_in, 16)
                act.dma_start(small[:, 3 * H:4 * H], bc(a["im_diag"])).then_inc(smalls_in, 16)
                act.dma_start(small[:, 4 * H:4 * H + K], bc(a["slopes"])).then_inc(smalls_in, 16)
                act.dma_start(k["sscale"][:, :], bc(a["score_scale"])).then_inc(smalls_in, 16)
                act.dma_start(k["wr"][:, :].rearrange("p (c f) -> p c f", c=CB),
                              a["wrt"].rearrange("(c p) f -> p c f", p=P)).then_inc(smalls_in, 16)
                for i, (n, _, (hi, lo)) in enumerate(loads):
                    act.wait_ge(weights_in[i % 3], 16 * (i // 3 + 1))
                    act.activation(hi, stage[i % 3][:, 0:n], ACT.Copy).then_inc(hi_done, 1)
                act.wait_ge(sp_in, 1)
                act.activation(small[:, 4 * H + K:4 * H + 2 * K], small[:, 4 * H + K:4 * H + 2 * K],
                               ACT.Exp).then_inc(sp_exp, 1)
                for j in range(TAPS):
                    act.wait_ge(folded, j + 1)
                    act.activation(k["wchi"][:, :].rearrange("p (c j f) -> p c j f", c=CB, j=TAPS)[:, :, j, :],
                                   qstage[:, 0:CB * MEM].rearrange("p (c f) -> p c f", c=CB),
                                   ACT.Copy).then_inc(hi_done, 1)
                act.wait_ge(folded, TAPS + 1)
                act.activation(k["wqhi"][:, :], qstage[:, :], ACT.Copy).then_inc(hi_done, 1)

            @block.vector
            def _(v):
                ch = Chain(v, v_chain)
                for g in range(GROUPS):
                    v.wait_ge(x_in[g], 16)
                    for i in range(g * GT, (g + 1) * GT):
                        ins = v.bn_stats(k["st"][:, 6 * i:6 * i + 6], k["x"][:, i * D:(i + 1) * D])
                ch.link(ins)
                rsqrt_rows(ch, v, k, tmp)
                ch.link(v.memset(k["halfpi"][:, :], math.pi / 2.0))
                for e in range(E):
                    ch.link(v.memset(k["iota8"][:, e:e + 1], float(e)))
                for i, (n, _, (hi, lo)) in enumerate(loads):
                    v.wait_ge(weights_in[i % 3], 16 * (i // 3 + 1))
                    v.wait_ge(hi_done, i + 1)
                    v.tensor_tensor(lo, stage[i % 3][:, 0:n], hi.bitcast(F32), ALU.subtract).then_inc(lo_done, 1)
                v.wait_ge(consts, 2)
                ch.link(v.tensor_copy(k["pos"][:, :], ipos[:, :]))
                ch.link(v.tensor_scalar(k["dist"][:, :], k["pos"][:, :], -1.0, float(TOKENS - 1), ALU.mult, ALU.add))
                v.wait_ge(smalls_in, 16 * 11)
                ch.link(v.tensor_scalar(k["theta"][:, :], k["theta"][:, :], 1.0 / (2.0 * math.pi), None, ALU.mult))
                o = 4 * H
                s, e_, z, z2, q, r = (small[:, o + i * K:o + (i + 1) * K] for i in range(6))
                ch.link(v.tensor_scalar(z, s, -1.0, None, ALU.mult))
                ch.link(v.tensor_tensor(e_, s, z, ALU.min))
                v.tensor_copy(q, e_).then_inc(sp_in, 1)
                v.wait_ge(sp_exp, 1)
                ch.link(v.tensor_scalar(z2, e_, 2.0, None, ALU.add))
                ch.link(v.reciprocal(r, z2))
                ch.link(v.tensor_tensor(z, e_, r, ALU.mult))
                ch.link(v.tensor_tensor(z2, z, z, ALU.mult))
                ch.link(v.memset(q, 1.0 / 19.0))
                for n in range(17, 0, -2):
                    ch.link(v.tensor_tensor(q, q, z2, ALU.mult))
                    ch.link(v.tensor_scalar(q, q, 1.0 / n, None, ALU.add))
                ch.link(v.tensor_tensor(q, q, z, ALU.mult))
                ch.link(v.tensor_scalar(s, s, 0.0, None, ALU.max))
                ch.link(v.scalar_tensor_tensor(q, q, 2.0, s, ALU.mult, ALU.add))
                ch.link(v.tensor_scalar(k["slope"][:, :], q, -1.0, None, ALU.mult))
                wm = stage[0][:, 0:CB * MEM].rearrange("p (c f) -> p c f", c=CB)
                for j in range(TAPS):
                    if j:
                        v.wait_ge(lo_done, NL + j)
                    tap = convb[:, j * MEM:(j + 1) * MEM].unsqueeze(1).to_broadcast([P, CB, MEM])
                    v.tensor_tensor(qstage[:, 0:CB * MEM].rearrange("p (c f) -> p c f", c=CB), wm, tap,
                                    ALU.mult).then_inc(folded, 1)
                    v.wait_ge(folded, j + 1)
                    v.wait_ge(hi_done, NL + j + 1)
                    v.tensor_tensor(k["wclo"][:, :].rearrange("p (c j f) -> p c j f", c=CB, j=TAPS)[:, :, j, :],
                                    qstage[:, 0:CB * MEM].rearrange("p (c f) -> p c f", c=CB),
                                    k["wchi"][:, :].bitcast(F32).rearrange("p (c j f) -> p c j f", c=CB, j=TAPS)[:, :, j, :],
                                    ALU.subtract).then_inc(lo_done, 1)
                v.wait_ge(lo_done, NL + TAPS)
                ch.link(v.tensor_tensor(small[:, 2 * H:3 * H], small[:, 0:H], small[:, 2 * H:3 * H], ALU.mult))
                ch.link(v.tensor_tensor(small[:, 3 * H:4 * H], small[:, H:2 * H], small[:, 3 * H:4 * H], ALU.mult))

                def hs(i):
                    return small[:, i * H:(i + 1) * H].unsqueeze(1).unsqueeze(3).to_broadcast([P, KQ, H, M])

                def v4(ap):
                    return ap.rearrange("p (q h m) -> p q h m", q=KQ, h=H)

                for cb in range(CB):
                    re = v4(stage[1][:, cb * QW:(cb + 1) * QW])
                    im = v4(stage[2][:, cb * QW:(cb + 1) * QW])
                    t = v4(qtmp[:, cb * QW:(cb + 1) * QW])
                    q1 = v4(qstage[:, cb * 2 * QW:cb * 2 * QW + QW])
                    q2 = v4(qstage[:, cb * 2 * QW + QW:(cb + 1) * 2 * QW])
                    ch.link(v.tensor_tensor(q1, re, hs(2), ALU.mult))
                    ch.link(v.tensor_tensor(t, im, hs(3), ALU.mult))
                    ch.link(v.tensor_tensor(q1, q1, t, ALU.subtract))
                    ch.link(v.tensor_tensor(q2, im, hs(2), ALU.mult))
                    ch.link(v.tensor_tensor(t, re, hs(3), ALU.mult))
                    last = v.tensor_tensor(q2, q2, t, ALU.add)
                    if cb < CB - 1:
                        ch.link(last)
                last.then_inc(folded, 1)
                v.wait_ge(folded, TAPS + 1)
                v.wait_ge(hi_done, NL + TAPS + 1)
                v.tensor_tensor(k["wqlo"][:, :], qstage[:, :], k["wqhi"][:, :].bitcast(F32),
                                ALU.subtract).then_inc(lo_done, 1)


def ffn(nc, a, k, sem, sb, ph, store):
    with ExitStack() as c:
        t = {"w2" + part: sb(c, ph + "w2" + part, [P, FB * D], F32R) for part in ("hi", "lo")}
        t["slot"] = sb(c, ph + "slot", [P, TILES * TOP], U32)
        t["gate"] = sb(c, ph + "gate", [P, TILES * TOP])
        t["expert"] = sb(c, ph + "expert", [1, PAIRS], I32)
        route(nc, a, k, t, sem, sb, ph + "r_")
        shared(nc, a, k, t, sem, sb, ph + "s_", 0, scatter=True)
        experts(nc, a, k, t, sem, sb, ph + "e_")
        shared(nc, a, k, t, sem, sb, ph + "c_", GROUPS // 2, scatter=False)
        finish(nc, a, k, sem, sb, ph + "z_", store)


def normalise(v, k, n, dst):
    return v.tensor_scalar(dst, k["x"][:, bass.ds(n * D, D)], k["mean"][:, bass.ds(n, 1)],
                           k["rstd"][:, bass.ds(n, 1)], ALU.subtract, ALU.mult)


def route(nc, a, k, t, sem, sb, ph):
    with ExitStack() as c:
        s = lambda n: sem(ph + n)
        raw = [sb(c, f"{ph}w2raw{i}", [P, FE // P * D]) for i in range(2)]
        xn = [sb(c, f"{ph}xn{i}", [P, GT * D]) for i in range(2)]
        xT = [sb(c, f"{ph}xT{i}", [P, CB * GN]) for i in range(2)]
        best, least = (sb(c, ph + n, [P, TOP * TILES]) for n in ("best", "least"))
        ge, den = (sb(c, ph + n, [P, TILES]) for n in ("ge", "den"))
        W = TILES * E
        oh = [sb(c, f"{ph}oh{j}", [P, W]) for j in range(TOP)]
        lg, eq, ids, ids8 = (sb(c, ph + n, [P, W]) for n in ("lg", "eq", "ids", "ids8"))
        both, run, pos, one = (sb(c, ph + n, [P, W]) for n in ("both", "run", "pos", "one"))
        e8 = sb(c, ph + "e8", [P, 4 * E])
        slotf = sb(c, ph + "slotf", [P, TILES])
        tile_no = sb(c, ph + "pair_no", [1, PAIRS], I32)
        tile_f = sb(c, ph + "pair_f", [1, PAIRS])
        past = sb(c, ph + "past", [1, PAIRS * E])
        psT = [c.enter_context(nc.psum_tensor(f"{ph}psT{i}", [P, GN], F32)) for i in range(2 * CB)]
        psL, psR, psC = (c.enter_context(nc.psum_tensor(ph + n, [P, GN], F32)) for n in ("psL", "psR", "psC"))
        w2_in, w2_ready = [s(f"w2_in{i}") for i in range(2)], s("w2_ready")
        xn_ready, xT_ready, xT_copied = s("xn_ready"), s("xT_ready"), [s(f"xT_copied{cb}") for cb in range(CB)]
        logits_ready, logits_read, gap_ready, exp_ready = s("logits_ready"), s("logits_read"), s("gap_ready"), s("exp_ready")
        chosen_ready, ranks_ready, iota_ready, chain = s("chosen_ready"), s("ranks_ready"), s("iota_ready"), s("dve_chain")
        FU = FE // P

        def steps(eng, step):
            for n in range(-2, 2):
                step(n, n % 2)
            with eng.Fori(0, (GROUPS - 4) // 2) as it:
                for par in range(2):
                    step(it * 2 + (2 + par), par)
            for n in range(GROUPS - 2, GROUPS):
                step(n, n % 2)

        def ahead(n, by):
            return not isinstance(n, int) or 0 <= n + by < GROUPS

        with nc.Block() as block:
            @block.tensor
            def _(pe):
                def step(n, par):
                    odd = 1 - par
                    if ahead(n, 1):
                        pe.wait_ge(xn_ready, n + 2)
                        for cb in range(CB):
                            need(pe, xT_copied[cb], n)
                            for i in range(GT):
                                ins = pe.transpose(psT[odd * CB + cb][:, i * P:(i + 1) * P],
                                                   xn[odd][:, i * D + cb * P:i * D + (cb + 1) * P], k["ident"][:, :])
                            ins.then_inc(xT_ready, 1)
                    if ahead(n, 0):
                        for cb in range(CB):
                            pe.wait_ge(xT_copied[cb], n + 1)
                        need(pe, logits_read, n)
                        for i in range(GT):
                            for cb in range(CB):
                                ins = pe.matmul(psL[:, i * E:(i + 1) * E], xT[par][:, cb * GN + i * P:cb * GN + (i + 1) * P],
                                                k["wr"][:, cb * E:(cb + 1) * E], start=(cb == 0), stop=(cb == CB - 1))
                        ins.then_inc(logits_ready, 1)

                steps(pe, step)
                pe.wait_ge(chosen_ready, 1)
                pe.matmul(psR[:, 0:W], k["tri"][:, :], both[:, :], start=True, stop=True)
                pe.matmul(psC[:, 0:W], k["ones"][:, :], both[:, :], start=True, stop=True).then_inc(ranks_ready, 1)

            @block.scalar
            def _(act):
                def step(n, par):
                    odd = 1 - par
                    if ahead(n, 1):
                        act.wait_ge(xT_ready, CB * (n + 1) + 1)
                        need(act, logits_ready, n)
                        act.activation(xT[odd][:, 0:GN], psT[odd * CB][:, :], ACT.Copy).then_inc(xT_copied[0], 1)

                steps(act, step)
                act.wait_ge(gap_ready, 1)
                act.activation(ge[:, :], den[:, :], ACT.Exp).then_inc(exp_ready, 1)

            @block.vector
            def _(v):
                ch = Chain(v, chain)
                best3 = best[:, :].rearrange("p (j n) -> p j n", j=TOP)
                least3 = least[:, :].rearrange("p (j n) -> p j n", j=TOP)

                def step(n, par):
                    odd = 1 - par
                    if ahead(n, 1):
                        v.wait_ge(xT_ready, CB * (n + 1) + 2)
                        need(v, logits_ready, n)
                        v.tensor_copy(xT[odd][:, GN:2 * GN], psT[odd * CB + 1][:, :]).then_inc(xT_copied[1], 1)
                    if ahead(n, 2):
                        need(v, xT_ready, CB * (n + 1))
                        for i in range(GT):
                            ins = normalise(v, k, (n + 2) * GT + i, xn[par][:, i * D:(i + 1) * D])
                        ins.then_inc(xn_ready, 1)
                    if ahead(n, 0):
                        v.wait_ge(logits_ready, n + 1)
                        v.tensor_copy(lg[:, bass.ds(n * (GT * E), GT * E)], psL[:, 0:GT * E]).then_inc(logits_read, 1)

                steps(v, step)

                def by_expert(ap):
                    return ap.rearrange("p (n e) -> p n e", e=E)

                def each(ap):
                    return ap.unsqueeze(2).to_broadcast([P, TILES, E])

                ch.link(v.tensor_copy(by_expert(ids[:, :]), k["iota8"][:, :].unsqueeze(1).to_broadcast([P, TILES, E])))
                ch.link(v.tensor_scalar(ids8[:, :], ids[:, :], float(-E), None, ALU.add))
                v.wait_ge(logits_read, GROUPS)
                for j in range(TOP):
                    ch.link(v.tensor_reduce(best3[:, j, :], by_expert(lg[:, :]), AX.X, ALU.max))
                    ch.link(v.tensor_tensor(by_expert(eq[:, :]), by_expert(lg[:, :]), each(best3[:, j, :]), ALU.is_equal))
                    ch.link(v.scalar_tensor_tensor(eq[:, :], eq[:, :], float(-E), ids[:, :], ALU.mult, ALU.add))
                    ch.link(v.tensor_reduce(least3[:, j, :], by_expert(eq[:, :]), AX.X, ALU.min))
                    ch.link(v.tensor_tensor(by_expert(oh[j][:, :]), by_expert(ids8[:, :]), each(least3[:, j, :]), ALU.is_equal))
                    if j == 0:
                        ch.link(v.scalar_tensor_tensor(lg[:, :], oh[0][:, :], -3e38, lg[:, :], ALU.mult, ALU.add))
                v.tensor_tensor(both[:, :], oh[0][:, :], oh[1][:, :], ALU.add).then_inc(chosen_ready, 1)
                v.tensor_tensor(den[:, :], best3[:, 1, :], best3[:, 0, :], ALU.subtract).then_inc(gap_ready, 1)
                ch.link(v.memset(one[:, :], 1.0))
                v.wait_ge(exp_ready, 1)
                gate3 = t["gate"][:, :].rearrange("p (j n) -> p j n", j=TOP)
                ch.link(v.tensor_scalar(den[:, :], ge[:, :], 2.0, 2.0, ALU.mult, ALU.add))
                ch.link(v.reciprocal(gate3[:, 0, :], den[:, :]))
                ch.link(v.tensor_tensor(gate3[:, 1, :], gate3[:, 0, :], ge[:, :], ALU.mult))
                v.wait_ge(ranks_ready, 1)
                ch.link(v.tensor_copy(pos[:, :], psC[:, 0:W]))
                for e in range(E):
                    ins = v.tensor_tensor_scan(by_expert(run[:, :])[:, :, e], by_expert(one[:, :])[:, :, e],
                                               by_expert(pos[:, :])[:, :, e], 0.0, ALU.mult, ALU.add)
                ch.link(ins)
                tiles, end, start, _ = (e8[:, i * E:(i + 1) * E] for i in range(4))
                ch.link(v.tensor_scalar(tiles, run[:, W - E:W], 1.0 / PT, 0.5 - 0.5 / PT, ALU.mult, ALU.add))
                ch.link(v.tensor_scalar(tiles, tiles, MAGIC, -MAGIC, ALU.add, ALU.add))
                ch.link(v.tensor_tensor_scan(end, one[:, 0:E], tiles, 0.0, ALU.mult, ALU.add))
                ch.link(v.tensor_tensor(start, end, tiles, ALU.subtract))
                ch.link(v.tensor_scalar(start, start, float(PT), -1.0, ALU.mult, ALU.add))
                ch.link(v.tensor_tensor(run[:, :], run[:, :], pos[:, :], ALU.subtract))
                ch.link(v.tensor_tensor(pos[:, :], run[:, :], psR[:, 0:W], ALU.add))
                ch.link(v.tensor_tensor(by_expert(pos[:, :]), by_expert(pos[:, :]),
                                        start.unsqueeze(1).to_broadcast([P, TILES, E]), ALU.add))
                for j in range(TOP):
                    ch.link(v.tensor_tensor(oh[j][:, :], oh[j][:, :], pos[:, :], ALU.mult))
                    ch.link(v.tensor_reduce(slotf[:, :], by_expert(oh[j][:, :]), AX.X, ALU.add))
                    ch.link(v.tensor_copy(t["slot"][:, j * TILES:(j + 1) * TILES], slotf[:, :]))
                v.wait_ge(iota_ready, 1)
                ch.link(v.tensor_copy(tile_f[:, :], tile_no[:, :]))
                past3 = past[:, :].rearrange("p (n e) -> p n e", e=E)
                ch.link(v.tensor_tensor(past3, tile_f[:, :].unsqueeze(2).to_broadcast([1, PAIRS, E]),
                                        end[0:1, :].unsqueeze(1).to_broadcast([1, PAIRS, E]), ALU.is_ge))
                ch.link(v.tensor_reduce(tile_f[:, :], past3, AX.X, ALU.add))
                ch.link(v.tensor_scalar(tile_f[:, :], tile_f[:, :], float(E - 1), None, ALU.min))
                ch.link(v.tensor_copy(t["expert"][:, :], tile_f[:, :]))

            @block.gpsimd
            def _(g):
                g.iota(tile_no[:, :], pattern=[[1, PAIRS]], base=0, channel_multiplier=0).then_inc(iota_ready, 1)
                for u in range(UNITS):
                    cols = slice(u * FU * D, (u + 1) * FU * D)
                    g.wait_ge(w2_in[u % 2], 16 * (u // 2 + 1))
                    g.tensor_copy(t["w2hi"][:, cols], raw[u % 2][:, :]).then_inc(w2_ready, 1)
                    g.wait_ge(w2_ready, 2 * u + 1)
                    g.tensor_tensor(t["w2lo"][:, cols], raw[u % 2][:, :], t["w2hi"][:, cols].bitcast(F32),
                                    ALU.subtract).then_inc(w2_ready, 1)

            @block.sync
            def _(sp):
                w2v = a["w2t"].rearrange("(u b p) d -> u p b d", p=P, b=FU)
                for u in range(UNITS):
                    if u >= 2:
                        sp.wait_ge(w2_ready, 2 * (u - 1))
                    sp.dma_start(raw[u % 2][:, :].rearrange("p (b d) -> p b d", d=D),
                                 w2v[u]).then_inc(w2_in[u % 2], 16)


def shared(nc, a, k, t, sem, sb, ph, g0, scatter):
    HALF = GROUPS // 2
    ST = TILES // HALF
    FSB, F0 = FS // P, E * FE // P
    with ExitStack() as c:
        s = lambda n: sem(ph + n)
        xn = sb(c, ph + "xn", [P, GT * D])
        xh, xl = (sb(c, ph + n, [P, CB * GN], F32R) for n in ("xh", "xl"))
        r, h = ([sb(c, f"{ph}{n}{i}", [P, GN]) for i in range(2)] for n in ("relu", "h"))
        hh, hl = ([sb(c, f"{ph}{n}{i}", [P, GN], F32R) for i in range(FSB)] for n in ("hh", "hl"))
        rows = [sb(c, f"{ph}rows{i}", [P, D if scatter else TOP * D]) for i in range(ST)]
        slot_now = sb(c, ph + "slot_now", [P, ST * TOP], U32)
        idle = sb(c, ph + "idle", [1, 3])
        psT = [c.enter_context(nc.psum_tensor(f"{ph}psT{i}", [P, GN], F32)) for i in range(CB)]
        psU = [c.enter_context(nc.psum_tensor(f"{ph}psU{i}", [P, GN], F32)) for i in range(FSB)]
        psO = [c.enter_context(nc.psum_tensor(f"{ph}psO{i}", [P, GN], F32)) for i in range(2)]
        xn_ready, xT_ready, xh_ready, xl_ready = s("xn_ready"), s("xT_ready"), s("xh_ready"), s("xl_ready")
        up_ready, relu_ready, h_ready, hh_ready, hl_ready = s("up_ready"), s("relu_ready"), s("h_ready"), s("hh_ready"), s("hl_ready")
        out_ready, out_added, slots_staged = s("out_ready"), s("out_added"), s("slots_staged")
        rows_ready, stats_done, idle_set = s("rows_ready"), s("stats_done"), s("idle_set")
        moved = k["moved"][ph[:-1]]

        def groups(eng, group):
            group(0)
            with eng.Fori(0, HALF - 2) as it:
                group(it + 1)
            group(HALF - 1)

        def last(g):
            return isinstance(g, int) and g == HALF - 1

        with nc.Block() as block:
            @block.tensor
            def _(pe):
                def transposes(g):
                    pe.wait_ge(xn_ready, g + 1)
                    for cb in range(CB):
                        for i in range(GT):
                            ins = pe.transpose(psT[cb][:, i * P:(i + 1) * P], xn[:, i * D + cb * P:i * D + (cb + 1) * P],
                                               k["ident"][:, :])
                        ins.then_inc(xT_ready, 1)

                def group(g):
                    pe.wait_ge(xh_ready, CB * (g + 1))
                    pe.wait_ge(xl_ready, CB * (g + 1))
                    need(pe, h_ready, FSB * g)
                    for f in range(FSB):
                        n = 0
                        for cb in range(CB):
                            w = slice(cb * FALL + (F0 + f) * P, cb * FALL + (F0 + f + 1) * P)
                            for xp, wp in ((xh, "hi"), (xl, "hi"), (xh, "lo")):
                                ins = pe.matmul(psU[f][:, :], k["w1" + wp][:, w], xp[:, cb * GN:(cb + 1) * GN],
                                                start=(n == 0), stop=(n == 5))
                                n += 1
                        ins.then_inc(up_ready, 1)
                    if not last(g):
                        transposes(g + 1)
                    need(pe, out_added, 2 * g)
                    for i in range(GT):
                        o = psO[i // 2][:, (i % 2) * D:(i % 2 + 1) * D]
                        for f in range(FSB):
                            if i == 0:
                                pe.wait_ge(hh_ready, g * FSB + (f + 1))
                                pe.wait_ge(hl_ready, g * FSB + (f + 1))
                            for n, (hp, wp) in enumerate(((hh, "hi"), (hl, "hi"), (hh, "lo"))):
                                ins = pe.matmul(o, hp[f][:, i * P:(i + 1) * P], t["w2" + wp][:, (F0 + f) * D:(F0 + f + 1) * D],
                                                start=(f == 0 and n == 0), stop=(f == FSB - 1 and n == 2))
                        if i % 2:
                            ins.then_inc(out_ready, 1)

                transposes(0)
                groups(pe, group)

            @block.scalar
            def _(act):
                def high(g):
                    for cb in range(CB):
                        act.wait_ge(xT_ready, g * CB + (cb + 1))
                        act.activation(xh[:, cb * GN:(cb + 1) * GN], psT[cb][:, :], ACT.Copy).then_inc(xh_ready, 1)

                def group(g):
                    need(act, out_ready, 2 * g)
                    for f in range(FSB + 1):
                        if f < FSB:
                            act.wait_ge(up_ready, g * FSB + (f + 1))
                            need(act, h_ready, g * FSB + (f - 1))
                            act.activation(r[f % 2][:, :], psU[f][:, :], ACT.Relu).then_inc(relu_ready, 1)
                        if f:
                            act.wait_ge(h_ready, g * FSB + f)
                            act.activation(hh[f - 1][:, :], h[(f - 1) % 2][:, :], ACT.Copy).then_inc(hh_ready, 1)
                    if not last(g):
                        high(g + 1)

                high(0)
                groups(act, group)

            @block.vector
            def _(v):
                X = k["x"]

                def norm(g):
                    for i in range(GT):
                        ins = normalise(v, k, (g0 + g) * GT + i, xn[:, i * D:(i + 1) * D])
                    ins.then_inc(xn_ready, 1)

                def low(g):
                    for cb in range(CB):
                        v.wait_ge(xh_ready, g * CB + (cb + 1))
                        v.tensor_tensor(xl[:, cb * GN:(cb + 1) * GN], psT[cb][:, :],
                                        xh[:, cb * GN:(cb + 1) * GN].bitcast(F32), ALU.subtract).then_inc(xl_ready, 1)

                def stage(g, half):
                    n = ST // 2
                    for j in range(TOP):
                        ins = v.tensor_copy(slot_now[:, j * ST + half * n:j * ST + (half + 1) * n],
                                            t["slot"][:, bass.ds(g * ST + (j * TILES + half * n), n)])
                    ins.then_inc(slots_staged, 1)

                def fill(g, i):
                    normalise(v, k, g * ST + i, rows[i][:, :]).then_inc(rows_ready, 1)

                def combine(g, i):
                    tiles = [(X[:, bass.ds((g * ST + i + q) * D, D)], g * ST + i + q) for q in range(2)]
                    done = g * (ST * TOP) + TOP * i
                    for j in range(TOP):
                        for q, (xs, n) in enumerate(tiles):
                            if j == 0:
                                v.wait_ge(moved[i + q], 32 * (g + 1))
                            else:
                                v.wait_ge(rows_ready, done + (q + 1))
                            v.scalar_tensor_tensor(xs, rows[i + q][:, j * D:(j + 1) * D], t["gate"][:, bass.ds(n + j * TILES, 1)],
                                                   xs, ALU.mult, ALU.add).then_inc(rows_ready, 1)
                    for q, (xs, n) in enumerate(tiles):
                        v.wait_ge(rows_ready, done + (q + 3))
                        v.bn_stats(k["st"][:, bass.ds(n * 6, 6)], xs).then_inc(stats_done, 1)

                def beside(g, i):
                    if scatter:
                        if last(g):
                            return
                        for q in range(2):
                            v.wait_ge(moved[i + q], 32 * (g + 1))
                            fill(g + 1, i + q)
                    else:
                        combine(g, i)
                    if (i + 2) % (ST // 2) == 0 and not last(g):
                        stage(g + 1, i // (ST // 2))

                def add(g):
                    for q in range(2):
                        v.wait_ge(out_ready, 2 * g + (q + 1))
                        xs = X[:, bass.ds((g0 + g) * GT * D + q * 2 * D, 2 * D)]
                        v.scalar_tensor_tensor(xs, psO[q][:, :], 0.5, xs, ALU.mult, ALU.add).then_inc(out_added, 1)

                def group(g):
                    need(v, out_added, 2 * g)
                    need(v, out_ready, 2 * g)
                    if not last(g):
                        v.wait_ge(xT_ready, CB * (g + 1))
                        norm(g + 1)
                    for f in range(FSB + 1):
                        if f < FSB:
                            v.wait_ge(relu_ready, g * FSB + (f + 1))
                            need(v, hh_ready, g * FSB + (f - 1))
                            need(v, hl_ready, g * FSB + (f - 1))
                            v.scalar_tensor_tensor(h[f % 2][:, :], psU[f][:, :], 0.0, r[f % 2][:, :],
                                                   ALU.max, ALU.mult).then_inc(h_ready, 1)
                        if f:
                            v.wait_ge(hh_ready, g * FSB + f)
                            v.tensor_tensor(hl[f - 1][:, :], h[(f - 1) % 2][:, :], hh[f - 1][:, :].bitcast(F32),
                                            ALU.subtract).then_inc(hl_ready, 1)
                    if not last(g):
                        low(g + 1)
                        for i in range(0, ST, 2):
                            beside(g, i)
                        add(g)
                    else:
                        for i in range(0, ST // 2, 2):
                            beside(g, i)
                        add(g)
                        v.wait_ge(out_added, 2 * HALF)
                        for i in range(ST // 2, ST, 2):
                            beside(g, i)

                norm(0)
                if scatter:
                    for i in range(ST):
                        fill(0, i)
                for half in range(2):
                    stage(0, half)
                low(0)
                group(0)
                with v.Fori(0, HALF - 2) as it:
                    group(it + 1)
                group(HALF - 1)

            @block.gpsimd
            def _(g):
                per = ST + 2 if scatter else 2

                def idle_for(sem_, value, it, nth):
                    g.wait_ge(idle_set, it * per + (nth + 1))
                    g.wait_ge(sem_, value)
                    g.tensor_tensor(idle[:, 2:3], idle[:, 0:1], idle[:, 1:2], ALU.add).then_inc(idle_set, 1)

                g.memset(idle[:, 0:2], 0.0).then_inc(idle_set, 1)
                g.wait_ge(idle_set, 1)
                with g.Fori(0, HALF) as it:
                    nth = 0
                    for i in range(ST):
                        if i % (ST // 2) == 0:
                            idle_for(slots_staged, 2 * it + (i // (ST // 2) + 1), it, nth)
                            nth += 1
                        if scatter:
                            idle_for(rows_ready, it * ST + (i + 1), it, nth)
                            nth += 1
                        for j in range(TOP):
                            where = bass.IndirectOffsetOnAxis(ap=slot_now[:, j * ST + i:j * ST + i + 1], axis=0)
                            if scatter:
                                ins = g.indirect_dma_start(out=a["slots_x"][:, :], out_offset=where, in_=rows[i][:, :], in_offset=None)
                            else:
                                ins = g.indirect_dma_start(out=rows[i][:, j * D:(j + 1) * D], out_offset=None,
                                                           in_=a["slots_y"][:, :], in_offset=where)
                            ins.then_inc(moved[i], 16)
                for i in range(ST):
                    g.wait_ge(moved[i], 32 * HALF)


def experts(nc, a, k, t, sem, sb, ph):
    PW = 2 * D
    with ExitStack() as c:
        s = lambda n: sem(ph + n)
        two = lambda n, dt=F32: [sb(c, f"{ph}{n}{i}", [P, PW], dt) for i in range(2)]
        xs, r, h, out = two("xs"), two("relu"), two("h"), two("out")
        xh, xl, hh, hl = two("xh", F32R), two("xl", F32R), two("hh", F32R), two("hl", F32R)
        banks = lambda n: [c.enter_context(nc.psum_tensor(f"{ph}{n}{i}", [P, PW], F32)) for i in range(2)]
        psX, psU, psH, psO = banks("psX"), banks("psU"), banks("psH"), banks("psO")
        xs_in, stored = [s(f"xs_in{i}") for i in range(2)], [s(f"stored{i}") for i in range(2)]
        xT_ready, up_ready, hT_ready, down_ready = s("xT_ready"), s("up_ready"), s("hT_ready"), s("down_ready")
        xh_ready, relu_ready, hh_ready = s("xh_ready"), s("relu_ready"), s("hh_ready")
        xl_ready, h_ready, hl_ready, out_ready = s("xl_ready"), s("h_ready"), s("hl_ready"), s("out_ready")
        BODY, FIRST = 4, 4
        PASSES = (PAIRS - 2 - FIRST) // BODY

        def steps(eng, step, before=None):
            for n in range(-2, FIRST):
                step(n, n % 2)
            if before:
                before()
            with eng.Fori(0, PASSES) as it:
                for q in range(BODY):
                    step(it * BODY + (FIRST + q), q % 2)
            if before:
                before()
            for n in range(FIRST + PASSES * BODY, PAIRS + 1):
                step(n, n % 2)

        def ahead(n, by):
            return not isinstance(n, int) or 0 <= n + by < PAIRS

        def filled(n, par):
            return 16 * (n // 2 + 1) if isinstance(n, int) else (n + (2 - par)) * 8

        def quarter(block, tile):
            return slice(block * D + tile * P, block * D + (tile + 1) * P)

        with nc.Block() as block:
            @block.tensor
            def _(pe):
                held = []

                def expert_of(pair):
                    return pe.value_load(t["expert"][0:1, bass.ds(pair, 1)], min_val=0, max_val=E - 1)

                def through(dst, xp, rows, w, cols):
                    m = 0
                    for cb in range(2):
                        for part, lefts in (("hi", xp), ("lo", xp[0:1])):
                            right = w[part][:, cols(cb)]
                            for i in range(2):
                                for left in lefts:
                                    ins = pe.matmul(dst[:, i * D:(i + 1) * D], left[:, rows(cb, i)], right,
                                                    start=(m == 0), stop=(m == 11))
                                    m += 1
                    return ins

                w1, w2 = ({part: tensors[name + part] for part in ("hi", "lo")} for tensors, name in ((k, "w1"), (t, "w2")))

                def step(n, par):
                    odd = 1 - par
                    if ahead(n, 2):
                        pe.wait_ge(xs_in[par], filled(n + 2, par))
                        need(pe, xl_ready, n + 1)
                        for cb in range(CB):
                            for i in range(2):
                                ins = pe.transpose(psX[par][:, quarter(cb, i)], xs[par][:, i * D + cb * P:i * D + (cb + 1) * P],
                                                   k["ident"][:, :])
                        ins.then_inc(xT_ready, 1)
                    if ahead(n, 1):
                        which = expert_of(n + 1)
                        held.append((n + 1, which))
                        pe.wait_ge(xh_ready, n + 2)
                        pe.wait_ge(xl_ready, n + 2)
                        need(pe, h_ready, n)
                        through(psU[odd], (xh[odd], xl[odd]), quarter, w1,
                                lambda cb: bass.ds(which * FE + cb * FALL, FE)).then_inc(up_ready, 1)
                    if ahead(n, 0):
                        pe.wait_ge(h_ready, n + 1)
                        need(pe, hl_ready, n - 1)
                        for fb in range(2):
                            for i in range(2):
                                ins = pe.transpose(psH[par][:, quarter(fb, i)], h[par][:, i * D + fb * P:i * D + (fb + 1) * P],
                                                   k["ident"][:, :])
                        ins.then_inc(hT_ready, 1)
                    if ahead(n, -1):
                        mine = held[-3][1] if len(held) > 2 else expert_of(n - 1)
                        pe.wait_ge(hh_ready, n)
                        pe.wait_ge(hl_ready, n)
                        need(pe, out_ready, n - 2)
                        through(psO[odd], (hh[odd], hl[odd]), quarter, w2,
                                lambda fb: bass.ds(mine * (2 * D) + fb * D, D)).then_inc(down_ready, 1)

                steps(pe, step, held.clear)

            @block.scalar
            def _(act):
                def step(n, par):
                    odd = 1 - par
                    if ahead(n, 2):
                        act.wait_ge(xT_ready, n + 3)
                        need(act, up_ready, n + 1)
                        act.activation(xh[par][:, :], psX[par][:, :], ACT.Copy).then_inc(xh_ready, 1)
                    if ahead(n, 1):
                        act.wait_ge(up_ready, n + 2)
                        need(act, h_ready, n)
                        act.activation(r[odd][:, :], psU[odd][:, :], ACT.Relu).then_inc(relu_ready, 1)
                    if ahead(n, 0):
                        act.wait_ge(hT_ready, n + 1)
                        need(act, down_ready, n - 1)
                        act.activation(hh[par][:, :], psH[par][:, :], ACT.Copy).then_inc(hh_ready, 1)
                    if ahead(n, -1):
                        act.wait_ge(down_ready, n)
                        if not isinstance(n, int) or n > 2:
                            act.wait_ge(stored[odd], filled(n - 3, odd) if isinstance(n, int) else (n - (2 - par)) * 8)
                        act.activation(out[odd][:, :], psO[odd][:, :], ACT.Copy).then_inc(out_ready, 1)

                steps(act, step)

            @block.vector
            def _(v):
                def step(n, par):
                    odd = 1 - par
                    if ahead(n, 2):
                        v.wait_ge(xh_ready, n + 3)
                        need(v, up_ready, n + 1)
                        v.tensor_tensor(xl[par][:, :], psX[par][:, :], xh[par][:, :].bitcast(F32), ALU.subtract).then_inc(xl_ready, 1)
                    if ahead(n, 1):
                        v.wait_ge(relu_ready, n + 2)
                        need(v, hT_ready, n)
                        v.scalar_tensor_tensor(h[odd][:, :], psU[odd][:, :], 0.0, r[odd][:, :],
                                               ALU.max, ALU.mult).then_inc(h_ready, 1)
                    if ahead(n, 0):
                        v.wait_ge(hh_ready, n + 1)
                        need(v, down_ready, n - 1)
                        v.tensor_tensor(hl[par][:, :], psH[par][:, :], hh[par][:, :].bitcast(F32), ALU.subtract).then_inc(hl_ready, 1)

                steps(v, step)

            @block.sync
            def _(sp):
                xv = a["slots_x"].rearrange("(n i p) d -> n p i d", p=P, i=2)
                yv = a["slots_y"].rearrange("(n i p) d -> n p i d", p=P, i=2)

                def load(n, par):
                    sp.dma_start(xs[par][:, :].rearrange("p (i d) -> p i d", i=2),
                                 xv[bass.ds(n, 1)].rearrange("o p i d -> (o p) i d")).then_inc(xs_in[par], 16)

                load(0, 0)
                load(1, 1)

                def step(n, par):
                    if ahead(n, 4):
                        sp.wait_ge(xT_ready, n + 3)
                        load(n + 4, par)
                    if ahead(n, -1):
                        odd = 1 - par
                        sp.wait_ge(out_ready, n)
                        sp.dma_start(yv[bass.ds(n - 1, 1)].rearrange("o p i d -> (o p) i d"),
                                     out[odd][:, :].rearrange("p (i d) -> p i d", i=2)).then_inc(stored[odd], 16)

                for n in range(-2, FIRST):
                    step(n, n % 2)
                with sp.Fori(0, (PAIRS - 4 - FIRST) // 2) as it:
                    for q in range(2):
                        step(it * 2 + (FIRST + q), q)
                for n in range(FIRST + (PAIRS - 4 - FIRST) // 2 * 2, PAIRS + 1):
                    step(n, n % 2)
                for par in range(2):
                    sp.wait_ge(stored[par], 16 * ((PAIRS + 1 - par) // 2))


def finish(nc, a, k, sem, sb, ph, store):
    with ExitStack() as c:
        s = lambda n: sem(ph + n)
        tmp = sb(c, ph + "root_tmp", [P, 2 * TILES])
        chain, stored = s("dve_chain"), s("stored")
        with nc.Block() as block:
            if store:
                @block.sync
                def _(sp):
                    ov = a["out"].rearrange("(n p) d -> p n d", p=P)
                    for g in range(GROUPS):
                        sp.dma_start(ov[:, g * GT:(g + 1) * GT, :],
                                     k["x"][:, g * GT * D:(g + 1) * GT * D].rearrange("p (n d) -> p n d", d=D)).then_inc(stored, 16)
                    sp.wait_ge(stored, 16 * GROUPS)
            else:
                @block.vector
                def _(v):
                    ch = Chain(v, chain)
                    rsqrt_rows(ch, v, k, tmp)


def attention(nc, a, k, sem, sb):
    X = k["x"]
    TWO_PI = 2.0 * math.pi
    XC = P + TAPS
    with ExitStack() as c:
        s = lambda n: sem("at_" + n)
        xn = sb(c, "at_xn", [P, D])
        xh, xl = ([sb(c, f"at_{n}{i}", [P, CB * XC], F32R) for i in range(2)] for n in ("xh", "xl"))
        turns = sb(c, "at_turns", [P, CH])
        feat = [sb(c, f"at_feat{i}", [P, 2 * CH]) for i in range(2)]
        qs = [sb(c, f"at_qs{i}", [P, 2 * QW]) for i in range(2)]
        prod = sb(c, "at_prod", [P, 2 * CHUNK])
        srow = sb(c, "at_srow", [P, ROW])
        crow = [sb(c, f"at_crow{i}", [HALF[i], RW]) for i in range(2)]
        split = [sb(c, f"at_split{i}", [HALF[i], 2 * RW], F32R) for i in range(2)]
        ones, ones_set = sb(c, "at_ones", [HALF[1], RW]), s("ones_set")
        carry = sb(c, "at_carry", [2, ROW], F32R)
        pw = [sb(c, f"at_p{i}", [P, K]) for i in range(2)]
        ex = sb(c, "at_exp", [P, 8 * K])
        pow2 = sb(c, "at_pow2", [P, K], I32)
        y2 = sb(c, "at_y2", [P, 2 * KH])
        y = sb(c, "at_y", [P, KH])
        ys = y
        yh, yl = (sb(c, "at_" + n, [P, KH], F32R) for n in ("yh", "yl"))
        rden = sb(c, "at_rden", [P, 2 * K])
        tmp = sb(c, "at_rt", [P, 2 * TILES])
        ps = lambda n: c.enter_context(nc.psum_tensor("at_ps" + n, [P, 512], F32))
        psT, psK, psQ, psY = ps("T"), ps("K"), ps("Q"), ps("Y")
        psS = [ps(f"S{i}") for i in range(4)]
        den = psY[:, 0:K]

        xT_ready, mem_ready, q_ready, yT_ready = s("xT_ready"), s("mem_ready"), s("q_ready"), s("yT_ready")
        den_ready, sums_ready, out_ready = s("den_ready"), s("sums_ready"), s("out_ready")
        xh_ready, yh_ready, whole_ready, tanh_ready = s("xh_ready"), s("yh_ready"), s("whole_ready"), s("tanh_ready")
        feat_ready, row_ready, q_copied, silu_ready = s("feat_ready"), s("row_ready"), s("q_copied"), s("silu_ready")
        xn_ready, xl_ready, turns_ready, mem_read = s("xn_ready"), s("xl_ready"), s("turns_ready"), s("mem_read")
        rem_ready, p_ready, frac_ready, prod_done = s("rem_ready"), s("p_ready"), s("frac_ready"), s("prod_done")
        den_read, y_ready, yl_ready, x_added = s("den_read"), s("y_ready"), s("yl_ready"), s("x_added")
        v_ready = s("v_ready")
        split_ready, row_moved, carry_in = ([s(f"{n}{i}") for i in range(2)] for n in ("split_ready", "row_moved", "carry_in"))
        v_chain, a_chain = s("dve_chain"), s("act_chain")

        def steps(eng, step, chain=None, per=0):
            pairs = (TILES - 6) // 2
            for n in range(-4, 2):
                step(n, n % 2)
            with eng.Fori(0, pairs) as it:
                if chain:
                    chain.enter(it, per)
                for par in range(2):
                    step(it * 2 + (2 + par), par)
                if chain:
                    chain.leave(pairs)
            for n in range(TILES - 4, TILES + 1):
                step(n, n % 2)

        def has(n):
            return not isinstance(n, int) or 0 <= n < TILES

        def first(n):
            return isinstance(n, int) and n == 0

        def ahead(n, by):
            return not isinstance(n, int) or 0 <= n + by < TILES

        with nc.Block() as block:
            @block.tensor
            def _(pe):
                def step(n, par):
                    odd = 1 - par

                    def transposes():
                        if ahead(n, 3):
                            pe.wait_ge(xn_ready, n + 4)
                            need(pe, xl_ready, n + 3)
                            for cb in range(CB):
                                ins = pe.transpose(psT[:, cb * P:(cb + 1) * P], xn[:, cb * P:(cb + 1) * P], k["ident"][:, :])
                            ins.then_inc(xT_ready, 1)
                        if ahead(n, -1):
                            pe.wait_ge(silu_ready, n)
                            need(pe, x_added, n - 1)
                            pe.wait_ge(den_read, n)
                            if has(n):
                                pe.wait_ge(row_ready, 9 * n)
                            for cb in range(CB):
                                ins = pe.transpose(psY[:, cb * P:(cb + 1) * P], ys[:, cb * P:(cb + 1) * P], k["ident"][:, :])
                            ins.then_inc(yT_ready, 1)

                    def project_out():
                        if not ahead(n, -1):
                            return
                        pe.wait_ge(yh_ready, n)
                        pe.wait_ge(yl_ready, n)
                        i = 0
                        for cb in range(CB):
                            for yp, wp in ((yh, "hi"), (yl, "hi"), (yh, "lo")):
                                ins = pe.matmul(psY[:, D:2 * D], yp[:, cb * P:(cb + 1) * P],
                                                k["wo" + wp][:, cb * D:(cb + 1) * D], start=(i == 0), stop=(i == 5))
                                i += 1
                        ins.then_inc(out_ready, 1)

                    def project_queries():
                        if not ahead(n, 2):
                            return
                        need(pe, q_copied, n + 2)
                        parts = ((xh[par], "hi"), (xl[par], "hi"), (xh[par], "lo"))
                        i = 0
                        for cb in range(CB):
                            for xp, wp in parts:
                                ins = pe.matmul(psQ[:, :], xp[:, cb * XC + TAPS - 1:cb * XC + TAPS - 1 + P],
                                                k["wq" + wp][:, cb * 2 * QW:(cb + 1) * 2 * QW],
                                                start=(i == 0), stop=(i == 5))
                                i += 1
                        ins.then_inc(q_ready, 1)

                    def project_memory():
                        if not ahead(n, 3):
                            return
                        pe.wait_ge(xh_ready, n + 4)
                        pe.wait_ge(xl_ready, n + 4)
                        need(pe, mem_read, n + 3)
                        parts = ((xh[odd], "hi"), (xl[odd], "hi"), (xh[odd], "lo"))
                        total, i = CB * TAPS * 3, 0
                        for cb in range(CB):
                            for j in range(TAPS):
                                for xp, wp in parts:
                                    ins = pe.matmul(psK[:, 0:MEM], xp[:, cb * XC + j:cb * XC + j + P],
                                                    k["wc" + wp][:, (cb * TAPS + j) * MEM:(cb * TAPS + j + 1) * MEM],
                                                    start=(i == 0), stop=(i == total - 1))
                                    i += 1
                        ins.then_inc(mem_ready, 1)

                    if has(n):
                        for e in range(CHUNKS):
                            if e % KQ == 0:
                                if not first(n):
                                    pe.wait_ge(carry_in[e // KQ], 32 * n)
                                pe.wait_ge(v_ready, 2 * n + e // KQ + 1)
                            need(pe, prod_done, 8 * n + (e - 3))
                            if ahead(n, 1) or e < 4:
                                need(pe, row_ready, 9 * n + (e - 3) - (0 if e > 3 or first(n) else 1))
                            cols = slice(*chunk_cols(e))
                            last = pe.matmul(psS[e % 4][:, :], k["tri"][:, :], feat[par][:, cols], start=True, stop=first(n))
                            if not first(n):
                                last = pe.matmul(psS[e % 4][:, :], k["ones2"][:, :], carry[:, slice(*row_cols(e))], start=False, stop=True)
                            last.then_inc(sums_ready, 1)
                            if e == 1:
                                transposes()
                            if e == 5:
                                project_queries()
                            if e == OUT_AFTER:
                                project_out()
                                pe.wait_ge(p_ready, n + 1)
                                last = pe.matmul(den, k["tri"][:, :], pw[par][:, :], start=True, stop=first(n))
                                if not first(n):
                                    last = pe.matmul(den, k["ones2"][:, :], carry[:, 2 * CH:ROW], start=False, stop=True)
                                last.then_inc(den_ready, 1)
                    else:
                        transposes()
                        project_queries()
                        project_out()
                    project_memory()

                steps(pe, step)

            @block.scalar
            def _(act):
                ch = Chain(act, a_chain)

                def step(n, par):
                    odd = 1 - par

                    def rows(lo, hi):
                        if not (has(n) and ahead(n, 1)):
                            return
                        for e in range(lo, hi):
                            act.wait_ge(prod_done, 8 * n + (e + 1))
                            if e % KQ == 0:
                                need(act, row_moved[e // KQ], 16 * n)
                            act.activation(srow[96:P, slice(*row_cols(e))], psS[e % 4][96:P, :], ACT.Copy).then_inc(row_ready, 1)

                    f = feat[odd]
                    if ahead(n, 1):
                        act.wait_ge(frac_ready, n + 2)
                        whole_abs = ch.mark(act.activation(f[:, 0:CH], f[:, CH:2 * CH], ACT.Abs))
                    rows(0, 2)
                    if ahead(n, 1):
                        ch.wait(whole_abs)
                        act.activation(f[:, CH:2 * CH], f[:, CH:2 * CH], ACT.Sin, scale=-TWO_PI).then_inc(feat_ready, 1)
                    if ahead(n, 3):
                        act.wait_ge(xT_ready, n + 4)
                        need(act, q_ready, n + 2)
                        x3 = [t[:, :].rearrange("p (c t) -> p c t", c=CB) for t in xh]
                        if isinstance(n, int) and n == -3:
                            ch.link(act.activation(x3[odd][:, :, 0:TAPS - 1], psT[:, 0:CB * (TAPS - 1)].rearrange(
                                "p (c t) -> p c t", c=CB), ACT.Copy, scale=0.0))
                        else:
                            act.wait_ge(xh_ready, n + 3)
                            ch.link(act.activation(x3[odd][:, :, 0:TAPS - 1],
                                                   x3[par][:, :, P:P + TAPS - 1].bitcast(F32), ACT.Copy))
                        act.activation(x3[odd][:, :, TAPS - 1:TAPS - 1 + P],
                                       psT[:, 0:D].rearrange("p (c t) -> p c t", c=CB), ACT.Copy).then_inc(xh_ready, 1)
                    if ahead(n, -1):
                        act.wait_ge(yT_ready, n)
                        need(act, out_ready, n - 1)
                        act.activation(yh[:, :], psY[:, 0:KH], ACT.Copy).then_inc(yh_ready, 1)
                    rows(2, 4)
                    if ahead(n, 1):
                        act.activation(f[:, 0:CH], f[:, 0:CH], ACT.Sin, scale=-TWO_PI,
                                       bias=k["halfpi"][:, 0:1]).then_inc(feat_ready, 1)
                    rows(4, 8)
                    if has(n) and ahead(n, 1):
                        act.wait_ge(den_read, n + 1)
                        need(act, x_added, n)
                        act.activation(srow[96:P, 2 * CH:ROW], den[96:P, :], ACT.Copy).then_inc(row_ready, 1)
                    if ahead(n, 2):
                        act.wait_ge(rem_ready, n + 3)
                        act.activation(ex[:, 4 * K:5 * K], ex[:, 3 * K:4 * K], ACT.Tanh, scale=0.5).then_inc(tanh_ready, 1)
                        act.wait_ge(q_ready, n + 3)
                        need(act, prod_done, 8 * n + 8)
                        act.activation(qs[par][:, :], psQ[:, :], ACT.Copy).then_inc(q_copied, 1)
                    if has(n):
                        act.wait_ge(y_ready, n + 1)
                        act.activation(ys[:, :], y[:, :], ACT.Silu).then_inc(silu_ready, 1)

                steps(act, step, ch, 2 * ACT_LINKS)

            @block.vector
            def _(v):
                ch = Chain(v, v_chain)
                lp, t0, k2, rem, th, t1, t2, _ = (ex[:, i * K:(i + 1) * K] for i in range(8))
                y2v = y2[:, :].rearrange("p (c f) -> p c f", c=2)

                def step(n, par):
                    odd = 1 - par

                    def product(e):
                        if not has(n):
                            return
                        part, q = 1 - e // KQ, e % KQ
                        v.wait_ge(sums_ready, 8 * n + (e + 1))
                        if e == 0:
                            v.wait_ge(q_copied, n + 1)
                        v.tensor_tensor(prod[:, (e % 2) * CHUNK:(e % 2 + 1) * CHUNK].rearrange("p (r f) -> p r f", r=REP),
                                        psS[e % 4][:, :].rearrange("p (r f) -> p r f", r=REP),
                                        qs[par][:, part * QW + q * HM:part * QW + (q + 1) * HM].unsqueeze(1).to_broadcast([P, REP, HM]),
                                        ALU.mult).then_inc(prod_done, 1)

                    def total(e):
                        part, q = 1 - e // KQ, e % KQ
                        v.wait_ge(prod_done, 8 * n + (e + 1))
                        return ch.mark(v.tensor_reduce(y2v[:, part, (q - 1) * HM:(q + 1) * HM],
                                                       prod[:, :].rearrange("p (c m) -> p c m", m=M), AX.X, ALU.add))

                    product(0)
                    product(1)
                    if has(n):
                        summed = total(1)
                    if ahead(n, 2):
                        v.wait_ge(mem_ready, n + 3)
                        need(v, frac_ready, n + 2)
                        v.tensor_tensor(turns[:, :].rearrange("p (c m) -> p c m", m=M),
                                        psK[:, 0:KH].unsqueeze(2).to_broadcast([P, KH, M]),
                                        k["theta"][:, :].rearrange("p (c m) -> p c m", m=M), ALU.mult).then_inc(turns_ready, 1)
                        v.tensor_tensor(t0, psK[:, KH:MEM], k["sscale"][:, :], ALU.mult).then_inc(mem_read, 1)
                    if has(n):
                        ch.wait(summed)
                    product(2)
                    if ahead(n, 2):
                        v.wait_ge(mem_read, n + 3)
                        m = ch.mark(v.tensor_scalar(t0, t0, 20.0, -20.0, ALU.min, ALU.max))
                    product(3)
                    if ahead(n, 2):
                        ch.wait(m)
                        v.scalar_tensor_tensor(lp[:, 0:NDECAY], k["slope"][:, 0:NDECAY], k["dist"][:, bass.ds(n + 2, 1)],
                                               t0[:, 0:NDECAY], ALU.mult, ALU.add)
                        m = ch.mark(v.scalar_tensor_tensor(lp[:, NDECAY:K], k["slope"][:, NDECAY:K],
                                                           k["pos"][:, bass.ds(n + 2, 1)], t0[:, NDECAY:K], ALU.mult, ALU.add))
                    if has(n):
                        summed = total(3)
                    if ahead(n, 2):
                        ch.wait(m)
                        m = ch.mark(v.tensor_scalar(k2, lp, LOG2E, MAGIC, ALU.mult, ALU.add))
                    if ahead(n, 3):
                        v.wait_ge(xh_ready, n + 4)
                        need(v, q_ready, n + 2)
                        x3 = [t[:, :].rearrange("p (c t) -> p c t", c=CB) for t in xl]
                        h3 = xh[odd][:, :].rearrange("p (c t) -> p c t", c=CB)
                        if isinstance(n, int) and n == -3:
                            before = ch.mark(v.memset(x3[odd][:, :, 0:TAPS - 1].bitcast(F32), 0.0))
                        else:
                            v.wait_ge(xl_ready, n + 3)
                            before = ch.mark(v.tensor_copy(x3[odd][:, :, 0:TAPS - 1],
                                                           x3[par][:, :, P:P + TAPS - 1].bitcast(F32)))
                        ch.wait(before)
                        v.tensor_tensor(x3[odd][:, :, TAPS - 1:TAPS - 1 + P],
                                        psT[:, 0:D].rearrange("p (c t) -> p c t", c=CB),
                                        h3[:, :, TAPS - 1:TAPS - 1 + P].bitcast(F32), ALU.subtract).then_inc(xl_ready, 1)
                    if ahead(n, 2):
                        ch.wait(m)
                        m = ch.mark(v.tensor_scalar(k2, k2, -MAGIC, None, ALU.add))
                    if ahead(n, -1):
                        v.wait_ge(yh_ready, n)
                        v.tensor_tensor(yl[:, :], psY[:, 0:KH], yh[:, :].bitcast(F32), ALU.subtract).then_inc(yl_ready, 1)
                    if has(n):
                        ch.wait(summed)
                    product(4)
                    if ahead(n, 2):
                        ch.wait(m)
                        m = ch.mark(v.scalar_tensor_tensor(rem, k2, -LN2_HI, lp, ALU.mult, ALU.add))
                    product(5)
                    if ahead(n, 2):
                        ch.wait(m)
                        v.scalar_tensor_tensor(rem, k2, -LN2_LO, rem, ALU.mult, ALU.add).then_inc(rem_ready, 1)
                    if has(n):
                        summed = total(5)
                    if ahead(n, 2):
                        v.wait_ge(rem_ready, n + 3)
                        m = ch.mark(v.tensor_scalar(k2, k2, -127.0, 127.0, ALU.max, ALU.add))
                    if ahead(n, 2):
                        v.wait_ge(turns_ready, n + 3)
                        need(v, sums_ready, 8 * (n + 1))
                        v.tensor_scalar(feat[par][:, 0:CH], turns[:, :], MAGIC, -MAGIC, ALU.add, ALU.add).then_inc(whole_ready, 1)
                    if has(n):
                        ch.wait(summed)
                    product(6)
                    if ahead(n, 2):
                        ch.wait(m)
                        raised = ch.mark(v.tensor_scalar(pow2[:, :], k2, 8388608.0, None, ALU.mult))
                    product(7)
                    if has(n):
                        v.wait_ge(den_ready, n + 1)
                        v.tensor_scalar(rden[:, 0:K], den, 1e-4, None, ALU.max).then_inc(den_read, 1)
                    if ahead(n, -1):
                        v.wait_ge(out_ready, n)
                        xs = X[:, bass.ds((n - 1) * D, D)]
                        v.tensor_tensor(xs, psY[:, D:2 * D], xs, ALU.add).then_inc(x_added, 1)
                    if has(n):
                        summed = total(7)
                        v.wait_ge(den_read, n + 1)
                        inverse = ch.mark(v.reciprocal(rden[:, K:2 * K], rden[:, 0:K]))
                        ch.wait(summed)
                        summed = ch.mark(v.tensor_tensor(y2[:, 0:KH], y2[:, 0:KH], y2[:, KH:2 * KH], ALU.add))
                    if ahead(n, 2):
                        v.wait_ge(tanh_ready, n + 3)
                        m = ch.mark(v.tensor_scalar(t1, th, -1.0, 1.0, ALU.mult, ALU.add))
                    if has(n):
                        ch.wait(inverse)
                        ch.wait(summed)
                        need(v, yT_ready, n)
                        v.tensor_tensor(y[:, :].rearrange("p (k h) -> p k h", h=H),
                                        y2[:, 0:KH].rearrange("p (k h) -> p k h", h=H),
                                        rden[:, K:2 * K].unsqueeze(2).to_broadcast([P, K, H]), ALU.mult).then_inc(y_ready, 1)
                    if ahead(n, 2):
                        ch.wait(m)
                        m = ch.mark(v.reciprocal(t2, t1))
                    if ahead(n, 4):
                        need(v, xT_ready, n + 4)
                        v.tensor_scalar(xn[:, :], X[:, bass.ds((n + 4) * D, D)], k["mean"][:, bass.ds(n + 4, 1)],
                                        k["rstd"][:, bass.ds(n + 4, 1)], ALU.subtract, ALU.mult).then_inc(xn_ready, 1)
                    if ahead(n, 2):
                        ch.wait(m)
                        m = ch.mark(v.scalar_tensor_tensor(t1, th, 1.0, t2, ALU.add, ALU.mult))
                    if ahead(n, -1):
                        v.wait_ge(x_added, n)
                        v.bn_stats(k["st"][:, bass.ds((n - 1) * 6, 6)], X[:, bass.ds((n - 1) * D, D)])
                    if ahead(n, 2):
                        ch.wait(m)
                        ch.wait(raised)
                        need(v, den_ready, n + 1)
                        need(v, v_ready, 2 * (n + 1))
                        v.tensor_tensor(pw[par][:, :], t1, pow2[:, :].bitcast(F32), ALU.mult).then_inc(p_ready, 1)

                steps(v, step, ch, 2 * DVE_LINKS)
                ch.link(v.memset(tmp[:, 0:1], 0.0))
                rsqrt_rows(ch, v, k, tmp)

            @block.gpsimd
            def _(g):
                g.memset(ones[:, :], 1.0).then_inc(ones_set, 1)
                g.wait_ge(ones_set, 1)

                def split_row(n, i):
                    if has(n) and ahead(n, 1):
                        rows = HALF[i]
                        g.wait_ge(row_moved[i], 16 * n + 16)
                        need(g, carry_in[i], 32 * n)
                        g.tensor_tensor(split[i][:, 0:RW], crow[i][:, :], ones[0:rows, :], ALU.mult).then_inc(split_ready[i], 1)
                        g.wait_ge(split_ready[i], 2 * n + 1)
                        g.tensor_tensor(split[i][:, RW:2 * RW], crow[i][:, :], split[i][:, 0:RW].bitcast(F32),
                                        ALU.subtract).then_inc(split_ready[i], 1)

                def step(n, par):
                    odd = 1 - par
                    if ahead(n, 1):
                        g.wait_ge(p_ready, n + 2)
                        for i, part in enumerate((1, 0)):
                            g.wait_ge(feat_ready, 2 * n + 3 + i)
                            f = feat[odd][:, part * CH:(part + 1) * CH].rearrange("p (k f) -> p k f", k=K)
                            g.tensor_tensor(f, f, pw[odd][:, :].unsqueeze(2).to_broadcast([P, K, HM]),
                                            ALU.mult).then_inc(v_ready, 1)
                    split_row(n, 0)
                    if ahead(n, 2):
                        g.wait_ge(whole_ready, n + 3)
                        g.tensor_tensor(feat[par][:, CH:2 * CH], feat[par][:, 0:CH], turns[:, :],
                                        ALU.subtract).then_inc(frac_ready, 1)
                    split_row(n, 1)

                steps(g, step)

            @block.sync
            def _(sp):
                def step(n, par):
                    if has(n) and ahead(n, 1):
                        for i, copied in enumerate((KQ, CHUNKS + 1)):
                            lo, hi = i * CH, i * CH + HALF[i] * RW
                            sp.wait_ge(row_ready, 9 * n + copied)
                            sp.dma_start(crow[i][:, :], srow[P - 1:P, lo:hi].rearrange("o (r w) -> o r w", r=HALF[i])).then_inc(row_moved[i], 16)
                            sp.wait_ge(split_ready[i], 2 * n + 2)
                            for part in range(2):
                                sp.dma_start(carry[part:part + 1, lo:hi].bitcast(F32).rearrange("o (r w) -> o r w", r=HALF[i]),
                                             split[i][:, part * RW:(part + 1) * RW].bitcast(F32)).then_inc(carry_in[i], 16)

                steps(sp, step)


def kernel(**inputs):
    import concourse.bacc as bacc
    from concourse.bass_utils import run_bass_kernel_spmd

    g = {n[3:]: np.asarray(v) for n, v in inputs.items()}
    nk = KH + K
    w_in = g["attn_W_in"]
    wq = w_in[:, nk:].reshape(D, KQ, H, M, 2)
    arrays = {
        "x": g["attn_x"].reshape(TOKENS, D),
        "w1t": np.concatenate([g["ffn_w1_stack"].reshape(E * FE, D), g["ffn_ws1"]]).T,
        "w2t": np.concatenate([g["ffn_w2_stack"].transpose(0, 2, 1).reshape(E * FE, D), g["ffn_ws2"].T]),
        "wrt": g["ffn_w_router"].T,
        "w_out": g["attn_W_out"],
        "w_mem": w_in[:, :nk],
        "w_qre": wq[..., 0].reshape(D, QW),
        "w_qim": wq[..., 1].reshape(D, QW),
        "conv_k": g["attn_conv_k"].reshape(TAPS * MEM),
        "theta": g["attn_theta"].reshape(CH),
        "norm_scale": g["attn_norm_scale"],
        "re_diag": np.diagonal(g["attn_W_re"]),
        "im_diag": np.diagonal(g["attn_W_im"]),
        "slopes": np.concatenate([g["attn_decay_slopes"], g["attn_anchor_slopes"]]),
        "score_scale": g["attn_score_scale"],
    }
    arrays = {n: np.ascontiguousarray(v) for n, v in arrays.items()}
    nc = bacc.Bacc("TRN2", target_bir_lowering=False, num_devices=1)
    aps = {n: nc.dram_tensor("in_" + n, v.shape, F32, kind="ExternalInput").ap() for n, v in arrays.items()}
    for n in ("slots_x", "slots_y"):
        aps[n] = nc.dram_tensor(n, (PAIRS * PT, D), F32, kind="Internal").ap()
    aps["out"] = nc.dram_tensor("out_x", (TOKENS, D), F32, kind="ExternalOutput").ap()
    build(nc, aps)
    r = run_bass_kernel_spmd(nc, [{"in_" + n: v for n, v in arrays.items()}], core_ids=[0])
    return r.results[0]["out_x"].reshape(1, TOKENS, D)
```

```python
import math
from contextlib import ExitStack

import numpy as np
import concourse.bass as bass
from concourse import mybir

F32 = mybir.dt.float32
F32R = mybir.dt.float32r
I32 = mybir.dt.int32
U32 = mybir.dt.uint32
ALU = mybir.AluOpType
ACT = mybir.ActivationFunctionType
AX = mybir.AxisListType

P = 128
TOKENS, D = 4096, 256
TILES = TOKENS // P
CB = D // P
E, FE, FS = 8, 256, 512
FALL = E * FE + FS
FB = FALL // P
UNITS = FALL // FE
GT = 4
GROUPS = TILES // GT
GN = GT * P
K, H, M, KQ, TAPS = 32, 8, 8, 4, 4
NDECAY = 28
KH = K * H
CH = K * H * M
HM = H * M
REP = K // KQ
QW = KQ * HM
MEM = KH + K
CHUNK = REP * HM
CHUNKS = 2 * KQ
ROW = 2 * CH + K
RW = 32
HALF = (CH // RW, (CH + K) // RW)
EPS = 1e-5
TOP = 2
PT = 2 * P
PAIRS = (TOP * TOKENS + E * (PT - 1)) // PT
MAGIC = 12582912.0
LOG2E = 1.0 / math.log(2.0)
LN2_HI = 0.693359375
LN2_LO = math.log(2.0) - LN2_HI


class Chain:

    def __init__(self, eng, sem):
        self.eng, self.sem, self.base, self.n = eng, sem, 0, 0

    def mark(self, ins):
        ins.then_inc(self.sem, 1)
        self.n += 1
        return self.base + self.n

    def wait(self, mark):
        self.eng.wait_ge(self.sem, mark)

    def link(self, ins):
        self.wait(self.mark(ins))

    def enter(self, it, per):
        self.start, self.per, self.before = self.n, per, self.base
        self.base = it * per

    def leave(self, passes):
        assert self.n - self.start == self.per, (self.n - self.start, self.per)
        self.base = 0
        self.n = self.start + self.per * passes


ACT_LINKS, DVE_LINKS = 1, 17
KV = KH // 4
OUT_AFTER = 7


def chunk_cols(e):
    lo = (1 - e // KQ) * CH + (e % KQ) * CHUNK
    return lo, lo + CHUNK


def row_cols(e):
    return e * CHUNK, (e + 1) * CHUNK


def need(eng, sem, value):
    if not (isinstance(value, int) and value <= 0):
        eng.wait_ge(sem, value)


def build(nc, a):
    with ExitStack() as top:
        def sem(name):
            return top.enter_context(nc.semaphore(name))

        def sb(stack, name, shape, dt=F32):
            return stack.enter_context(nc.sbuf_tensor(name, shape, dt))

        k = {}
        k["x"] = sb(top, "x_all", [P, TILES * D])
        for part in ("hi", "lo"):
            k["w1" + part] = sb(top, "w1" + part, [P, CB * FALL], F32R)
            k["wo" + part] = sb(top, "wo" + part, [P, CB * D], F32R)
            k["wc" + part] = sb(top, "wc" + part, [P, CB * TAPS * MEM], F32R)
            k["wq" + part] = sb(top, "wq" + part, [P, CB * 2 * QW], F32R)
        k["wr"] = sb(top, "w_router", [P, CB * E])
        k["theta"] = sb(top, "theta_turns", [P, CH])
        k["ident"] = sb(top, "ident", [P, P])
        k["halfpi"] = sb(top, "half_pi", [P, 1])
        k["tri"] = sb(top, "tri", [P, P])
        k["ones"] = sb(top, "ones", [P, P])
        k["ones2"] = sb(top, "ones2", [2, P], F32R)
        k["slope"] = sb(top, "neg_slope", [P, K])
        k["sscale"] = sb(top, "score_scale", [P, K])
        k["pos"] = sb(top, "pos_all", [P, TILES])
        k["dist"] = sb(top, "dist_all", [P, TILES])
        k["iota8"] = sb(top, "iota8", [P, E])
        k["st"] = sb(top, "bn_all", [P, TILES * 6])
        k["mean"] = sb(top, "mean_all", [P, TILES])
        k["rstd"] = sb(top, "rstd_all", [P, TILES])

        setup(nc, a, k, sem, sb)
        k["moved"] = {ph: [sem(f"{ph}_moved{i}") for i in range(2 * TILES // GROUPS)] for ph in ("f1s", "f1c", "f2s", "f2c")}
        with_semaphores(nc, lambda sem: ffn(nc, a, k, sem, sb, "f1", store=False))
        with_semaphores(nc, lambda sem: attention(nc, a, k, sem, sb))
        with_semaphores(nc, lambda sem: ffn(nc, a, k, sem, sb, "f2", store=True))


def with_semaphores(nc, part):
    taken = []

    def sem(name):
        taken.append(nc.alloc_semaphore(name=name))
        return taken[-1]

    part(sem)
    nc.clear_and_free_semaphores(taken)
    nc.all_engine_barrier()


def rsqrt_rows(ch, v, k, tmp):
    st = k["st"][:, :].rearrange("p (n s) -> p n s", s=6)
    var, t, y = tmp[:, 0:TILES], tmp[:, TILES:2 * TILES], k["rstd"][:, :]
    ch.link(v.tensor_tensor(t, st[:, :, 1], st[:, :, 4], ALU.subtract))
    ch.link(v.tensor_tensor(t, t, t, ALU.mult))
    ch.link(v.tensor_tensor(var, st[:, :, 2], st[:, :, 5], ALU.add))
    ch.link(v.tensor_scalar(var, var, 1.0 / D, EPS, ALU.mult, ALU.add))
    ch.link(v.scalar_tensor_tensor(var, t, 0.25, var, ALU.mult, ALU.add))
    ch.link(v.tensor_tensor(t, st[:, :, 1], st[:, :, 4], ALU.add))
    ch.link(v.tensor_scalar(k["mean"][:, :], t, 0.5, None, ALU.mult))
    ch.link(v.tensor_copy(t, var.bitcast(I32)))
    ch.link(v.tensor_scalar(y.bitcast(I32), t, -0.5, 1597463007.0, ALU.mult, ALU.add))
    for _ in range(4):
        ch.link(v.tensor_tensor(t, y, y, ALU.mult))
        ch.link(v.tensor_tensor(t, t, var, ALU.mult))
        ch.link(v.tensor_scalar(t, t, -0.5, 1.5, ALU.mult, ALU.add))
        ch.link(v.tensor_tensor(y, y, t, ALU.mult))


def setup(nc, a, k, sem, sb):
    SW = FALL
    with ExitStack() as c:
        jobs = (("w1a", SW, a["w1t"][0:P, :], ("w1", 0)), ("w1b", SW, a["w1t"][P:2 * P, :], ("w1", SW)),
                ("wo", CB * D, a["w_out"].rearrange("(c p) f -> p c f", p=P), ("wo", 0)))
        raw = {n: sb(c, "raw_" + n, [P, w]) for n, w, _, _ in jobs}
        raw_in = {n: sem("raw_in_" + n) for n in ("w1a", "w1b", "wo", "mem", "q", "conv", "small", "theta", "wr")}
        mem = sb(c, "raw_mem", [P, CB * MEM])
        qre, qim = (sb(c, "raw_q" + n, [P, CB * QW]) for n in ("re", "im"))
        folded = [sb(c, f"mem_tap{i}", [P, CB * MEM]) for i in range(2)]
        convb = sb(c, "conv_rows", [P, TAPS * MEM])
        qstage = sb(c, "q_stage", [P, CB * 2 * QW])
        qtmp = sb(c, "q_tmp", [P, CB * 2 * QW])
        small = sb(c, "small", [P, 4 * H + 8 * K])
        ipos = sb(c, "ipos", [P, TILES], I32)
        tmp = sb(c, "root_tmp", [P, 2 * TILES])
        x_in = [sem(f"x_in{g}") for g in range(GROUPS)]
        hi_done, lo_done, fold_done, tap_hi, tap_lo = (sem(n) for n in ("w_hi_done", "w_lo_done", "fold_done", "tap_hi", "tap_lo"))
        sp_in, sp_exp, consts, q_folded, q_hi = (sem(n) for n in ("softplus_in", "softplus_exp", "consts", "q_folded", "q_hi"))
        g_chain, v_chain = sem("setup_pool_chain"), sem("setup_dve_chain")

        xv = a["x"].rearrange("(n p) d -> p n d", p=P)
        by_tap = lambda ap: ap.rearrange("p (c j f) -> p c j f", c=CB, j=TAPS)
        by_block = lambda ap: ap.rearrange("p (c f) -> p c f", c=CB)
        part = lambda job, which: k[job[3][0] + which][:, job[3][1]:job[3][1] + job[1]]

        with nc.Block() as block:
            @block.sync
            def _(sp):
                for g in range(GROUPS):
                    sp.dma_start(k["x"][:, g * GT * D:(g + 1) * GT * D].rearrange("p (n d) -> p n d", d=D),
                                 xv[:, g * GT:(g + 1) * GT, :]).then_inc(x_in[g], 16)
                for n, w, src, _ in jobs:
                    dst = raw[n][:, :]
                    sp.dma_start(by_block(dst) if n == "wo" else dst, src).then_inc(raw_in[n], 16)

            @block.scalar
            def _(act):
                bc = lambda ap: ap.partition_broadcast(P)
                act.dma_start(by_block(mem[:, :]), a["w_mem"].rearrange("(c p) f -> p c f", p=P)).then_inc(raw_in["mem"], 16)
                act.dma_start(convb[:, :], bc(a["conv_k"])).then_inc(raw_in["conv"], 16)
                for at, n, nm in ((0, 2 * H, "norm_scale"), (2 * H, H, "re_diag"), (3 * H, H, "im_diag"), (4 * H, K, "slopes")):
                    act.dma_start(small[:, at:at + n], bc(a[nm])).then_inc(raw_in["small"], 16)
                for dst, nm in ((qre, "w_qre"), (qim, "w_qim")):
                    act.dma_start(by_block(dst[:, :]), a[nm].rearrange("(c p) f -> p c f", p=P)).then_inc(raw_in["q"], 16)
                act.dma_start(by_block(k["wr"][:, :]), a["wrt"].rearrange("(c p) f -> p c f", p=P)).then_inc(raw_in["wr"], 16)
                act.dma_start(k["sscale"][:, :], bc(a["score_scale"])).then_inc(raw_in["theta"], 16)
                act.dma_start(k["theta"][:, :], bc(a["theta"])).then_inc(raw_in["theta"], 16)
                act.wait_ge(sp_in, 1)
                act.activation(small[:, 4 * H + K:4 * H + 2 * K], small[:, 4 * H + K:4 * H + 2 * K],
                               ACT.Exp).then_inc(sp_exp, 1)
                for j in range(TAPS):
                    act.wait_ge(fold_done, j + 1)
                    act.activation(by_tap(k["wchi"][:, :])[:, :, j, :], by_block(folded[j % 2][:, :]), ACT.Copy).then_inc(tap_hi, 1)
                act.wait_ge(q_folded, 1)
                act.activation(k["wqhi"][:, :], qstage[:, :], ACT.Copy).then_inc(q_hi, 1)
                for job in jobs:
                    act.wait_ge(raw_in[job[0]], 16)
                    act.activation(part(job, "hi"), raw[job[0]][:, :], ACT.Copy).then_inc(hi_done, 1)
                act.wait_ge(raw_in["wr"], 16)

            @block.gpsimd
            def _(g):
                ch = Chain(g, g_chain)
                for nm in ("ident", "tri"):
                    ch.link(g.memset(k[nm][:, :], 0.0 if nm == "ident" else 1.0))
                ch.link(g.affine_select(out=k["ident"][:, :], in_=k["ident"][:, :], compare_op=ALU.not_equal,
                                        fill=1.0, base=0, pattern=[[-1, P]], channel_multiplier=1))
                ch.link(g.affine_select(out=k["tri"][:, :], in_=k["tri"][:, :], compare_op=ALU.is_ge,
                                        fill=0.0, base=0, pattern=[[1, P]], channel_multiplier=-1))
                ch.link(g.memset(k["ones"][:, :], 1.0))
                g.memset(k["ones2"][:, :].bitcast(F32), 1.0).then_inc(consts, 1)
                g.iota(ipos[:, :], pattern=[[P, TILES]], base=0, channel_multiplier=1).then_inc(consts, 1)
                g.wait_ge(raw_in["small"], 16 * 4)
                g.wait_ge(raw_in["q"], 16 * 2)
                g.tensor_tensor(small[:, 2 * H:3 * H], small[:, 0:H], small[:, 2 * H:3 * H], ALU.mult)
                ch.link(g.tensor_tensor(small[:, 3 * H:4 * H], small[:, H:2 * H], small[:, 3 * H:4 * H], ALU.mult))

                def scale(i):
                    return small[:, i * H:(i + 1) * H].unsqueeze(1).unsqueeze(3).to_broadcast([P, KQ, H, M])

                def v4(ap):
                    return ap.rearrange("p (q h m) -> p q h m", q=KQ, h=H)

                halves = [(dst, [dst[:, i * QW:(i + 1) * QW] for i in range(2 * CB)]) for dst in (qstage, qtmp)]
                for cb in range(CB):
                    re, im = (v4(t[:, cb * QW:(cb + 1) * QW]) for t in (qre, qim))
                    for i, (x1, x2) in enumerate(((re, im), (im, re))):
                        g.tensor_tensor(v4(halves[0][1][2 * cb + i]), x1, scale(2), ALU.mult)
                        last = g.tensor_tensor(v4(halves[1][1][2 * cb + i]), x2, scale(3), ALU.mult)
                ch.link(last)
                for cb in range(CB):
                    for i, op in enumerate((ALU.subtract, ALU.add)):
                        q = halves[0][1][2 * cb + i]
                        last = g.tensor_tensor(q, q, halves[1][1][2 * cb + i], op)
                last.then_inc(q_folded, 1)
                g.wait_ge(q_hi, 1)
                g.tensor_tensor(k["wqlo"][:, :], qstage[:, :], k["wqhi"][:, :].bitcast(F32), ALU.subtract).then_inc(lo_done, 1)

            @block.vector
            def _(v):
                ch = Chain(v, v_chain)
                for g in range(GROUPS):
                    v.wait_ge(x_in[g], 16)
                    for i in range(g * GT, (g + 1) * GT):
                        ins = v.bn_stats(k["st"][:, 6 * i:6 * i + 6], k["x"][:, i * D:(i + 1) * D])
                ch.link(ins)
                rsqrt_rows(ch, v, k, tmp)
                ch.link(v.memset(k["halfpi"][:, :], math.pi / 2.0))
                for e in range(E):
                    last = v.memset(k["iota8"][:, e:e + 1], float(e))
                ch.link(last)
                v.wait_ge(consts, 2)
                ch.link(v.tensor_copy(k["pos"][:, :], ipos[:, :]))
                ch.link(v.tensor_scalar(k["dist"][:, :], k["pos"][:, :], -1.0, float(TOKENS - 1), ALU.mult, ALU.add))
                v.wait_ge(raw_in["small"], 16 * 4)
                o = 4 * H
                s, e_, z, z2, q, r = (small[:, o + i * K:o + (i + 1) * K] for i in range(6))
                ch.link(v.tensor_scalar(z, s, -1.0, None, ALU.mult))
                ch.link(v.tensor_tensor(e_, s, z, ALU.min))
                v.tensor_copy(q, e_).then_inc(sp_in, 1)
                v.wait_ge(sp_exp, 1)
                ch.link(v.tensor_scalar(z2, e_, 2.0, None, ALU.add))
                ch.link(v.reciprocal(r, z2))
                ch.link(v.tensor_tensor(z, e_, r, ALU.mult))
                ch.link(v.tensor_tensor(z2, z, z, ALU.mult))
                step = ch.mark(v.memset(q, 1.0 / 19.0))
                series = iter(range(17, 0, -2))

                def term():
                    n = next(series, None)
                    if n is not None:
                        ch.link(v.tensor_tensor(q, q, z2, ALU.mult))
                        return ch.mark(v.tensor_scalar(q, q, 1.0 / n, None, ALU.add))

                v.wait_ge(raw_in["mem"], 16)
                v.wait_ge(raw_in["conv"], 16)
                for j in range(TAPS + 1):
                    ch.wait(step)
                    if j < TAPS:
                        tap = convb[:, j * MEM:(j + 1) * MEM].unsqueeze(1).to_broadcast([P, CB, MEM])
                        if j >= 2:
                            v.wait_ge(tap_lo, j - 1)
                        v.tensor_tensor(by_block(folded[j % 2][:, :]), by_block(mem[:, :]), tap, ALU.mult).then_inc(fold_done, 1)
                    step = term()
                    if j:
                        v.wait_ge(tap_hi, j)
                        v.tensor_tensor(by_tap(k["wclo"][:, :])[:, :, j - 1, :], by_block(folded[(j - 1) % 2][:, :]),
                                        by_tap(k["wchi"][:, :].bitcast(F32))[:, :, j - 1, :], ALU.subtract).then_inc(tap_lo, 1)
                while step is not None:
                    ch.wait(step)
                    step = term()
                ch.link(v.tensor_tensor(q, q, z, ALU.mult))
                ch.link(v.tensor_scalar(s, s, 0.0, None, ALU.max))
                ch.link(v.scalar_tensor_tensor(q, q, 2.0, s, ALU.mult, ALU.add))
                ch.link(v.tensor_scalar(k["slope"][:, :], q, -1.0, None, ALU.mult))
                for i, job in enumerate(jobs):
                    v.wait_ge(hi_done, i + 1)
                    v.tensor_tensor(part(job, "lo"), raw[job[0]][:, :], part(job, "hi").bitcast(F32), ALU.subtract).then_inc(lo_done, 1)
                v.wait_ge(raw_in["theta"], 16 * 2)
                ch.link(v.tensor_scalar(k["theta"][:, :], k["theta"][:, :], 1.0 / (2.0 * math.pi), None, ALU.mult))


def ffn(nc, a, k, sem, sb, ph, store):
    with ExitStack() as c:
        t = {"w2" + part: sb(c, ph + "w2" + part, [P, FB * D], F32R) for part in ("hi", "lo")}
        t["slot"] = sb(c, ph + "slot", [P, TILES * TOP], U32)
        t["gate"] = sb(c, ph + "gate", [P, TILES * TOP])
        t["expert"] = sb(c, ph + "expert", [1, PAIRS], I32)
        route(nc, a, k, t, sem, sb, ph + "r_", clear=not store)
        shared(nc, a, k, t, sem, sb, ph + "s_", 0, scatter=True)
        experts(nc, a, k, t, sem, sb, ph + "e_")
        shared(nc, a, k, t, sem, sb, ph + "c_", GROUPS // 2, scatter=False, store=store)
        if not store:
            statistics(nc, k, sem, sb, ph + "z_")


def normalise(v, k, n, dst):
    return v.tensor_scalar(dst, k["x"][:, bass.ds(n * D, D)], k["mean"][:, bass.ds(n, 1)],
                           k["rstd"][:, bass.ds(n, 1)], ALU.subtract, ALU.mult)


def route(nc, a, k, t, sem, sb, ph, clear):
    ZT = 6
    with ExitStack() as c:
        s = lambda n: sem(ph + n)
        raw = [sb(c, f"{ph}w2raw{i}", [P, FE // P * D]) for i in range(2)]
        xn = [sb(c, f"{ph}xn{i}", [P, GT * D]) for i in range(2)]
        xT = [sb(c, f"{ph}xT{i}", [P, CB * GN]) for i in range(2)]
        best, least = (sb(c, ph + n, [P, TOP * TILES]) for n in ("best", "least"))
        ge, den = (sb(c, ph + n, [P, TILES]) for n in ("ge", "den"))
        W = TILES * E
        oh = [sb(c, f"{ph}oh{j}", [P, W]) for j in range(TOP)]
        lg, eq, ids, ids8 = (sb(c, ph + n, [P, W]) for n in ("lg", "eq", "ids", "ids8"))
        both, run, pos, one = (sb(c, ph + n, [P, W]) for n in ("both", "run", "pos", "one"))
        e8 = sb(c, ph + "e8", [P, 4 * E])
        slotf = sb(c, ph + "slotf", [P, TILES])
        tile_no = sb(c, ph + "pair_no", [1, PAIRS], I32)
        tile_f = sb(c, ph + "pair_f", [1, PAIRS])
        past = sb(c, ph + "past", [1, PAIRS * E])
        psT = [c.enter_context(nc.psum_tensor(f"{ph}psT{i}", [P, GN], F32)) for i in range(2 * CB)]
        psL, psR, psC = (c.enter_context(nc.psum_tensor(ph + n, [P, GN], F32)) for n in ("psL", "psR", "psC"))
        psE = c.enter_context(nc.psum_tensor(ph + "psE", [E, GN], F32))
        lT = sb(c, ph + "lT", [E, GN])
        logits_copied, logits_turned = s("logits_copied"), s("logits_turned")
        w2_in, w2_ready = [s(f"w2_in{i}") for i in range(2)], s("w2_ready")
        xn_ready, xT_ready, xT_copied = s("xn_ready"), s("xT_ready"), [s(f"xT_copied{cb}") for cb in range(CB)]
        logits_ready, logits_read, gap_ready, exp_ready = s("logits_ready"), s("logits_read"), s("gap_ready"), s("exp_ready")
        chosen_ready, ranks_ready, iota_ready, chain = s("chosen_ready"), s("ranks_ready"), s("iota_ready"), s("dve_chain")
        if clear:
            zeros, zeros_ready, slots_cleared = sb(c, ph + "zeros", [P, ZT * D]), s("zeros_ready"), s("slots_cleared")
        FU = FE // P

        def steps(eng, step):
            for n in range(-2, 2):
                step(n, n % 2)
            with eng.Fori(0, (GROUPS - 4) // 2) as it:
                for par in range(2):
                    step(it * 2 + (2 + par), par)
            for n in range(GROUPS - 2, GROUPS + 1):
                step(n, n % 2)

        def ahead(n, by):
            return not isinstance(n, int) or 0 <= n + by < GROUPS

        with nc.Block() as block:
            @block.tensor
            def _(pe):
                def step(n, par):
                    odd = 1 - par
                    if ahead(n, 1):
                        pe.wait_ge(xn_ready, n + 2)
                        for cb in range(CB):
                            need(pe, xT_copied[cb], n)
                            for i in range(GT):
                                ins = pe.transpose(psT[odd * CB + cb][:, i * P:(i + 1) * P],
                                                   xn[odd][:, i * D + cb * P:i * D + (cb + 1) * P], k["ident"][:, :])
                            ins.then_inc(xT_ready, 1)
                    if ahead(n, 0):
                        for cb in range(CB):
                            pe.wait_ge(xT_copied[cb], n + 1)
                        need(pe, logits_copied, n)
                        for cb in range(CB):
                            ins = pe.matmul(psE[:, :], k["wr"][:, cb * E:(cb + 1) * E], xT[par][:, cb * GN:(cb + 1) * GN],
                                            start=(cb == 0), stop=(cb == CB - 1))
                        ins.then_inc(logits_ready, 1)
                    if ahead(n, -1):
                        pe.wait_ge(logits_copied, n)
                        need(pe, logits_read, n - 1)
                        for i in range(GT):
                            ins = pe.matmul(psL[:, i * E:(i + 1) * E], lT[:, i * P:(i + 1) * P], k["ident"][0:E, 0:E],
                                            start=True, stop=True)
                        ins.then_inc(logits_turned, 1)

                steps(pe, step)
                pe.wait_ge(chosen_ready, 1)
                pe.matmul(psR[:, 0:W], k["tri"][:, :], both[:, :], start=True, stop=True)
                pe.matmul(psC[:, 0:W], k["ones"][:, :], both[:, :], start=True, stop=True).then_inc(ranks_ready, 1)

            @block.scalar
            def _(act):
                def step(n, par):
                    odd = 1 - par
                    if ahead(n, 1):
                        act.wait_ge(xT_ready, CB * (n + 1) + 1)
                        need(act, logits_ready, n)
                        act.activation(xT[odd][:, 0:GN], psT[odd * CB][:, :], ACT.Copy).then_inc(xT_copied[0], 1)
                    if ahead(n, 0):
                        act.wait_ge(logits_ready, n + 1)
                        need(act, logits_turned, n)
                        act.activation(lT[:, :], psE[:, :], ACT.Copy).then_inc(logits_copied, 1)

                if clear:
                    zv = a["slots_x"].rearrange("(n p) d -> p n d", p=P)
                    act.wait_ge(zeros_ready, 1)
                    for i in range(2 * PAIRS // ZT):
                        act.dma_start(zv[:, ZT * i:ZT * (i + 1), :],
                                      zeros[:, :].rearrange("p (n d) -> p n d", d=D)).then_inc(slots_cleared, 16)
                steps(act, step)
                act.wait_ge(gap_ready, 1)
                act.activation(ge[:, :], den[:, :], ACT.Exp).then_inc(exp_ready, 1)
                if clear:
                    act.wait_ge(slots_cleared, 16 * (2 * PAIRS // ZT))

            @block.vector
            def _(v):
                ch = Chain(v, chain)
                best3 = best[:, :].rearrange("p (j n) -> p j n", j=TOP)
                least3 = least[:, :].rearrange("p (j n) -> p j n", j=TOP)

                def step(n, par):
                    odd = 1 - par
                    if ahead(n, 1):
                        v.wait_ge(xT_ready, CB * (n + 1) + 2)
                        need(v, logits_ready, n)
                        v.tensor_copy(xT[odd][:, GN:2 * GN], psT[odd * CB + 1][:, :]).then_inc(xT_copied[1], 1)
                    if ahead(n, 2):
                        need(v, xT_ready, CB * (n + 1))
                        for i in range(GT):
                            ins = normalise(v, k, (n + 2) * GT + i, xn[par][:, i * D:(i + 1) * D])
                        ins.then_inc(xn_ready, 1)
                    if ahead(n, -1):
                        v.wait_ge(logits_turned, n)
                        v.tensor_copy(lg[:, bass.ds((n - 1) * (GT * E), GT * E)], psL[:, 0:GT * E]).then_inc(logits_read, 1)

                steps(v, step)

                def by_expert(ap):
                    return ap.rearrange("p (n e) -> p n e", e=E)

                def each(ap):
                    return ap.unsqueeze(2).to_broadcast([P, TILES, E])

                ch.link(v.tensor_copy(by_expert(ids[:, :]), k["iota8"][:, :].unsqueeze(1).to_broadcast([P, TILES, E])))
                ch.link(v.tensor_scalar(ids8[:, :], ids[:, :], float(-E), None, ALU.add))
                v.wait_ge(logits_read, GROUPS)
                for j in range(TOP):
                    ch.link(v.tensor_reduce(best3[:, j, :], by_expert(lg[:, :]), AX.X, ALU.max))
                    ch.link(v.tensor_tensor(by_expert(eq[:, :]), by_expert(lg[:, :]), each(best3[:, j, :]), ALU.is_equal))
                    ch.link(v.scalar_tensor_tensor(eq[:, :], eq[:, :], float(-E), ids[:, :], ALU.mult, ALU.add))
                    ch.link(v.tensor_reduce(least3[:, j, :], by_expert(eq[:, :]), AX.X, ALU.min))
                    ch.link(v.tensor_tensor(by_expert(oh[j][:, :]), by_expert(ids8[:, :]), each(least3[:, j, :]), ALU.is_equal))
                    if j == 0:
                        ch.link(v.scalar_tensor_tensor(lg[:, :], oh[0][:, :], -3e38, lg[:, :], ALU.mult, ALU.add))
                v.tensor_tensor(both[:, :], oh[0][:, :], oh[1][:, :], ALU.add).then_inc(chosen_ready, 1)
                v.tensor_tensor(den[:, :], best3[:, 1, :], best3[:, 0, :], ALU.subtract).then_inc(gap_ready, 1)
                ch.link(v.memset(one[:, :], 1.0))
                v.wait_ge(exp_ready, 1)
                gate3 = t["gate"][:, :].rearrange("p (j n) -> p j n", j=TOP)
                ch.link(v.tensor_scalar(den[:, :], ge[:, :], 2.0, 2.0, ALU.mult, ALU.add))
                ch.link(v.reciprocal(gate3[:, 0, :], den[:, :]))
                ch.link(v.tensor_tensor(gate3[:, 1, :], gate3[:, 0, :], ge[:, :], ALU.mult))
                v.wait_ge(ranks_ready, 1)
                ch.link(v.tensor_copy(pos[:, :], psC[:, 0:W]))
                for e in range(E):
                    ins = v.tensor_tensor_scan(by_expert(run[:, :])[:, :, e], by_expert(one[:, :])[:, :, e],
                                               by_expert(pos[:, :])[:, :, e], 0.0, ALU.mult, ALU.add)
                ch.link(ins)
                tiles, end, start, _ = (e8[:, i * E:(i + 1) * E] for i in range(4))
                ch.link(v.tensor_scalar(tiles, run[:, W - E:W], 1.0 / PT, 0.5 - 0.5 / PT, ALU.mult, ALU.add))
                ch.link(v.tensor_scalar(tiles, tiles, MAGIC, -MAGIC, ALU.add, ALU.add))
                ch.link(v.tensor_tensor_scan(end, one[:, 0:E], tiles, 0.0, ALU.mult, ALU.add))
                ch.link(v.tensor_tensor(start, end, tiles, ALU.subtract))
                ch.link(v.tensor_scalar(start, start, float(PT), -1.0, ALU.mult, ALU.add))
                ch.link(v.tensor_tensor(run[:, :], run[:, :], pos[:, :], ALU.subtract))
                ch.link(v.tensor_tensor(pos[:, :], run[:, :], psR[:, 0:W], ALU.add))
                ch.link(v.tensor_tensor(by_expert(pos[:, :]), by_expert(pos[:, :]),
                                        start.unsqueeze(1).to_broadcast([P, TILES, E]), ALU.add))
                for j in range(TOP):
                    ch.link(v.tensor_tensor(oh[j][:, :], oh[j][:, :], pos[:, :], ALU.mult))
                    ch.link(v.tensor_reduce(slotf[:, :], by_expert(oh[j][:, :]), AX.X, ALU.add))
                    ch.link(v.tensor_copy(t["slot"][:, j * TILES:(j + 1) * TILES], slotf[:, :]))
                v.wait_ge(iota_ready, 1)
                ch.link(v.tensor_copy(tile_f[:, :], tile_no[:, :]))
                past3 = past[:, :].rearrange("p (n e) -> p n e", e=E)
                ch.link(v.tensor_tensor(past3, tile_f[:, :].unsqueeze(2).to_broadcast([1, PAIRS, E]),
                                        end[0:1, :].unsqueeze(1).to_broadcast([1, PAIRS, E]), ALU.is_ge))
                ch.link(v.tensor_reduce(tile_f[:, :], past3, AX.X, ALU.add))
                ch.link(v.tensor_scalar(tile_f[:, :], tile_f[:, :], float(E - 1), None, ALU.min))
                ch.link(v.tensor_copy(t["expert"][:, :], tile_f[:, :]))

            @block.gpsimd
            def _(g):
                g.iota(tile_no[:, :], pattern=[[1, PAIRS]], base=0, channel_multiplier=0).then_inc(iota_ready, 1)
                if clear:
                    g.memset(zeros[:, :], 0.0).then_inc(zeros_ready, 1)
                for u in range(UNITS):
                    cols = slice(u * FU * D, (u + 1) * FU * D)
                    g.wait_ge(w2_in[u % 2], 16 * (u // 2 + 1))
                    g.tensor_copy(t["w2hi"][:, cols], raw[u % 2][:, :]).then_inc(w2_ready, 1)
                    g.wait_ge(w2_ready, 2 * u + 1)
                    g.tensor_tensor(t["w2lo"][:, cols], raw[u % 2][:, :], t["w2hi"][:, cols].bitcast(F32),
                                    ALU.subtract).then_inc(w2_ready, 1)

            @block.sync
            def _(sp):
                w2v = a["w2t"].rearrange("(u b p) d -> u p b d", p=P, b=FU)
                for u in range(UNITS):
                    if u >= 2:
                        sp.wait_ge(w2_ready, 2 * (u - 1))
                    sp.dma_start(raw[u % 2][:, :].rearrange("p (b d) -> p b d", d=D),
                                 w2v[u]).then_inc(w2_in[u % 2], 16)


def shared(nc, a, k, t, sem, sb, ph, g0, scatter, store=False):
    HALF = GROUPS // 2
    ST = TILES // HALF
    FSB, F0 = FS // P, E * FE // P
    with ExitStack() as c:
        s = lambda n: sem(ph + n)
        xn = sb(c, ph + "xn", [P, GT * D])
        xh, xl = (sb(c, ph + n, [P, CB * GN], F32R) for n in ("xh", "xl"))
        r, h = ([sb(c, f"{ph}{n}{i}", [P, GN]) for i in range(2)] for n in ("relu", "h"))
        hh, hl = ([sb(c, f"{ph}{n}{i}", [P, GN], F32R) for i in range(FSB)] for n in ("hh", "hl"))
        rows = [sb(c, f"{ph}rows{i}", [P, D if scatter else TOP * D]) for i in range(ST)]
        slot_now = sb(c, ph + "slot_now", [P, ST * TOP], U32)
        idle = sb(c, ph + "idle", [1, 3])
        psT = [c.enter_context(nc.psum_tensor(f"{ph}psT{i}", [P, GN], F32)) for i in range(CB)]
        psU = [c.enter_context(nc.psum_tensor(f"{ph}psU{i}", [P, GN], F32)) for i in range(FSB)]
        psO = [c.enter_context(nc.psum_tensor(f"{ph}psO{i}", [P, GN], F32)) for i in range(2)]
        xn_ready, xT_ready, xh_ready, xl_ready = s("xn_ready"), s("xT_ready"), s("xh_ready"), s("xl_ready")
        up_ready, relu_ready, h_ready, hh_ready, hl_ready = s("up_ready"), s("relu_ready"), s("h_ready"), s("hh_ready"), s("hl_ready")
        out_ready, out_added, slots_staged = s("out_ready"), s("out_added"), s("slots_staged")
        rows_ready, stats_done, idle_set, stored = s("rows_ready"), s("stats_done"), s("idle_set"), s("stored")
        moved = k["moved"][ph[:-1]]

        def groups(eng, group):
            group(0)
            with eng.Fori(0, HALF - 2) as it:
                group(it + 1)
            group(HALF - 1)

        def last(g):
            return isinstance(g, int) and g == HALF - 1

        with nc.Block() as block:
            @block.tensor
            def _(pe):
                def transposes(g):
                    pe.wait_ge(xn_ready, g + 1)
                    for cb in range(CB):
                        for i in range(GT):
                            ins = pe.transpose(psT[cb][:, i * P:(i + 1) * P], xn[:, i * D + cb * P:i * D + (cb + 1) * P],
                                               k["ident"][:, :])
                        ins.then_inc(xT_ready, 1)

                def group(g):
                    pe.wait_ge(xh_ready, CB * (g + 1))
                    pe.wait_ge(xl_ready, CB * (g + 1))
                    need(pe, h_ready, FSB * g)
                    for f in range(FSB):
                        n = 0
                        for cb in range(CB):
                            w = slice(cb * FALL + (F0 + f) * P, cb * FALL + (F0 + f + 1) * P)
                            for xp, wp in ((xh, "hi"), (xl, "hi"), (xh, "lo")):
                                ins = pe.matmul(psU[f][:, :], k["w1" + wp][:, w], xp[:, cb * GN:(cb + 1) * GN],
                                                start=(n == 0), stop=(n == 5))
                                n += 1
                        ins.then_inc(up_ready, 1)
                    if not last(g):
                        transposes(g + 1)
                    need(pe, out_added, 2 * g)
                    for i in range(GT):
                        o = psO[i // 2][:, (i % 2) * D:(i % 2 + 1) * D]
                        for f in range(FSB):
                            if i == 0:
                                pe.wait_ge(hh_ready, g * FSB + (f + 1))
                                pe.wait_ge(hl_ready, g * FSB + (f + 1))
                            for n, (hp, wp) in enumerate(((hh, "hi"), (hl, "hi"), (hh, "lo"))):
                                ins = pe.matmul(o, hp[f][:, i * P:(i + 1) * P], t["w2" + wp][:, (F0 + f) * D:(F0 + f + 1) * D],
                                                start=(f == 0 and n == 0), stop=(f == FSB - 1 and n == 2))
                        if i % 2:
                            ins.then_inc(out_ready, 1)

                transposes(0)
                groups(pe, group)

            @block.scalar
            def _(act):
                def high(g):
                    for cb in range(CB):
                        act.wait_ge(xT_ready, g * CB + (cb + 1))
                        act.activation(xh[:, cb * GN:(cb + 1) * GN], psT[cb][:, :], ACT.Copy).then_inc(xh_ready, 1)

                def group(g):
                    need(act, out_ready, 2 * g)
                    for f in range(FSB + 1):
                        if f < FSB:
                            act.wait_ge(up_ready, g * FSB + (f + 1))
                            need(act, h_ready, g * FSB + (f - 1))
                            act.activation(r[f % 2][:, :], psU[f][:, :], ACT.Relu).then_inc(relu_ready, 1)
                        if f:
                            act.wait_ge(h_ready, g * FSB + f)
                            act.activation(hh[f - 1][:, :], h[(f - 1) % 2][:, :], ACT.Copy).then_inc(hh_ready, 1)
                    if not last(g):
                        high(g + 1)

                high(0)
                groups(act, group)

            @block.vector
            def _(v):
                X = k["x"]

                def norm(g):
                    for i in range(GT):
                        ins = normalise(v, k, (g0 + g) * GT + i, xn[:, i * D:(i + 1) * D])
                    ins.then_inc(xn_ready, 1)

                def low(g):
                    for cb in range(CB):
                        v.wait_ge(xh_ready, g * CB + (cb + 1))
                        v.tensor_tensor(xl[:, cb * GN:(cb + 1) * GN], psT[cb][:, :],
                                        xh[:, cb * GN:(cb + 1) * GN].bitcast(F32), ALU.subtract).then_inc(xl_ready, 1)

                def stage(g, half):
                    n = ST // 2
                    for j in range(TOP):
                        ins = v.tensor_copy(slot_now[:, j * ST + half * n:j * ST + (half + 1) * n],
                                            t["slot"][:, bass.ds(g * ST + (j * TILES + half * n), n)])
                    ins.then_inc(slots_staged, 1)

                def fill(g, i):
                    normalise(v, k, g * ST + i, rows[i][:, :]).then_inc(rows_ready, 1)

                def combine(g, i):
                    tiles = [(X[:, bass.ds((g * ST + i + q) * D, D)], g * ST + i + q) for q in range(2)]
                    done = g * (ST * TOP) + TOP * i
                    for j in range(TOP):
                        for q, (xs, n) in enumerate(tiles):
                            if j == 0:
                                v.wait_ge(moved[i + q], 32 * (g + 1))
                            else:
                                v.wait_ge(rows_ready, done + (q + 1))
                            v.scalar_tensor_tensor(xs, rows[i + q][:, j * D:(j + 1) * D], t["gate"][:, bass.ds(n + j * TILES, 1)],
                                                   xs, ALU.mult, ALU.add).then_inc(rows_ready, 1)
                    for q, (xs, n) in enumerate(tiles) if not store else ():
                        v.wait_ge(rows_ready, done + (q + 3))
                        v.bn_stats(k["st"][:, bass.ds(n * 6, 6)], xs).then_inc(stats_done, 1)

                def beside(g, i):
                    if scatter:
                        if last(g):
                            return
                        for q in range(2):
                            v.wait_ge(moved[i + q], 32 * (g + 1))
                            fill(g + 1, i + q)
                    else:
                        combine(g, i)
                    if (i + 2) % (ST // 2) == 0 and not last(g):
                        stage(g + 1, i // (ST // 2))

                def add(g):
                    for q in range(2):
                        v.wait_ge(out_ready, 2 * g + (q + 1))
                        xs = X[:, bass.ds((g0 + g) * GT * D + q * 2 * D, 2 * D)]
                        v.scalar_tensor_tensor(xs, psO[q][:, :], 0.5, xs, ALU.mult, ALU.add).then_inc(out_added, 1)

                def group(g):
                    need(v, out_added, 2 * g)
                    need(v, out_ready, 2 * g)
                    if not last(g):
                        v.wait_ge(xT_ready, CB * (g + 1))
                        norm(g + 1)
                    for f in range(FSB + 1):
                        if f < FSB:
                            v.wait_ge(relu_ready, g * FSB + (f + 1))
                            need(v, hh_ready, g * FSB + (f - 1))
                            need(v, hl_ready, g * FSB + (f - 1))
                            v.scalar_tensor_tensor(h[f % 2][:, :], psU[f][:, :], 0.0, r[f % 2][:, :],
                                                   ALU.max, ALU.mult).then_inc(h_ready, 1)
                        if f:
                            v.wait_ge(hh_ready, g * FSB + f)
                            v.tensor_tensor(hl[f - 1][:, :], h[(f - 1) % 2][:, :], hh[f - 1][:, :].bitcast(F32),
                                            ALU.subtract).then_inc(hl_ready, 1)
                    if not last(g):
                        low(g + 1)
                        for i in range(0, ST, 2):
                            beside(g, i)
                        add(g)
                    else:
                        for i in range(0, ST // 2, 2):
                            beside(g, i)
                        add(g)
                        v.wait_ge(out_added, 2 * HALF)
                        for i in range(ST // 2, ST, 2):
                            beside(g, i)

                norm(0)
                if scatter:
                    for i in range(ST):
                        fill(0, i)
                for half in range(2):
                    stage(0, half)
                low(0)
                group(0)
                with v.Fori(0, HALF - 2) as it:
                    group(it + 1)
                group(HALF - 1)

            @block.gpsimd
            def _(g):
                per = ST + 2 if scatter else 2

                def idle_for(sem_, value, it, nth):
                    g.wait_ge(idle_set, it * per + (nth + 1))
                    g.wait_ge(sem_, value)
                    g.tensor_tensor(idle[:, 2:3], idle[:, 0:1], idle[:, 1:2], ALU.add).then_inc(idle_set, 1)

                g.memset(idle[:, 0:2], 0.0).then_inc(idle_set, 1)
                g.wait_ge(idle_set, 1)
                with g.Fori(0, HALF) as it:
                    nth = 0
                    for i in range(ST):
                        if i % (ST // 2) == 0:
                            idle_for(slots_staged, 2 * it + (i // (ST // 2) + 1), it, nth)
                            nth += 1
                        if scatter:
                            idle_for(rows_ready, it * ST + (i + 1), it, nth)
                            nth += 1
                        for j in range(TOP):
                            where = bass.IndirectOffsetOnAxis(ap=slot_now[:, j * ST + i:j * ST + i + 1], axis=0)
                            if scatter:
                                ins = g.indirect_dma_start(out=a["slots_x"][:, :], out_offset=where, in_=rows[i][:, :], in_offset=None)
                            else:
                                ins = g.indirect_dma_start(out=rows[i][:, j * D:(j + 1) * D], out_offset=None,
                                                           in_=a["slots_y"][:, :], in_offset=where)
                            ins.then_inc(moved[i], 16)
                for i in range(ST):
                    g.wait_ge(moved[i], 32 * HALF)

            if store:
                @block.sync
                def _(sp):
                    ov = a["out"].rearrange("(n p) d -> p n d", p=P)
                    n = ST // 2
                    with sp.Fori(0, HALF) as it:
                        for half in range(2):
                            sp.wait_ge(rows_ready, it * (ST * TOP) + (half + 1) * n * TOP)
                            sp.dma_start(ov[:, bass.ds(it * ST + half * n, n), :],
                                         k["x"][:, bass.ds((it * ST + half * n) * D, n * D)].rearrange(
                                             "p (n d) -> p n d", d=D)).then_inc(stored, 16)
                    sp.wait_ge(stored, 16 * 2 * HALF)


def experts(nc, a, k, t, sem, sb, ph):
    PW = 2 * D
    with ExitStack() as c:
        s = lambda n: sem(ph + n)
        two = lambda n, dt=F32: [sb(c, f"{ph}{n}{i}", [P, PW], dt) for i in range(2)]
        xs, r, h, out = two("xs"), two("relu"), two("h"), two("out")
        xh, xl, hh, hl = two("xh", F32R), two("xl", F32R), two("hh", F32R), two("hl", F32R)
        banks = lambda n: [c.enter_context(nc.psum_tensor(f"{ph}{n}{i}", [P, PW], F32)) for i in range(2)]
        psX, psU, psH, psO = banks("psX"), banks("psU"), banks("psH"), banks("psO")
        xs_in, stored = [s(f"xs_in{i}") for i in range(2)], [s(f"stored{i}") for i in range(2)]
        xT_ready, up_ready, hT_ready, down_ready = s("xT_ready"), s("up_ready"), s("hT_ready"), s("down_ready")
        xh_ready, relu_ready, hh_ready = s("xh_ready"), s("relu_ready"), s("hh_ready")
        xl_ready, h_ready, hl_ready, out_ready = s("xl_ready"), s("h_ready"), s("hl_ready"), s("out_ready")
        BODY, FIRST = 4, 4
        PASSES = (PAIRS - 2 - FIRST) // BODY

        def steps(eng, step, before=None):
            for n in range(-2, FIRST):
                step(n, n % 2)
            if before:
                before()
            with eng.Fori(0, PASSES) as it:
                for q in range(BODY):
                    step(it * BODY + (FIRST + q), q % 2)
            if before:
                before()
            for n in range(FIRST + PASSES * BODY, PAIRS + 1):
                step(n, n % 2)

        def ahead(n, by):
            return not isinstance(n, int) or 0 <= n + by < PAIRS

        def filled(n, par):
            return 16 * (n // 2 + 1) if isinstance(n, int) else (n + (2 - par)) * 8

        def quarter(block, tile):
            return slice(block * D + tile * P, block * D + (tile + 1) * P)

        with nc.Block() as block:
            @block.tensor
            def _(pe):
                held = []

                def expert_of(pair):
                    return pe.value_load(t["expert"][0:1, bass.ds(pair, 1)], min_val=0, max_val=E - 1)

                def through(dst, xp, rows, w, cols):
                    m = 0
                    for cb in range(2):
                        for part, lefts in (("hi", xp), ("lo", xp[0:1])):
                            right = w[part][:, cols(cb)]
                            for i in range(2):
                                for left in lefts:
                                    ins = pe.matmul(dst[:, i * D:(i + 1) * D], left[:, rows(cb, i)], right,
                                                    start=(m == 0), stop=(m == 11))
                                    m += 1
                    return ins

                w1, w2 = ({part: tensors[name + part] for part in ("hi", "lo")} for tensors, name in ((k, "w1"), (t, "w2")))

                def step(n, par):
                    odd = 1 - par
                    if ahead(n, 2):
                        pe.wait_ge(xs_in[par], filled(n + 2, par))
                        need(pe, xl_ready, n + 1)
                        for cb in range(CB):
                            for i in range(2):
                                ins = pe.transpose(psX[par][:, quarter(cb, i)], xs[par][:, i * D + cb * P:i * D + (cb + 1) * P],
                                                   k["ident"][:, :])
                        ins.then_inc(xT_ready, 1)
                    if ahead(n, 1):
                        which = expert_of(n + 1)
                        held.append((n + 1, which))
                        pe.wait_ge(xh_ready, n + 2)
                        pe.wait_ge(xl_ready, n + 2)
                        need(pe, h_ready, n)
                        through(psU[odd], (xh[odd], xl[odd]), quarter, w1,
                                lambda cb: bass.ds(which * FE + cb * FALL, FE)).then_inc(up_ready, 1)
                    if ahead(n, 0):
                        pe.wait_ge(h_ready, n + 1)
                        need(pe, hl_ready, n - 1)
                        for fb in range(2):
                            for i in range(2):
                                ins = pe.transpose(psH[par][:, quarter(fb, i)], h[par][:, i * D + fb * P:i * D + (fb + 1) * P],
                                                   k["ident"][:, :])
                        ins.then_inc(hT_ready, 1)
                    if ahead(n, -1):
                        mine = held[-3][1] if len(held) > 2 else expert_of(n - 1)
                        pe.wait_ge(hh_ready, n)
                        pe.wait_ge(hl_ready, n)
                        need(pe, out_ready, n - 2)
                        through(psO[odd], (hh[odd], hl[odd]), quarter, w2,
                                lambda fb: bass.ds(mine * (2 * D) + fb * D, D)).then_inc(down_ready, 1)

                steps(pe, step, held.clear)

            @block.scalar
            def _(act):
                def step(n, par):
                    odd = 1 - par
                    if ahead(n, 2):
                        act.wait_ge(xT_ready, n + 3)
                        need(act, up_ready, n + 1)
                        act.activation(xh[par][:, :], psX[par][:, :], ACT.Copy).then_inc(xh_ready, 1)
                    if ahead(n, 1):
                        act.wait_ge(up_ready, n + 2)
                        need(act, h_ready, n)
                        act.activation(r[odd][:, :], psU[odd][:, :], ACT.Relu).then_inc(relu_ready, 1)
                    if ahead(n, 0):
                        act.wait_ge(hT_ready, n + 1)
                        need(act, down_ready, n - 1)
                        act.activation(hh[par][:, :], psH[par][:, :], ACT.Copy).then_inc(hh_ready, 1)
                    if ahead(n, -1):
                        act.wait_ge(down_ready, n)
                        if not isinstance(n, int) or n > 2:
                            act.wait_ge(stored[odd], filled(n - 3, odd) if isinstance(n, int) else (n - (2 - par)) * 8)
                        act.activation(out[odd][:, :], psO[odd][:, :], ACT.Copy).then_inc(out_ready, 1)

                steps(act, step)

            @block.vector
            def _(v):
                def step(n, par):
                    odd = 1 - par
                    if ahead(n, 2):
                        v.wait_ge(xh_ready, n + 3)
                        need(v, up_ready, n + 1)
                        v.tensor_tensor(xl[par][:, :], psX[par][:, :], xh[par][:, :].bitcast(F32), ALU.subtract).then_inc(xl_ready, 1)
                    if ahead(n, 1):
                        v.wait_ge(relu_ready, n + 2)
                        need(v, hT_ready, n)
                        v.scalar_tensor_tensor(h[odd][:, :], psU[odd][:, :], 0.0, r[odd][:, :],
                                               ALU.max, ALU.mult).then_inc(h_ready, 1)
                    if ahead(n, 0):
                        v.wait_ge(hh_ready, n + 1)
                        need(v, down_ready, n - 1)
                        v.tensor_tensor(hl[par][:, :], psH[par][:, :], hh[par][:, :].bitcast(F32), ALU.subtract).then_inc(hl_ready, 1)

                steps(v, step)

            @block.sync
            def _(sp):
                xv = a["slots_x"].rearrange("(n i p) d -> n p i d", p=P, i=2)
                yv = a["slots_y"].rearrange("(n i p) d -> n p i d", p=P, i=2)

                def load(n, par):
                    sp.dma_start(xs[par][:, :].rearrange("p (i d) -> p i d", i=2),
                                 xv[bass.ds(n, 1)].rearrange("o p i d -> (o p) i d")).then_inc(xs_in[par], 16)

                load(0, 0)
                load(1, 1)

                def step(n, par):
                    if ahead(n, 4):
                        sp.wait_ge(xT_ready, n + 3)
                        load(n + 4, par)
                    if ahead(n, -1):
                        odd = 1 - par
                        sp.wait_ge(out_ready, n)
                        sp.dma_start(yv[bass.ds(n - 1, 1)].rearrange("o p i d -> (o p) i d"),
                                     out[odd][:, :].rearrange("p (i d) -> p i d", i=2)).then_inc(stored[odd], 16)

                for n in range(-2, FIRST):
                    step(n, n % 2)
                with sp.Fori(0, (PAIRS - 4 - FIRST) // 2) as it:
                    for q in range(2):
                        step(it * 2 + (FIRST + q), q)
                for n in range(FIRST + (PAIRS - 4 - FIRST) // 2 * 2, PAIRS + 1):
                    step(n, n % 2)
                for par in range(2):
                    sp.wait_ge(stored[par], 16 * ((PAIRS + 1 - par) // 2))


def statistics(nc, k, sem, sb, ph):
    with ExitStack() as c:
        tmp = sb(c, ph + "root_tmp", [P, 2 * TILES])
        chain = sem(ph + "dve_chain")
        with nc.Block() as block:
            @block.vector
            def _(v):
                rsqrt_rows(Chain(v, chain), v, k, tmp)


def attention(nc, a, k, sem, sb):
    X = k["x"]
    TWO_PI = 2.0 * math.pi
    XC = P + TAPS
    with ExitStack() as c:
        s = lambda n: sem("at_" + n)
        xn = sb(c, "at_xn", [P, D])
        xh, xl = ([sb(c, f"at_{n}{i}", [P, CB * XC], F32R) for i in range(2)] for n in ("xh", "xl"))
        turns = sb(c, "at_turns", [P, CH])
        kv = sb(c, "at_kv", [P, KH - KV])
        feat = [sb(c, f"at_feat{i}", [P, 2 * CH]) for i in range(2)]
        qs = [sb(c, f"at_qs{i}", [P, 2 * QW]) for i in range(2)]
        prod = sb(c, "at_prod", [P, 2 * CHUNK])
        srow = sb(c, "at_srow", [P, ROW])
        crow = [sb(c, f"at_crow{i}", [HALF[i], RW]) for i in range(2)]
        split = [sb(c, f"at_split{i}", [HALF[i], 2 * RW], F32R) for i in range(2)]
        ones, ones_set = sb(c, "at_ones", [HALF[1], RW]), s("ones_set")
        carry = sb(c, "at_carry", [2, ROW], F32R)
        pw = [sb(c, f"at_p{i}", [P, K]) for i in range(2)]
        ex = sb(c, "at_exp", [P, 8 * K])
        pow2 = sb(c, "at_pow2", [P, K], I32)
        y2 = sb(c, "at_y2", [P, 2 * KH])
        y = sb(c, "at_y", [P, KH])
        ys = y
        yh, yl = (sb(c, "at_" + n, [P, KH], F32R) for n in ("yh", "yl"))
        rden = sb(c, "at_rden", [P, 2 * K])
        tmp = sb(c, "at_rt", [P, 2 * TILES])
        ps = lambda n: c.enter_context(nc.psum_tensor("at_ps" + n, [P, 512], F32))
        psT, psK, psQ, psY = ps("T"), ps("K"), ps("Q"), ps("Y")
        psS = [ps(f"S{i}") for i in range(4)]
        den = psY[:, 0:K]

        xT_ready, mem_ready, q_ready, yT_ready = s("xT_ready"), s("mem_ready"), s("q_ready"), s("yT_ready")
        den_ready, sums_ready, out_ready = s("den_ready"), s("sums_ready"), s("out_ready")
        xh_ready, yh_ready, whole_ready, tanh_ready = s("xh_ready"), s("yh_ready"), s("whole_ready"), s("tanh_ready")
        feat_ready, row_ready, q_copied, silu_ready = s("feat_ready"), s("row_ready"), s("q_copied"), s("silu_ready")
        xn_ready, xl_ready, turns_ready, mem_read = s("xn_ready"), s("xl_ready"), s("turns_ready"), s("mem_read")
        rem_ready, p_ready, frac_ready, prod_done = s("rem_ready"), s("p_ready"), s("frac_ready"), s("prod_done")
        den_read, y_ready, yl_ready, x_added = s("den_read"), s("y_ready"), s("yl_ready"), s("x_added")
        v_ready, kv_ready, shared_turns, abs_ready = s("v_ready"), s("kv_ready"), s("shared_turns"), s("abs_ready")
        split_ready, row_moved, carry_in = ([s(f"{n}{i}") for i in range(2)] for n in ("split_ready", "row_moved", "carry_in"))
        v_chain, a_chain = s("dve_chain"), s("act_chain")

        def steps(eng, step, chain=None, per=0):
            pairs = (TILES - 6) // 2
            for n in range(-4, 2):
                step(n, n % 2)
            with eng.Fori(0, pairs) as it:
                if chain:
                    chain.enter(it, per)
                for par in range(2):
                    step(it * 2 + (2 + par), par)
                if chain:
                    chain.leave(pairs)
            for n in range(TILES - 4, TILES + 1):
                step(n, n % 2)

        def has(n):
            return not isinstance(n, int) or 0 <= n < TILES

        def first(n):
            return isinstance(n, int) and n == 0

        def ahead(n, by):
            return not isinstance(n, int) or 0 <= n + by < TILES

        with nc.Block() as block:
            @block.tensor
            def _(pe):
                def step(n, par):
                    odd = 1 - par

                    def transposes():
                        if ahead(n, 3):
                            pe.wait_ge(xn_ready, n + 4)
                            need(pe, xl_ready, n + 3)
                            for cb in range(CB):
                                ins = pe.transpose(psT[:, cb * P:(cb + 1) * P], xn[:, cb * P:(cb + 1) * P], k["ident"][:, :])
                            ins.then_inc(xT_ready, 1)
                        if ahead(n, -1):
                            pe.wait_ge(silu_ready, n)
                            need(pe, x_added, n - 1)
                            pe.wait_ge(den_read, n)
                            if has(n):
                                pe.wait_ge(row_ready, 9 * n)
                            for cb in range(CB):
                                ins = pe.transpose(psY[:, cb * P:(cb + 1) * P], ys[:, cb * P:(cb + 1) * P], k["ident"][:, :])
                            ins.then_inc(yT_ready, 1)

                    def project_out():
                        if not ahead(n, -1):
                            return
                        pe.wait_ge(yh_ready, n)
                        pe.wait_ge(yl_ready, n)
                        i = 0
                        for cb in range(CB):
                            for yp, wp in ((yh, "hi"), (yl, "hi"), (yh, "lo")):
                                ins = pe.matmul(psY[:, D:2 * D], yp[:, cb * P:(cb + 1) * P],
                                                k["wo" + wp][:, cb * D:(cb + 1) * D], start=(i == 0), stop=(i == 5))
                                i += 1
                        ins.then_inc(out_ready, 1)

                    def project_queries():
                        if not ahead(n, 2):
                            return
                        need(pe, q_copied, n + 2)
                        parts = ((xh[par], "hi"), (xl[par], "hi"), (xh[par], "lo"))
                        i = 0
                        for cb in range(CB):
                            for xp, wp in parts:
                                ins = pe.matmul(psQ[:, :], xp[:, cb * XC + TAPS - 1:cb * XC + TAPS - 1 + P],
                                                k["wq" + wp][:, cb * 2 * QW:(cb + 1) * 2 * QW],
                                                start=(i == 0), stop=(i == 5))
                                i += 1
                        ins.then_inc(q_ready, 1)

                    def project_memory():
                        if not ahead(n, 3):
                            return
                        pe.wait_ge(xh_ready, n + 4)
                        pe.wait_ge(xl_ready, n + 4)
                        need(pe, mem_read, n + 3)
                        parts = ((xh[odd], "hi"), (xl[odd], "hi"), (xh[odd], "lo"))
                        total, i = CB * TAPS * 3, 0
                        for cb in range(CB):
                            for j in range(TAPS):
                                for xp, wp in parts:
                                    ins = pe.matmul(psK[:, 0:MEM], xp[:, cb * XC + j:cb * XC + j + P],
                                                    k["wc" + wp][:, (cb * TAPS + j) * MEM:(cb * TAPS + j + 1) * MEM],
                                                    start=(i == 0), stop=(i == total - 1))
                                    i += 1
                        ins.then_inc(mem_ready, 1)

                    if has(n):
                        for e in range(CHUNKS):
                            if e % KQ == 0:
                                if not first(n):
                                    pe.wait_ge(carry_in[e // KQ], 32 * n)
                                pe.wait_ge(v_ready, 2 * n + e // KQ + 1)
                            need(pe, prod_done, 8 * n + (e - 3))
                            if ahead(n, 1) or e < 4:
                                need(pe, row_ready, 9 * n + (e - 3) - (0 if e > 3 or first(n) else 1))
                            cols = slice(*chunk_cols(e))
                            last = pe.matmul(psS[e % 4][:, :], k["tri"][:, :], feat[par][:, cols], start=True, stop=first(n))
                            if not first(n):
                                last = pe.matmul(psS[e % 4][:, :], k["ones2"][:, :], carry[:, slice(*row_cols(e))], start=False, stop=True)
                            last.then_inc(sums_ready, 1)
                            if e == 1:
                                transposes()
                            if e == 3:
                                project_queries()
                            if e == OUT_AFTER:
                                project_out()
                                pe.wait_ge(p_ready, n + 1)
                                last = pe.matmul(den, k["tri"][:, :], pw[par][:, :], start=True, stop=first(n))
                                if not first(n):
                                    last = pe.matmul(den, k["ones2"][:, :], carry[:, 2 * CH:ROW], start=False, stop=True)
                                last.then_inc(den_ready, 1)
                    else:
                        transposes()
                        project_queries()
                        project_out()
                    project_memory()

                steps(pe, step)

            @block.scalar
            def _(act):
                ch = Chain(act, a_chain)

                def step(n, par):
                    odd = 1 - par

                    def rows(lo, hi):
                        if not (has(n) and ahead(n, 1)):
                            return
                        for e in range(lo, hi):
                            act.wait_ge(prod_done, 8 * n + (e + 1))
                            if e % KQ == 0:
                                need(act, row_moved[e // KQ], 16 * n)
                            act.activation(srow[96:P, slice(*row_cols(e))], psS[e % 4][96:P, :], ACT.Copy).then_inc(row_ready, 1)

                    f = feat[odd]
                    if ahead(n, 2):
                        act.wait_ge(mem_ready, n + 3)
                        need(act, shared_turns, n + 2)
                        act.activation(kv[:, :], psK[:, KV:KH], ACT.Copy).then_inc(kv_ready, 1)
                    if ahead(n, 1):
                        act.wait_ge(abs_ready, n + 2)
                        act.activation(f[:, CH:2 * CH], f[:, CH:2 * CH], ACT.Sin, scale=-TWO_PI).then_inc(feat_ready, 1)
                    rows(0, 2)
                    if ahead(n, 3):
                        act.wait_ge(xT_ready, n + 4)
                        need(act, q_ready, n + 2)
                        x3 = [t[:, :].rearrange("p (c t) -> p c t", c=CB) for t in xh]
                        if isinstance(n, int) and n == -3:
                            ch.link(act.activation(x3[odd][:, :, 0:TAPS - 1], psT[:, 0:CB * (TAPS - 1)].rearrange(
                                "p (c t) -> p c t", c=CB), ACT.Copy, scale=0.0))
                        else:
                            act.wait_ge(xh_ready, n + 3)
                            ch.link(act.activation(x3[odd][:, :, 0:TAPS - 1],
                                                   x3[par][:, :, P:P + TAPS - 1].bitcast(F32), ACT.Copy))
                        act.activation(x3[odd][:, :, TAPS - 1:TAPS - 1 + P],
                                       psT[:, 0:D].rearrange("p (c t) -> p c t", c=CB), ACT.Copy).then_inc(xh_ready, 1)
                    if ahead(n, -1):
                        act.wait_ge(yT_ready, n)
                        need(act, out_ready, n - 1)
                        act.activation(yh[:, :], psY[:, 0:KH], ACT.Copy).then_inc(yh_ready, 1)
                    if ahead(n, 1):
                        act.activation(f[:, 0:CH], f[:, 0:CH], ACT.Sin, scale=-TWO_PI,
                                       bias=k["halfpi"][:, 0:1]).then_inc(feat_ready, 1)
                    rows(2, 8)
                    if has(n) and ahead(n, 1):
                        act.wait_ge(den_read, n + 1)
                        need(act, x_added, n)
                        act.activation(srow[96:P, 2 * CH:ROW], den[96:P, :], ACT.Copy).then_inc(row_ready, 1)
                    if ahead(n, 2):
                        act.wait_ge(rem_ready, n + 3)
                        act.activation(ex[:, 4 * K:5 * K], ex[:, 3 * K:4 * K], ACT.Tanh, scale=0.5).then_inc(tanh_ready, 1)
                        act.wait_ge(q_ready, n + 3)
                        need(act, prod_done, 8 * n + 8)
                        act.activation(qs[par][:, :], psQ[:, :], ACT.Copy).then_inc(q_copied, 1)
                        act.wait_ge(frac_ready, n + 3)
                        need(act, sums_ready, 8 * (n + 1))
                        act.activation(feat[par][:, 0:CH], feat[par][:, CH:2 * CH], ACT.Abs).then_inc(abs_ready, 1)
                    if has(n):
                        act.wait_ge(y_ready, n + 1)
                        act.activation(ys[:, :], y[:, :], ACT.Silu).then_inc(silu_ready, 1)

                steps(act, step, ch, 2 * ACT_LINKS)

            @block.vector
            def _(v):
                ch = Chain(v, v_chain)
                lp, t0, k2, rem, th, t1, t2, _ = (ex[:, i * K:(i + 1) * K] for i in range(8))
                y2v = y2[:, :].rearrange("p (c f) -> p c f", c=2)

                def step(n, par):
                    odd = 1 - par

                    def product(e):
                        if not has(n):
                            return
                        part, q = 1 - e // KQ, e % KQ
                        v.wait_ge(sums_ready, 8 * n + (e + 1))
                        if e == 0:
                            v.wait_ge(q_copied, n + 1)
                        v.tensor_tensor(prod[:, (e % 2) * CHUNK:(e % 2 + 1) * CHUNK].rearrange("p (r f) -> p r f", r=REP),
                                        psS[e % 4][:, :].rearrange("p (r f) -> p r f", r=REP),
                                        qs[par][:, part * QW + q * HM:part * QW + (q + 1) * HM].unsqueeze(1).to_broadcast([P, REP, HM]),
                                        ALU.mult).then_inc(prod_done, 1)

                    def total(e):
                        part, q = 1 - e // KQ, e % KQ
                        v.wait_ge(prod_done, 8 * n + (e + 1))
                        return ch.mark(v.tensor_reduce(y2v[:, part, (q - 1) * HM:(q + 1) * HM],
                                                       prod[:, :].rearrange("p (c m) -> p c m", m=M), AX.X, ALU.add))

                    product(0)
                    product(1)
                    if has(n):
                        summed = total(1)
                    if ahead(n, 2):
                        v.wait_ge(kv_ready, n + 3)
                        need(v, frac_ready, n + 2)
                        v.tensor_tensor(turns[:, 0:KV * M].rearrange("p (c m) -> p c m", m=M),
                                        psK[:, 0:KV].unsqueeze(2).to_broadcast([P, KV, M]),
                                        k["theta"][:, 0:KV * M].rearrange("p (c m) -> p c m", m=M), ALU.mult).then_inc(turns_ready, 1)
                        v.tensor_tensor(t0, psK[:, KH:MEM], k["sscale"][:, :], ALU.mult).then_inc(mem_read, 1)
                        v.wait_ge(turns_ready, n + 3)
                        v.wait_ge(shared_turns, n + 3)
                        if has(n):
                            v.wait_ge(sums_ready, 8 * n + KQ)
                        v.tensor_scalar(feat[par][:, CH:2 * CH], turns[:, :], MAGIC, -MAGIC, ALU.add, ALU.add).then_inc(whole_ready, 1)
                    if has(n):
                        ch.wait(summed)
                    product(2)
                    if ahead(n, 2):
                        v.wait_ge(mem_read, n + 3)
                        m = ch.mark(v.tensor_scalar(t0, t0, 20.0, -20.0, ALU.min, ALU.max))
                    product(3)
                    if ahead(n, 2):
                        ch.wait(m)
                        v.scalar_tensor_tensor(lp[:, 0:NDECAY], k["slope"][:, 0:NDECAY], k["dist"][:, bass.ds(n + 2, 1)],
                                               t0[:, 0:NDECAY], ALU.mult, ALU.add)
                        m = ch.mark(v.scalar_tensor_tensor(lp[:, NDECAY:K], k["slope"][:, NDECAY:K],
                                                           k["pos"][:, bass.ds(n + 2, 1)], t0[:, NDECAY:K], ALU.mult, ALU.add))
                    if has(n):
                        summed = total(3)
                    if ahead(n, 2):
                        ch.wait(m)
                        m = ch.mark(v.tensor_scalar(k2, lp, LOG2E, MAGIC, ALU.mult, ALU.add))
                    if ahead(n, 3):
                        v.wait_ge(xh_ready, n + 4)
                        need(v, q_ready, n + 2)
                        x3 = [t[:, :].rearrange("p (c t) -> p c t", c=CB) for t in xl]
                        h3 = xh[odd][:, :].rearrange("p (c t) -> p c t", c=CB)
                        if isinstance(n, int) and n == -3:
                            before = ch.mark(v.memset(x3[odd][:, :, 0:TAPS - 1].bitcast(F32), 0.0))
                        else:
                            v.wait_ge(xl_ready, n + 3)
                            before = ch.mark(v.tensor_copy(x3[odd][:, :, 0:TAPS - 1],
                                                           x3[par][:, :, P:P + TAPS - 1].bitcast(F32)))
                        ch.wait(before)
                        v.tensor_tensor(x3[odd][:, :, TAPS - 1:TAPS - 1 + P],
                                        psT[:, 0:D].rearrange("p (c t) -> p c t", c=CB),
                                        h3[:, :, TAPS - 1:TAPS - 1 + P].bitcast(F32), ALU.subtract).then_inc(xl_ready, 1)
                    if ahead(n, 2):
                        ch.wait(m)
                        m = ch.mark(v.tensor_scalar(k2, k2, -MAGIC, None, ALU.add))
                    if ahead(n, -1):
                        v.wait_ge(yh_ready, n)
                        v.tensor_tensor(yl[:, :], psY[:, 0:KH], yh[:, :].bitcast(F32), ALU.subtract).then_inc(yl_ready, 1)
                    if has(n):
                        ch.wait(summed)
                    product(4)
                    if ahead(n, 2):
                        ch.wait(m)
                        m = ch.mark(v.scalar_tensor_tensor(rem, k2, -LN2_HI, lp, ALU.mult, ALU.add))
                    product(5)
                    if ahead(n, 2):
                        ch.wait(m)
                        v.scalar_tensor_tensor(rem, k2, -LN2_LO, rem, ALU.mult, ALU.add).then_inc(rem_ready, 1)
                    if has(n):
                        summed = total(5)
                    if ahead(n, 2):
                        v.wait_ge(rem_ready, n + 3)
                        m = ch.mark(v.tensor_scalar(k2, k2, -127.0, 127.0, ALU.max, ALU.add))
                    if has(n):
                        ch.wait(summed)
                    product(6)
                    if ahead(n, 2):
                        ch.wait(m)
                        raised = ch.mark(v.tensor_scalar(pow2[:, :], k2, 8388608.0, None, ALU.mult))
                    product(7)
                    if has(n):
                        v.wait_ge(den_ready, n + 1)
                        v.tensor_scalar(rden[:, 0:K], den, 1e-4, None, ALU.max).then_inc(den_read, 1)
                    if ahead(n, -1):
                        v.wait_ge(out_ready, n)
                        xs = X[:, bass.ds((n - 1) * D, D)]
                        v.tensor_tensor(xs, psY[:, D:2 * D], xs, ALU.add).then_inc(x_added, 1)
                    if has(n):
                        summed = total(7)
                        v.wait_ge(den_read, n + 1)
                        inverse = ch.mark(v.reciprocal(rden[:, K:2 * K], rden[:, 0:K]))
                        ch.wait(summed)
                        summed = ch.mark(v.tensor_tensor(y2[:, 0:KH], y2[:, 0:KH], y2[:, KH:2 * KH], ALU.add))
                    if ahead(n, 2):
                        v.wait_ge(tanh_ready, n + 3)
                        m = ch.mark(v.tensor_scalar(t1, th, -1.0, 1.0, ALU.mult, ALU.add))
                    if has(n):
                        ch.wait(inverse)
                        ch.wait(summed)
                        need(v, yT_ready, n)
                        v.tensor_tensor(y[:, :].rearrange("p (k h) -> p k h", h=H),
                                        y2[:, 0:KH].rearrange("p (k h) -> p k h", h=H),
                                        rden[:, K:2 * K].unsqueeze(2).to_broadcast([P, K, H]), ALU.mult).then_inc(y_ready, 1)
                    if ahead(n, 2):
                        ch.wait(m)
                        m = ch.mark(v.reciprocal(t2, t1))
                    if ahead(n, 4):
                        need(v, xT_ready, n + 4)
                        v.tensor_scalar(xn[:, :], X[:, bass.ds((n + 4) * D, D)], k["mean"][:, bass.ds(n + 4, 1)],
                                        k["rstd"][:, bass.ds(n + 4, 1)], ALU.subtract, ALU.mult).then_inc(xn_ready, 1)
                    if ahead(n, 2):
                        ch.wait(m)
                        m = ch.mark(v.scalar_tensor_tensor(t1, th, 1.0, t2, ALU.add, ALU.mult))
                    if ahead(n, -1):
                        v.wait_ge(x_added, n)
                        v.bn_stats(k["st"][:, bass.ds((n - 1) * 6, 6)], X[:, bass.ds((n - 1) * D, D)])
                    if ahead(n, 2):
                        ch.wait(m)
                        ch.wait(raised)
                        need(v, den_ready, n + 1)
                        need(v, v_ready, 2 * (n + 1))
                        v.tensor_tensor(pw[par][:, :], t1, pow2[:, :].bitcast(F32), ALU.mult).then_inc(p_ready, 1)

                steps(v, step, ch, 2 * DVE_LINKS)
                ch.link(v.memset(tmp[:, 0:1], 0.0))
                rsqrt_rows(ch, v, k, tmp)

            @block.gpsimd
            def _(g):
                g.memset(ones[:, :], 1.0).then_inc(ones_set, 1)
                g.wait_ge(ones_set, 1)

                def split_row(n, i):
                    if has(n) and ahead(n, 1):
                        rows = HALF[i]
                        g.wait_ge(row_moved[i], 16 * n + 16)
                        need(g, carry_in[i], 32 * n)
                        g.tensor_tensor(split[i][:, 0:RW], crow[i][:, :], ones[0:rows, :], ALU.mult).then_inc(split_ready[i], 1)
                        g.wait_ge(split_ready[i], 2 * n + 1)
                        g.tensor_tensor(split[i][:, RW:2 * RW], crow[i][:, :], split[i][:, 0:RW].bitcast(F32),
                                        ALU.subtract).then_inc(split_ready[i], 1)

                def step(n, par):
                    odd = 1 - par
                    if ahead(n, 2):
                        g.wait_ge(kv_ready, n + 3)
                        need(g, frac_ready, n + 2)
                        g.tensor_tensor(turns[:, KV * M:CH].rearrange("p (c m) -> p c m", m=M),
                                        kv[:, :].unsqueeze(2).to_broadcast([P, KH - KV, M]),
                                        k["theta"][:, KV * M:CH].rearrange("p (c m) -> p c m", m=M), ALU.mult).then_inc(shared_turns, 1)

                    def weigh(i, part):
                        if ahead(n, 1):
                            if i == 0:
                                g.wait_ge(p_ready, n + 2)
                            g.wait_ge(feat_ready, 2 * n + 3 + i)
                            f = feat[odd][:, part * CH:(part + 1) * CH].rearrange("p (k f) -> p k f", k=K)
                            g.tensor_tensor(f, f, pw[odd][:, :].unsqueeze(2).to_broadcast([P, K, HM]),
                                            ALU.mult).then_inc(v_ready, 1)

                    weigh(0, 1)
                    if ahead(n, 2):
                        g.wait_ge(whole_ready, n + 3)
                        sines = feat[par][:, CH:2 * CH]
                        g.tensor_tensor(sines, sines, turns[:, :], ALU.subtract).then_inc(frac_ready, 1)
                    split_row(n, 0)
                    weigh(1, 0)
                    split_row(n, 1)

                steps(g, step)

            @block.sync
            def _(sp):
                def step(n, par):
                    if has(n) and ahead(n, 1):
                        for i, copied in enumerate((KQ, CHUNKS + 1)):
                            lo, hi = i * CH, i * CH + HALF[i] * RW
                            sp.wait_ge(row_ready, 9 * n + copied)
                            sp.dma_start(crow[i][:, :], srow[P - 1:P, lo:hi].rearrange("o (r w) -> o r w", r=HALF[i])).then_inc(row_moved[i], 16)
                            for part in range(2):
                                sp.wait_ge(split_ready[i], 2 * n + (part + 1))
                                sp.dma_start(carry[part:part + 1, lo:hi].bitcast(F32).rearrange("o (r w) -> o r w", r=HALF[i]),
                                             split[i][:, part * RW:(part + 1) * RW].bitcast(F32)).then_inc(carry_in[i], 16)

                steps(sp, step)


def kernel(**inputs):
    import concourse.bacc as bacc
    from concourse.bass_utils import run_bass_kernel_spmd

    g = {n[3:]: np.asarray(v) for n, v in inputs.items()}
    nk = KH + K
    w_in = g["attn_W_in"]
    wq = w_in[:, nk:].reshape(D, KQ, H, M, 2)
    arrays = {
        "x": g["attn_x"].reshape(TOKENS, D),
        "w1t": np.concatenate([g["ffn_w1_stack"].reshape(E * FE, D), g["ffn_ws1"]]).T,
        "w2t": np.concatenate([g["ffn_w2_stack"].transpose(0, 2, 1).reshape(E * FE, D), g["ffn_ws2"].T]),
        "wrt": g["ffn_w_router"].T,
        "w_out": g["attn_W_out"],
        "w_mem": w_in[:, :nk],
        "w_qre": wq[..., 0].reshape(D, QW),
        "w_qim": wq[..., 1].reshape(D, QW),
        "conv_k": g["attn_conv_k"].reshape(TAPS * MEM),
        "theta": g["attn_theta"].reshape(CH),
        "norm_scale": g["attn_norm_scale"],
        "re_diag": np.diagonal(g["attn_W_re"]),
        "im_diag": np.diagonal(g["attn_W_im"]),
        "slopes": np.concatenate([g["attn_decay_slopes"], g["attn_anchor_slopes"]]),
        "score_scale": g["attn_score_scale"],
    }
    arrays = {n: np.ascontiguousarray(v) for n, v in arrays.items()}
    nc = bacc.Bacc("TRN2", target_bir_lowering=False, num_devices=1)
    aps = {n: nc.dram_tensor("in_" + n, v.shape, F32, kind="ExternalInput").ap() for n, v in arrays.items()}
    for n in ("slots_x", "slots_y"):
        aps[n] = nc.dram_tensor(n, (PAIRS * PT, D), F32, kind="Internal").ap()
    aps["out"] = nc.dram_tensor("out_x", (TOKENS, D), F32, kind="ExternalOutput").ap()
    build(nc, aps)
    r = run_bass_kernel_spmd(nc, [{"in_" + n: v for n, v in arrays.items()}], core_ids=[0])
    return r.results[0]["out_x"].reshape(1, TOKENS, D)
```
